# Optimizing a Trainium2 kernel written in Bass

```python
import numpy as np
import jax
import jax.numpy as jnp

def _softmax(x, axis=-1):
    return jax.nn.softmax(x, axis=axis)

def _gelu(x):
    return jax.nn.gelu(x, approximate=True)

def _silu(x):
    return jax.nn.silu(x)

def _sigmoid(x):
    return jax.nn.sigmoid(x)

def _layernorm(x, axis=-1, eps=1e-05):
    m = jnp.mean(x, axis=axis, keepdims=True)
    v = jnp.var(x, axis=axis, keepdims=True)
    return (x - m) / jnp.sqrt(v + eps)

def _scatter_add(tgt, idx, src, axis=0):
    return tgt.at[idx].add(src)

def _segment_sum(src, seg, n):
    return jax.ops.segment_sum(src, seg, n)
kernel_name = 'mk_gps_d2_gnn_r8_4cd7da'

def setup_inputs(seed: int=0):
    np.random.seed(seed)
    _w = jnp.asarray

    def _rec_inputs():
        import jax
        import jax.numpy as jnp
        _gk = jax.random.key(seed)
        x = -0.0002928 + 1 * jax.random.normal(jax.random.fold_in(_gk, 1), (1024, 512), jnp.float32)
        _s = jax.random.randint(jax.random.fold_in(_gk, 2), (16384,), 0, 1024, jnp.int32)
        _d = jax.random.randint(jax.random.fold_in(_gk, 3), (16384,), 0, 1024, jnp.int32)
        _loop = jnp.arange(1024, dtype=jnp.int32)
        src = jnp.concatenate([_s, _d, _loop])
        dst = jnp.concatenate([_d, _s, _loop])
        _o = jnp.argsort(dst, stable=True)
        src = src[_o]
        dst = dst[_o]
        edge_attr_64 = 0.000189758 + 1.00013 * jax.random.normal(jax.random.fold_in(_gk, 12), (33792, 64), jnp.float32)
        return (x, src, dst, edge_attr_64)
    x, src, dst, edge_attr_64 = _rec_inputs()

    def _L0_gnn_setup():
        import jax, jax.numpy as jnp
        import numpy as np
        NEG = -1000000.0
        key = jax.random.key(seed)
        ks = jax.random.split(key, 8)
        N, D_IN, D_Q, D_K, E = (1024, 512, 512, 512, 32768)
        s = 1.0 / np.sqrt(D_IN)
        return {'x': jax.random.normal(ks[0], (N, D_IN), dtype=jnp.float32), 'edge_index': jax.random.randint(ks[1], (2, E), 0, N, dtype=jnp.int64), 'Wq': jax.random.normal(ks[2], (D_IN, D_Q), dtype=jnp.float32) * s, 'bq': jax.random.normal(ks[3], (D_Q,), dtype=jnp.float32) * 0.01, 'Wk': jax.random.normal(ks[4], (D_IN, D_K), dtype=jnp.float32) * s, 'bk': jax.random.normal(ks[5], (D_K,), dtype=jnp.float32) * 0.01, 'Wv': jax.random.normal(ks[6], (D_IN, D_K), dtype=jnp.float32) * s, 'bv': jax.random.normal(ks[7], (D_K,), dtype=jnp.float32) * 0.01}
    _L0_gnn_all = _L0_gnn_setup()
    _L0_gnn_in = {k: v for k, v in _L0_gnn_all.items() if k in ('Wq', 'bq', 'Wk', 'bk', 'Wv', 'bv')}
    del _L0_gnn_all

    def _L0_mix_setup():
        import jax, jax.numpy as jnp
        import numpy as np
        B, N, DIM = (4, 256, 512)
        H, HD = (8, 64)
        SCALE = 1.0 / float(np.sqrt(HD))
        key = jax.random.key(seed)
        k1, k2, k3 = jax.random.split(key, 3)
        x = jax.random.normal(k1, (B, N, DIM), dtype=jnp.float32)
        w_qkv = jax.random.normal(k2, (DIM, 3 * H * HD), dtype=jnp.float32) * 0.02
        w_out = jax.random.normal(k3, (H * HD, DIM), dtype=jnp.float32) * 0.02
        b_out = jnp.zeros((DIM,), dtype=jnp.float32)
        return {'x': x, 'w_qkv': w_qkv, 'w_out': w_out, 'b_out': b_out}
    _L0_mix_all = _L0_mix_setup()
    _L0_mix_in = {k: v for k, v in _L0_mix_all.items() if k in ('w_qkv', 'w_out', 'b_out')}
    del _L0_mix_all

    def _L0_ffn_setup():
        import jax, jax.numpy as jnp
        import numpy as np
        CAPACITY_FACTOR = 1.2
        key = jax.random.key(seed)
        k1, k2, k3 = jax.random.split(key, 3)
        B, S, D, E = (8, 512, 512, 16)
        x = jax.random.normal(k1, (B, S, D), dtype=jnp.float32)
        switch_w = jax.random.normal(k2, (E, D), dtype=jnp.float32) * 0.02
        switch_b = jnp.zeros((E,), dtype=jnp.float32)
        expert_w = jax.random.normal(k3, (E, D, D), dtype=jnp.float32) * 0.02
        expert_b = jnp.zeros((E, D), dtype=jnp.float32)
        return {'x': x, 'switch_w': switch_w, 'switch_b': switch_b, 'expert_w': expert_w, 'expert_b': expert_b}
    _L0_ffn_all = _L0_ffn_setup()
    _L0_ffn_in = {k: v for k, v in _L0_ffn_all.items() if k in ('switch_w', 'switch_b', 'expert_w', 'expert_b')}
    del _L0_ffn_all

    def _L1_gnn_setup():
        import jax, jax.numpy as jnp
        import numpy as np
        N_NODES = 6250
        N_EDGES = 100000
        NODE_IN = 512
        EDGE_IN = 64
        HID = 1024
        key = jax.random.key(seed)
        ks = jax.random.split(key, 6)
        x = jax.random.normal(ks[0], (N_NODES, NODE_IN), dtype=jnp.float32)
        edge_index = jax.random.randint(ks[1], (2, N_EDGES), 0, N_NODES, dtype=jnp.int64)
        edge_attr = jax.random.normal(ks[2], (N_EDGES, EDGE_IN), dtype=jnp.float32)
        u = jnp.zeros((1, 16), dtype=jnp.float32)
        batch = jnp.zeros((N_NODES,), dtype=jnp.int64)
        s1 = 1.0 / np.sqrt(NODE_IN + EDGE_IN)
        s2 = 1.0 / np.sqrt(HID)
        W1 = jax.random.normal(ks[3], (NODE_IN + EDGE_IN, HID), dtype=jnp.float32) * s1
        b1 = jnp.zeros((HID,), dtype=jnp.float32)
        W2 = jax.random.normal(ks[4], (HID, NODE_IN), dtype=jnp.float32) * s2
        b2 = jnp.zeros((NODE_IN,), dtype=jnp.float32)
        return {'x': x, 'edge_index': edge_index, 'edge_attr': edge_attr, 'u': u, 'batch': batch, 'W1': W1, 'b1': b1, 'W2': W2, 'b2': b2}
    _L1_gnn_all = _L1_gnn_setup()
    _L1_gnn_in = {k: v for k, v in _L1_gnn_all.items() if k in ('u', 'W1', 'b1', 'W2', 'b2')}
    del _L1_gnn_all

    def _L1_mix_setup():
        import jax, jax.numpy as jnp
        import numpy as np
        B, T, D = (4, 1024, 512)
        H, S = (8, 16)
        HD = D // H
        PRUNE_THRESH = 0.02
        key = jax.random.key(seed)
        ks = jax.random.split(key, 8)
        base_centers = jax.random.normal(ks[0], (H, S, HD), jnp.float32) * 0.3
        center_deltas = jax.random.normal(ks[1], (H, S, HD), jnp.float32) * 0.1
        log_scales = jnp.full((H, S), -0.5, jnp.float32) + 0.1 * jax.random.normal(ks[2], (H, S), jnp.float32)
        log_amps = jnp.full((H, S), -1.0, jnp.float32) + 0.1 * jax.random.normal(ks[3], (H, S), jnp.float32)
        movement_scale_param = jnp.array([0.05], jnp.float32)
        temperature = jnp.ones((1,), jnp.float32)
        qkv_w = jax.random.normal(ks[4], (3 * D, D), jnp.float32) * (1.0 / np.sqrt(D))
        out_w = jax.random.normal(ks[5], (D, D), jnp.float32) * (1.0 / np.sqrt(D))
        x = jax.random.normal(ks[6], (B, T, D), jnp.float32)
        return {'x': x, 'base_centers': base_centers, 'center_deltas': center_deltas, 'log_scales': log_scales, 'log_amps': log_amps, 'movement_scale_param': movement_scale_param, 'temperature': temperature, 'qkv_w': qkv_w, 'out_w': out_w}
    _L1_mix_all = _L1_mix_setup()
    _L1_mix_in = {k: v for k, v in _L1_mix_all.items() if k in ('base_centers', 'center_deltas', 'log_scales', 'log_amps', 'movement_scale_param', 'temperature', 'qkv_w', 'out_w')}
    del _L1_mix_all

    def _L1_ffn_setup():
        import jax, jax.numpy as jnp
        import numpy as np
        E = 64
        K = 2
        CAP = 512
        H = 512
        FFN = 256
        B, S = (8, 512)
        key = jax.random.key(seed)
        ks = jax.random.split(key, 6)
        hidden_states = jax.random.normal(ks[0], (B, S, H), dtype=jnp.float32)
        router_w = jax.random.normal(ks[1], (E, H), dtype=jnp.float32) * (0.01 / np.sqrt(H))
        w1 = jax.random.normal(ks[2], (FFN, H), dtype=jnp.float32) * (1.0 / np.sqrt(H))
        b1 = jnp.zeros((FFN,), dtype=jnp.float32)
        w2 = jax.random.normal(ks[3], (H, FFN), dtype=jnp.float32) * (1.0 / np.sqrt(FFN))
        b2 = jnp.zeros((H,), dtype=jnp.float32)
        return {'hidden_states': hidden_states, 'router_w': router_w, 'w1': w1, 'b1': b1, 'w2': w2, 'b2': b2}
    _L1_ffn_all = _L1_ffn_setup()
    _L1_ffn_in = {k: v for k, v in _L1_ffn_all.items() if k in ('router_w', 'w1', 'b1', 'w2', 'b2')}
    del _L1_ffn_all
    return {'x': x, 'src': src, 'dst': dst, 'edge_attr_64': edge_attr_64, 'L0_gnn_Wq': _L0_gnn_in['Wq'], 'L0_gnn_bq': _L0_gnn_in['bq'], 'L0_gnn_Wk': _L0_gnn_in['Wk'], 'L0_gnn_bk': _L0_gnn_in['bk'], 'L0_gnn_Wv': _L0_gnn_in['Wv'], 'L0_gnn_bv': _L0_gnn_in['bv'], 'L0_mix_w_qkv': _L0_mix_in['w_qkv'], 'L0_mix_w_out': _L0_mix_in['w_out'], 'L0_mix_b_out': _L0_mix_in['b_out'], 'L0_ffn_switch_w': _L0_ffn_in['switch_w'], 'L0_ffn_switch_b': _L0_ffn_in['switch_b'], 'L0_ffn_expert_w': _L0_ffn_in['expert_w'], 'L0_ffn_expert_b': _L0_ffn_in['expert_b'], 'L1_gnn_u': _L1_gnn_in['u'], 'L1_gnn_W1': _L1_gnn_in['W1'], 'L1_gnn_b1': _L1_gnn_in['b1'], 'L1_gnn_W2': _L1_gnn_in['W2'], 'L1_gnn_b2': _L1_gnn_in['b2'], 'L1_mix_base_centers': _L1_mix_in['base_centers'], 'L1_mix_center_deltas': _L1_mix_in['center_deltas'], 'L1_mix_log_scales': _L1_mix_in['log_scales'], 'L1_mix_log_amps': _L1_mix_in['log_amps'], 'L1_mix_movement_scale_param': _L1_mix_in['movement_scale_param'], 'L1_mix_temperature': _L1_mix_in['temperature'], 'L1_mix_qkv_w': _L1_mix_in['qkv_w'], 'L1_mix_out_w': _L1_mix_in['out_w'], 'L1_ffn_router_w': _L1_ffn_in['router_w'], 'L1_ffn_w1': _L1_ffn_in['w1'], 'L1_ffn_b1': _L1_ffn_in['b1'], 'L1_ffn_w2': _L1_ffn_in['w2'], 'L1_ffn_b2': _L1_ffn_in['b2']}

def reference(x, src, dst, edge_attr_64, L0_gnn_Wq, L0_gnn_bq, L0_gnn_Wk, L0_gnn_bk, L0_gnn_Wv, L0_gnn_bv, L0_mix_w_qkv, L0_mix_w_out, L0_mix_b_out, L0_ffn_switch_w, L0_ffn_switch_b, L0_ffn_expert_w, L0_ffn_expert_b, L1_gnn_u, L1_gnn_W1, L1_gnn_b1, L1_gnn_W2, L1_gnn_b2, L1_mix_base_centers, L1_mix_center_deltas, L1_mix_log_scales, L1_mix_log_amps, L1_mix_movement_scale_param, L1_mix_temperature, L1_mix_qkv_w, L1_mix_out_w, L1_ffn_router_w, L1_ffn_w1, L1_ffn_b1, L1_ffn_w2, L1_ffn_b2):
    import jax
    import jax.numpy as jnp

    def _L0_gnn_ref(x, edge_index, Wq, bq, Wk, bk, Wv, bv):
        import jax, jax.numpy as jnp
        import numpy as np
        NEG = -1000000.0
        q = x @ Wq + bq
        k = x @ Wk + bk
        v = x @ Wv + bv
        N = x.shape[0]
        adj = jnp.zeros((N, N), dtype=x.dtype).at[edge_index[0], edge_index[1]].set(1.0)
        a = q @ k.T / jnp.sqrt(jnp.asarray(q.shape[-1], dtype=x.dtype))
        a = a * adj + (1.0 - adj) * NEG
        attn = jax.nn.softmax(a, axis=-1)
        return attn @ v

    def _L0_mix_ref(x, w_qkv, w_out, b_out):
        import jax, jax.numpy as jnp
        import numpy as np
        B, N, DIM = (4, 256, 512)
        H, HD = (8, 64)
        SCALE = 1.0 / float(np.sqrt(HD))
        b, n, c = x.shape
        qkv = x @ w_qkv
        qkv = qkv.reshape(b, n, 3, H, HD)
        q = qkv[:, :, 0].transpose(0, 2, 1, 3)
        k = qkv[:, :, 1].transpose(0, 2, 1, 3)
        v = qkv[:, :, 2].transpose(0, 2, 1, 3)
        attn = jnp.einsum('bhnd,bhmd->bhnm', q, k) * (SCALE / n)
        out = jnp.einsum('bhnm,bhmd->bhnd', attn, v)
        out = out.transpose(0, 2, 1, 3).reshape(b, n, H * HD)
        return out @ w_out + b_out

    def _L0_ffn_ref(x, switch_w, switch_b, expert_w, expert_b):
        import jax, jax.numpy as jnp
        import numpy as np
        CAPACITY_FACTOR = 1.2
        B, S, D = x.shape
        E = switch_w.shape[0]
        N = B * S
        xf = x.reshape(N, D)
        logits = xf @ switch_w.T + switch_b
        probs = jax.nn.softmax(logits, axis=-1)
        route_probs = jnp.max(probs, axis=-1)
        routes = jnp.argmax(probs, axis=-1)
        oh = jax.nn.one_hot(routes, E, dtype=jnp.int32)
        pos = jnp.take_along_axis(jnp.cumsum(oh, axis=0), routes[:, None], axis=1)[:, 0] - 1
        capacity = int(CAPACITY_FACTOR * N / E)
        keep = pos < capacity
        buf = jnp.zeros((E, capacity, D), dtype=xf.dtype).at[routes, pos].set(xf)
        y = jnp.einsum('ecd,efd->ecf', buf, expert_w) + expert_b[:, None, :]
        gathered = y[routes, jnp.minimum(pos, capacity - 1)]
        out = jnp.where(keep[:, None], gathered, xf) * route_probs[:, None]
        return out.reshape(B, S, D)

    def _L1_gnn_ref(x, edge_index, edge_attr, u, batch, W1, b1, W2, b2):
        import jax, jax.numpy as jnp
        import numpy as np
        N_NODES = 6250
        N_EDGES = 100000
        NODE_IN = 512
        EDGE_IN = 64
        HID = 1024
        col = edge_index[1]
        summed = jax.ops.segment_sum(edge_attr, col, num_segments=x.shape[0])
        count = jax.ops.segment_sum(jnp.ones((edge_attr.shape[0],), dtype=x.dtype), col, num_segments=x.shape[0])
        agg = summed / jnp.maximum(count, 1.0)[:, None]
        h = jnp.concatenate([x, agg], axis=-1)
        h = jax.nn.relu(h @ W1 + b1)
        return x + h @ W2 + b2

    def _L1_mix_ref(x, base_centers, center_deltas, log_scales, log_amps, movement_scale_param, temperature, qkv_w, out_w):
        import jax, jax.numpy as jnp
        import numpy as np
        B, T, D = (4, 1024, 512)
        H, S = (8, 16)
        HD = D // H
        PRUNE_THRESH = 0.02
        b, t, d = x.shape
        h, s, hd = base_centers.shape
        qkv = (x @ qkv_w.T).reshape(b, t, 3, h, hd)
        q, k, v = (qkv[:, :, 0], qkv[:, :, 1], qkv[:, :, 2])
        ms = jax.nn.sigmoid(movement_scale_param[0]) * 0.1
        centers = base_centers + center_deltas * ms
        scales = jnp.clip(jnp.exp(log_scales), 0.0001, 2.0)
        amps = jnp.exp(log_amps)
        eff_amps = amps * (amps > PRUNE_THRESH).astype(amps.dtype)
        inv_var = 0.5 / (scales ** 2 + 1e-08)
        c_sq = jnp.sum(centers ** 2, -1)

        def splat_weights(tok):
            d2 = jnp.sum(tok ** 2, -1)[..., None] + c_sq[None, None] - 2.0 * jnp.einsum('bthd,hsd->bths', tok, centers)
            return jnp.exp(-d2 * inv_var[None, None]) * eff_amps[None, None]
        qw = splat_weights(q)
        kw = splat_weights(k)
        temp = jnp.maximum(temperature[0], 0.1)
        logits = jnp.einsum('bihs,bjhs->bijh', qw, kw) / temp
        attn = jax.nn.softmax(logits, axis=2)
        out = jnp.einsum('bijh,bjhd->bihd', attn, v).reshape(b, t, d)
        return out @ out_w.T

    def _L1_ffn_ref(hidden_states, router_w, w1, b1, w2, b2):
        import jax, jax.numpy as jnp
        import numpy as np
        E = 64
        K = 2
        CAP = 512
        H = 512
        FFN = 256
        B, S = (8, 512)
        orig_shape = hidden_states.shape
        x = hidden_states.reshape(-1, orig_shape[-1])
        T = x.shape[0]
        N = T * K
        logits = jnp.einsum('th,eh->te', x, router_w)
        probs_full = jax.nn.softmax(logits, axis=-1)
        probs, idx = jax.lax.top_k(probs_full, K)
        flat_e = idx.reshape(-1)
        flat_p = probs.reshape(-1)
        order = jnp.argsort(flat_e, stable=True)
        sorted_e = flat_e[order]
        counts = jnp.zeros((E,), jnp.int32).at[flat_e].add(1)
        offsets = jnp.concatenate([jnp.zeros((1,), jnp.int32), jnp.cumsum(counts)[:-1]])
        pos = jnp.arange(N, dtype=jnp.int32) - offsets[sorted_e]
        keep = pos < CAP
        slot = sorted_e * CAP + jnp.minimum(pos, CAP - 1)
        dest = jnp.where(keep, slot, E * CAP)
        tok = order // K
        buf = jnp.zeros((E * CAP + 1, x.shape[-1]), x.dtype).at[dest].set(x[tok])
        buf = buf[:-1]
        h = jax.nn.gelu(jnp.einsum('nh,fh->nf', buf, w1) + b1, approximate=False)
        y = jnp.einsum('nf,hf->nh', h, w2) + b2
        gate = jnp.where(keep, flat_p[order], 0.0)
        contrib = y[jnp.minimum(slot, E * CAP - 1)] * gate[:, None]
        out = jnp.zeros_like(x).at[tok].add(contrib)
        return out.reshape(orig_shape)
    edge_index = jnp.stack([src, dst])
    batch0 = jnp.zeros((1024,), jnp.int32)
    xn = _layernorm(x, axis=-1)
    x = x + _L0_gnn_ref(xn, edge_index, L0_gnn_Wq, L0_gnn_bq, L0_gnn_Wk, L0_gnn_bk, L0_gnn_Wv, L0_gnn_bv) + _L0_mix_ref(xn[None], L0_mix_w_qkv, L0_mix_w_out, L0_mix_b_out)[0]
    x = x + _L0_ffn_ref(_layernorm(x, axis=-1)[None], L0_ffn_switch_w, L0_ffn_switch_b, L0_ffn_expert_w, L0_ffn_expert_b)[0]
    xn = _layernorm(x, axis=-1)
    x = x + _L1_gnn_ref(xn, edge_index, edge_attr_64, L1_gnn_u, batch0, L1_gnn_W1, L1_gnn_b1, L1_gnn_W2, L1_gnn_b2) + _L1_mix_ref(xn[None], L1_mix_base_centers, L1_mix_center_deltas, L1_mix_log_scales, L1_mix_log_amps, L1_mix_movement_scale_param, L1_mix_temperature, L1_mix_qkv_w, L1_mix_out_w)[0]
    x = x + _L1_ffn_ref(_layernorm(x, axis=-1)[None], L1_ffn_router_w, L1_ffn_w1, L1_ffn_b1, L1_ffn_w2, L1_ffn_b2)[0]
    return x

_drawn_inputs = setup_inputs


def setup_inputs(seed=0):
    import zlib

    import numpy as np

    out = dict(_drawn_inputs(seed))
    spreads = {'L0_mix_b_out': (0.0, 0.744),
     'L0_ffn_switch_b': (0.0, 0.8),
     'L0_ffn_expert_b': (0.0, 2.0),
     'L1_gnn_u': (0.0, 0.1),
     'L1_gnn_b1': (0.0, 0.8),
     'L1_gnn_b2': (0.0, 0.798),
     'L1_ffn_b1': (0.0, 2.0),
     'L1_ffn_b2': (0.0, 2.0)}
    factors = {'edge_attr_64': 14.594,
     'L0_gnn_bq': 64.0,
     'L0_gnn_bk': 64.0,
     'L0_gnn_bv': 32.744,
     'L0_mix_w_qkv': 8.0,
     'L0_mix_w_out': 8.0,
     'L1_ffn_router_w': 64.0,
     'L1_ffn_w1': 6.566,
     'L1_ffn_w2': 6.058,
     'L0_ffn_switch_w': 5.984,
     'L0_ffn_expert_w': 8.0,
     'L1_mix_qkv_w': 8.0,
     'L1_mix_out_w': 8.0}
    for name, (base, spread) in spreads.items():
        noise = np.random.default_rng([zlib.crc32(name.encode()), seed]).standard_normal(out[name].shape)
        drawn = base * np.exp(spread * noise) if base else spread * noise
        out[name] = jnp.asarray(drawn.astype(out[name].dtype))
    for name, factor in factors.items():
        out[name] = (out[name] * factor).astype(out[name].dtype)
    return out
```

```python
from contextlib import ExitStack

import numpy as np

import concourse.bass as bass
from concourse import mybir

F32 = mybir.dt.float32
F32R = mybir.dt.float32r
I32 = mybir.dt.int32
BF16 = mybir.dt.bfloat16
U32 = mybir.dt.uint32
U16 = mybir.dt.uint16
ALU = mybir.AluOpType
ACT = mybir.ActivationFunctionType
AX = mybir.AxisListType.X

P = 128
N = 1024
D = 512
T = N // P
C = D // P
HALF = N // 2
TH = T // 2
EDGES = 33792
EK = 8
CHUNK = P * EK
NCH = EDGES // CHUNK
EA = 64
SCATTERS = EDGES // P
BATCH = 12
EXPERTS = 16
CAP = int(1.2 * N / EXPERTS)
SLOTS = EXPERTS * CAP
WRING = 6
E2 = 64
CAP2 = 512
HID = 1024
FFN = 256
HEADS = 8
PAIRS = HEADS // 2
HD = D // HEADS
SPLATS = 16
KROWS = 3 * SPLATS
MROWS = KROWS + 2
EPS = 1e-5
NEG = -1000000.0
BIG = 3.0e38
ATT_SCALE = float(1.0 / np.sqrt(np.float32(D)))
MIX_SCALE = 1.0 / float(np.sqrt(HD)) / N

K_ID, K_TRI, K_IOTA, K_ONE = 0, 128, 256, 384
K_TOK, K_REV16, K_REV64, K_LOQ, K_LOK, K_LO8, K_CUP, K_CDN, K_NHI = 512, 520, 536, 600, 601, 602, 610, 643, 676
K_COLS = 684


def const_table():
    t = np.zeros((P, K_COLS), np.float32)
    r = np.arange(P)
    t[:, K_ID:K_ID + P] = np.eye(P)
    t[:, K_TRI:K_TRI + P] = r[:, None] < r[None, :]
    t[:, K_IOTA:K_IOTA + P] = r[None, :]
    t[:, K_ONE:K_ONE + P] = 1.0
    t[:, K_TOK:K_TOK + T] = SLOTS + r[:, None] + P * np.arange(T)[None, :]
    t[:, K_REV16:K_REV16 + EXPERTS] = EXPERTS - np.arange(EXPERTS)[None, :]
    t[:, K_REV64:K_REV64 + E2] = E2 - np.arange(E2)[None, :]
    t[:, K_LOQ] = -((r % 64 // SPLATS) == 2).astype(np.float32)
    t[:, K_LOK] = -((r % 64 // SPLATS) == 1).astype(np.float32)
    t[:, K_LO8:K_LO8 + T] = P * np.arange(T)[None, :]
    t[:, K_NHI:K_NHI + T] = -(P * np.arange(T)[None, :] + P - 1)
    t[:, K_CUP:K_CUP + NCH] = 1 + np.arange(NCH)[None, :]
    t[:, K_CDN:K_CDN + NCH] = NCH - np.arange(NCH)[None, :]
    return t


def plan_jobs():
    jobs = []
    turn = [0]

    def add(*name, bank=None):
        if bank is None:
            bank = turn[0] % 8
            turn[0] += 1
        jobs.append((name, bank))

    add("span", bank=7)
    add("spanT", bank=7)
    for t in range(T):
        add("xT", 0, t, bank=t % 4)
    for m in range(C):
        add("G", m, bank=4 + m)
    for m in range(C):
        add("GK", m)
    add("VK")
    for m in range(C):
        add("M", m)
    for m in range(C):
        add("B", m)
    add("U")
    add("R")
    for m in range(C):
        add("A", m)
    for th in range(2):
        for c in range(C):
            add("Q", c, th)
    for n in range(T + 1):
        if n < T:
            add("seg", n)
        if n > 0:
            add("segT", n - 1)
    for it in range(T):
        for jh in range(2):
            add("S", it, jh)
    for t in range(T):
        add("V", t)
    for t in range(T + 1):
        if t < T:
            add("PT", t, 0, bank=2 * (t % 2))
            add("PT", t, 1, bank=2 * (t % 2) + 1)
        if t > 0:
            add("AV", t - 1, bank=4 + t % 2)
    turn[0] = 0
    for t in range(T):
        add("xT", 1, t)
    add("rt0")
    add("cum0")
    add("tot0")
    for e in range(EXPERTS):
        add("eT", e, bank=4 + e % 2)
        add("eY", e, bank=6 + e % 2)
    turn[0] = 0
    for t in range(T):
        add("xT", 2, t)
    add("aggT", 0)
    add("aggT", 1)
    for hh in range(2):
        for th in range(2):
            for m in range(C):
                add("H", hh, th, m)
            for t in range(TH):
                add("HW", hh, th, t)
    add("csq")
    for side in "qk":
        for c in range(PAIRS):
            for th in range(2):
                add("p", side, c, th)
            for th in range(2):
                add("d2", side, c, th)
    for step in attention_steps():
        if step[0] in ("L", "mT", "oU", "oT"):
            add(*step, bank=6 if step[:2] == ("L", 1) else 0)
        elif step[0] == "V1":
            add(*step, bank=2 + step[1] % 4)
        elif step[0] == "E":
            add(*step, bank=2 + 2 * (step[2] % 2))
        elif step[0] == "O" and step[2] == T - 1:
            add("O", step[1], bank=6)
    turn[0] = 0
    for t in range(T):
        add("X3", t)
    for t in range(T):
        add("xT", 3, t)
    add("rt1")
    add("cum1")
    add("tot1")
    for f in range(2):
        for th in range(2):
            add("F1", f, th)
    for t in range(T):
        add("F2", t)
    return jobs


def attention_steps():
    steps = []
    for t in range(T):
        steps += [("L", 0, t), ("L", 1, t)]
        if t % 2:
            steps.append(("V1", t // 2))
    steps.append(("mT", 0))
    for t in range(TH, T):
        steps += [("L", 2, t - TH), ("V1", t)]
    later = [("L", h, it) for h in range(2, HEADS) for it in range(T)][TH:]
    flat = [(h, jt) for h in range(HEADS) for jt in range(T)]
    for n, (h, jt) in enumerate(flat):
        steps.append(("E", h, jt))
        if later:
            steps.append(later.pop(0))
        if n % (2 * T) == 2 * T - TH and h // 2 + 1 < PAIRS:
            steps.append(("mT", h // 2 + 1))
        if n > 0:
            steps.append(("O", *flat[n - 1]))
        if h and jt == 2:
            steps.append(("oU", h - 1))
        if h >= 2 and n % (2 * T) == 5:
            steps.append(("oT", h // 2 - 1))
    steps += [("O", *flat[-1]), ("oU", HEADS - 1), ("oT", PAIRS - 1)]
    return steps


WEIGHTS = [("mWk", 1, None), ("mWv", 3, None), ("mWo", 1, ("GK", 3)), ("mWqT", 3, ("VK",)),
           ("WqT", 0, ("M", 3)), ("WkT", 2, ("B", 3)), ("Wv", 3, ("Q", 3, 1)),
           ("W1a", 0, ("AV", 7)), ("W2a", 1, ("AV", 7)), ("W1b", 0, ("H", 0, 1, 3)),
           ("W2b", 1, ("HW", 0, 1, 3)), ("Lq", 0, ("H", 1, 1, 3)), ("Lk", 1, ("HW", 1, 1, 3)),
           ("Lv", 0, ("p", "q", 3, 1)), ("Lo", 1, ("p", "k", 3, 1)), ("F", 0, ("V1", 7))]


def build(nc, a):
    jobs = plan_jobs()
    index = {name: i for i, (name, _) in enumerate(jobs)}
    assert len(index) == len(jobs)
    bank_of = dict(jobs)
    turn_of, seen = {}, [0] * 8
    for name, b in jobs:
        turn_of[name] = seen[b]
        seen[b] += 1
    windex = {name: i for i, (name, _, _) in enumerate(WEIGHTS)}

    with ExitStack() as ctx:
        def sb(name, shape, dt=F32):
            return ctx.enter_context(nc.sbuf_tensor(name, shape, dt))

        def sem(name):
            return ctx.enter_context(nc.semaphore(name))

        xn = sb("xn", [P, T, D])
        arena = sb("arena", [P, NCH * EK * (EA + 1)])
        wraw = sb("wraw", [P, 2, C * D])
        slot = [sb(f"slot{i}", [P, 2, C, D], F32R) for i in range(4)]
        xT = [sb(f"xT{i}", [P, 2, C, HALF], F32R) for i in range(2)]
        kst = sb("kst", [P, K_COLS])
        dstf = sb("dstf", [P, NCH, EK])
        key = sb("key", [P, SCATTERS], U32)
        rowa = sb("rowa", [P, D])
        rowb = sb("rowb", [P, D])
        agg = sb("agg", [P, T, EA])
        cols = sb("cols", [P, 192])
        keyring = sb("keyring", [P, 2, BATCH], U32)
        zero16 = sb("zero16", [P, 1], U16)
        spans = sb("spans", [P, 2, NCH])
        plan = sb("plan", [1, 2, T], I32)
        idx = sb("idx", [P, 2, T], U32)
        bank = ctx.enter_context(nc.psum_tensor("bank", [P, 8, 512], F32))

        iota = kst[:, K_IOTA:K_IOTA + P]
        ident = kst[:, K_ID:K_ID + P]
        tri = kst[:, K_TRI:K_TRI + P]
        ones = kst[:, K_ONE:K_ONE + P]
        zero_row = kst[0:1, K_TRI:K_TRI + 1].bitcast(BF16)[:, 0:1].to_broadcast([1, P])
        one_row = kst[0:1, K_ONE:K_ONE + 2 * P].bitcast(BF16)

        edges = arena[:, :].rearrange("p (c k d) -> p c k d", k=EK, d=EA + 1)
        AW = T * D
        xres = arena[:, 0:AW].rearrange("p (t d) -> p t d", t=T)
        scores = arena[:, AW:3 * AW].rearrange("p (t j) -> p t j", t=T)
        nadj = arena[:, 3 * AW:4 * AW].bitcast(U16).rearrange("p (t j) -> p t j", t=T)
        ering = arena[:, AW:AW + WRING * C * D].rearrange("p (w c d) -> p w c d", w=WRING, c=C)
        gath = arena[:, AW:2 * AW].rearrange("p (t d) -> p t d", t=T)
        aggT = arena[0:EA + 1, AW:AW + N]
        w1e = arena[0:EA + 1, AW + N:AW + 2 * N]
        vone = arena[:, AW:AW + T * HEADS * (HD + 1)].rearrange("p (t h m) -> p t h m", t=T, h=HEADS)
        otmp = arena[0:HD + 1, 3 * AW - 2 * N:3 * AW].rearrange("p (r i) -> p r i", r=2)
        pring = arena[:, 3 * AW:4 * AW].rearrange("p (r i) -> p r i", r=4)
        tail = arena[:, 4 * AW:4 * AW + 6 * P].rearrange("p (r t e) -> p r t e", r=6, t=T)
        big6 = arena[:, AW:AW + 8 * D].rearrange("p (r t e) -> p r t e", r=8, t=T)
        onehot = xn[:, 0:2, :].rearrange("p k (t n) -> p k t n", n=P)
        ecopy = xn[:, 2:4, :][:, :, 0:4 * (EA + 1)].rearrange("p k (t d) -> p k t d", t=4)
        seg = xn[0:EA + 1, 4, 0:2 * P].rearrange("p (r n) -> p r n", r=2)
        qsq = xn[:, :, :].rearrange("p (r v a) d -> p r v (a d)", r=2, v=2)
        xb = [wraw[0:CAP, r, 0:D] for r in range(2)]
        eb = [wraw[0:CAP, r, D:2 * D] for r in range(2)]
        ey = [wraw[0:CAP, r, 2 * D:3 * D] for r in range(2)]
        xbT = [wraw[:, r, 3 * D:3 * D + C * CAP].rearrange("p (c s) -> p c s", c=C) for r in range(2)]
        srci = wraw[:, 1, 0:SCATTERS].bitcast(I32)
        dsti = wraw[:, 1, SCATTERS:2 * SCATTERS].bitcast(I32)
        dstc = wraw[:, 1, 2 * SCATTERS:3 * SCATTERS].bitcast(I32)
        cblk = agg[:, :, :].rearrange("p (c a) e -> p c (a e)", c=PAIRS)
        onesblk = kst[:, K_IOTA:K_IOTA + P]
        mneg = [agg[0:2 * T, 2 * v:2 * v + 2, :].rearrange("p a e -> p (a e)").bitcast(F32R) for v in range(2)]
        wdump = agg[:, :, :].rearrange("p t e -> p (t e)")
        ctr = dstf[:, :, :].rearrange("p c k -> p (c k)")[:, 0:3 * PAIRS * SPLATS].rearrange(
            "p (v c s) -> p v c s", v=3, c=PAIRS)

        stat = cols[:, 0:48].rearrange("p (t s) -> p t s", t=T)
        mv = cols[:, 48:64].rearrange("p (t s) -> p t s", t=T)
        rstd = cols[:, 64:72]
        c_a, c_b, c_c, c_d, c_e, c_f, c_g, c_h = (cols[:, 72 + 8 * i:80 + 8 * i] for i in range(8))
        ucol = cols[:, 136:140]
        bbcol = cols[:, 140:141]
        bqc, bkc = cols[:, 144:148], cols[:, 148:152]
        rcol = cols[:, 152:160]
        f1c = cols[:, 168:170]
        tmpc = cols[:, 170:172]
        sbrow = sb("sbrow", [P, EXPERTS])
        swT = sb("swT", [P, C, EXPERTS])
        rwT = wraw[:, 0, 0:C * E2].rearrange("p (c e) -> p c e", c=C)
        par = sb("par", [P, 10, PAIRS])
        mx = sb("mx", [P, 2, 2, T])

        def dram(name, shape, dt=F32):
            return nc.dram_tensor(name, shape, dt, kind="Internal").ap()

        adjd = dram("not_adjacent", (N * N, 1), U16)
        xbuf = dram("expert_rows", (SLOTS + N, D))
        ybuf = dram("expert_results", (SLOTS, D))
        mdram = dram("row_maxima", (PAIRS, 2, 2, N))

        mm_done = sem("mm_done")
        evicted = [sem(f"evicted{b}") for b in range(8)]
        hi_done = sem("hi_done")
        w_in = [sem(f"w_in{i}") for i in range(2)]
        w_hi = sem("w_hi")
        w_split = sem("w_split")
        x_in = [sem(f"x_in{i}") for i in range(4)]
        const_in = sem("const_in")
        ids_in = sem("ids_in")
        rows_in = sem("rows_in")
        small_in = sem("small_in")
        edges_in = [sem(f"edges_in{i}") for i in range(3)]
        fills = sem("fills")
        adj_cleared = sem("adj_cleared")
        buf_cleared = sem("buf_cleared")
        keys_ready = sem("keys_ready")
        dst_ready = sem("dst_ready")
        key_copied = sem("key_copied")
        batch_ready = sem("batch_ready")
        scattered = [sem(f"scattered{i}") for i in range(2)]
        adj_in = sem("adj_in")
        xres_in = sem("xres_in")
        span_done = sem("span_done")
        plan_ready = sem("plan_ready")
        onehots = sem("onehots")
        edges_copied = sem("edges_copied")
        halves = sem("half_chunks_summed")
        var_ready = sem("var_ready")
        std_ready = sem("std_ready")
        xn_ready = sem("xn_ready")
        masked = sem("masked")
        exp_done = sem("exp_done")
        p_ready = sem("p_ready")
        chain = sem("vector_chain")
        achain = sem("scalar_chain")
        logit_ready = sem("logit_ready")
        lexp_done = sem("lexp_done")
        onehot_ready = sem("onehot_ready")
        route_ready = sem("route_ready")
        rows_sent = sem("rows_sent")
        xb_in = [sem(f"xb_in{i}") for i in range(2)]
        eb_in = [sem(f"eb_in{i}") for i in range(2)]
        ew_in = [sem(f"ew_in{i}") for i in range(WRING)]
        y_out = [sem(f"y_out{i}") for i in range(2)]
        gathered = [sem(f"gathered{i}") for i in range(T)]
        res_ready = sem("res_ready")
        w1e_in = sem("w1e_in")
        l1_in = sem("l1_in")
        rowa_in = sem("rowa_in")
        rowb_in = sem("rowb_in")
        bias_added = sem("bias_added")
        rows_added = sem("rows_added")
        par_exp = sem("par_exp")
        par_in = sem("par_in")
        blk_ready = sem("blk_ready")
        st_ready = sem("st_ready")
        p_used = sem("p_used")
        m_stored = sem("m_stored")
        m_in = sem("m_in")
        o_ready = sem("o_ready")
        f_ready = sem("f_ready")
        rw_in = sem("rw_in")
        y_ready = sem("y_ready")
        out_sent = sem("out_sent")

        def finished(eng, *name):
            eng.wait_ge(mm_done, index[name] + 1)

        def emptied(eng, *name):
            eng.wait_ge(evicted[bank_of[name]], turn_of[name] + 1)

        def at(*name):
            return bank[:, bank_of[name], :]

        def hl(buf, *where):
            return (buf[(slice(None), 0, *where)], buf[(slice(None), 1, *where)])

        def f32(ap):
            return ap.bitcast(F32)

        hi_order = {}
        def hi_number(name):
            return hi_order[name]

        split_jobs = ([("xT", 0, t) for t in range(T)] + [("G", m) for m in range(C)] + [("GK", m) for m in range(C)]
                      + [("VK",)] + [("M", m) for m in range(C)] + [("B", m) for m in range(C)]
                      + [("A", m) for m in range(C)] + [("Q", c, th) for th in range(2) for c in range(C)]
                      + [("V", t) for t in range(T)]
                      + [("PT", t, g) for t in range(T) for g in range(2)]
                      + [("xT", 1, t) for t in range(T)] + [("xT", 2, t) for t in range(T)]
                      + [("H", hh, th, m) for hh in range(2) for th in range(2) for m in range(C)]
                      + [("oT", c) for c in range(PAIRS)] + [("xT", 3, t) for t in range(T)])
        for i, name in enumerate(split_jobs):
            hi_order[name] = i

        def turned(t):
            return hl(xT[t // TH], slice(None), slice(t % TH * P, t % TH * P + P))

        def bankcols(name, t=None):
            return at(*name).rearrange("p (c s) -> p c s", c=C)

        def target(name):
            k = name[0]
            if k == "xT":
                return turned(name[2]), bankcols(name)
            if k == "G":
                return hl(slot[0], name[1]), at(*name)
            if k == "GK":
                return hl(slot[2], name[1]), at(*name)
            if k == "M":
                return hl(slot[2], name[1]), at(*name)
            if k == "B":
                return hl(slot[1], name[1]), at(*name)
            if k == "A":
                return hl(slot[3], name[1]), at(*name)
            if k == "Q":
                return hl(slot[2 * name[2]], name[1]), at(*name)
            if k == "V":
                return hl(slot[2 * (name[1] // TH)], name[1] % TH), at(*name)
            if k == "PT":
                ring = 2 * (name[1] % 2) + name[2]
                return hl(slot[3], ring), at(*name)
            if k == "H":
                return hl(slot[2 + name[2]], name[3]), at(*name)
            raise KeyError(name)

        blk = ctx.enter_context(nc.Block())

        @blk.sync
        def _(sp):
            sp.dma_start(kst[:, :], a["consts"]).then_inc(const_in, 16)
            xv = a["x"].rearrange("(t p) d -> p t d", p=P)
            for i in range(4):
                sp.dma_start(xn[:, 2 * i:2 * i + 2, :], xv[:, 2 * i:2 * i + 2, :]).then_inc(x_in[i], 16)
            for ap, name in ((srci, "src_scatter"), (dsti, "dst_scatter"), (dstc, "dst_chunks")):
                sp.dma_start(ap, a[name]).then_inc(ids_in, 16)

            wsrc = {
                "mWk": a["L0_mix_w_qkv"].rearrange("(c p) n -> p c n", p=P)[:, :, D:2 * D],
                "mWv": a["L0_mix_w_qkv"].rearrange("(c p) n -> p c n", p=P)[:, :, 2 * D:3 * D],
                "mWo": a["L0_mix_w_out"].rearrange("(c p) n -> p c n", p=P),
                "mWqT": a["mWqT"].rearrange("(c p) n -> p c n", p=P),
                "WqT": a["WqT"].rearrange("(c p) n -> p c n", p=P),
                "WkT": a["WkT"].rearrange("(c p) n -> p c n", p=P),
                "Wv": a["L0_gnn_Wv"].rearrange("(c p) n -> p c n", p=P),
                "W1a": a["L1_gnn_W1"][0:D].rearrange("(c p) n -> p c n", p=P)[:, :, 0:D],
                "W1b": a["L1_gnn_W1"][0:D].rearrange("(c p) n -> p c n", p=P)[:, :, D:2 * D],
                "W2a": a["L1_gnn_W2"][0:D].rearrange("(c p) n -> p c n", p=P),
                "W2b": a["L1_gnn_W2"][D:2 * D].rearrange("(c p) n -> p c n", p=P),
                "Lq": a["qkvT"].rearrange("(c p) n -> p c n", p=P)[:, :, 0:D],
                "Lk": a["qkvT"].rearrange("(c p) n -> p c n", p=P)[:, :, D:2 * D],
                "Lv": a["qkvT"].rearrange("(c p) n -> p c n", p=P)[:, :, 2 * D:3 * D],
                "Lo": a["outT"].rearrange("(c p) n -> p c n", p=P),
            }

            def load_weight(name):
                i = windex[name]
                dst = wraw[:, i % 2, :].rearrange("p (c n) -> p c n", c=C)
                if i >= 2:
                    sp.wait_ge(w_split, i - 1)
                if name == "F":
                    sp.dma_start(wraw[:, i % 2, 0:C * FFN].rearrange("p (c n) -> p c n", c=C),
                                 a["w1T"].rearrange("(c p) n -> p c n", p=P)).then_inc(w_in[i % 2], 16)
                    sp.dma_start(wraw[:, i % 2, C * FFN:2 * C * FFN].rearrange("p (c n) -> p c n", c=2),
                                 a["w2T"].rearrange("(c p) n -> p c n", p=P)).then_inc(w_in[i % 2], 16)
                else:
                    sp.dma_start(dst, wsrc[name]).then_inc(w_in[i % 2], 16)

            load_weight("mWk")
            sp.wait_ge(dst_ready, 1)
            sp.wait_ge(keys_ready, 1)
            load_weight("mWv")
            sp.wait_ge(fills, 2)
            sp.dma_start(adjd.rearrange("(p a j) b -> p a (j b)", p=P, a=T),
                         agg[:, :, :].rearrange("p t e -> p (t e)").bitcast(U16).unsqueeze(1)
                         .to_broadcast([P, T, N])).then_inc(adj_cleared, 16)
            sp.dma_start(xbuf[0:SLOTS].rearrange("(p e) d -> p e d", p=CAP),
                         rowb[0:CAP, :].unsqueeze(1).to_broadcast([CAP, EXPERTS, D])).then_inc(buf_cleared, 16)
            for name, dst in (("bq_col", bqc), ("bk_col", bkc)):
                sp.dma_start(dst, a[name]).then_inc(small_in, 16)
            sp.dma_start(swT[:, :, :], a["swT"].rearrange("(c p) e -> p c e", p=P)).then_inc(small_in, 16)
            sp.dma_start(sbrow[:, :], a["L0_ffn_switch_b"].rearrange("(a e) -> a e", a=1)
                         .to_broadcast([P, EXPERTS])).then_inc(small_in, 16)
            sp.dma_start(f1c, a["ffn_b1_col"]).then_inc(small_in, 16)
            sp.dma_start(rowa[:, :], a["L0_gnn_bv"].rearrange("(a d) -> a d", a=1).to_broadcast([P, D])).then_inc(rows_in, 16)
            sp.wait_ge(buf_cleared, 16)
            sp.dma_start(rowb[:, :], a["L0_mix_b_out"].rearrange("(a d) -> a d", a=1).to_broadcast([P, D])).then_inc(rows_in, 16)
            ev = a["edge_attr_64"].rearrange("(c p k) d -> p c k d", p=P, k=EK)
            third = NCH // 3
            for i in range(3):
                for c in range(i * third, (i + 1) * third):
                    sp.dma_start(edges[:, c, :, 0:EA], ev[:, c]).then_inc(edges_in[i], 16)
            for name in ("mWo", "mWqT", "WqT", "WkT", "Wv"):
                load_weight(name)
            for n in range(T):
                emptied(sp, "seg", n)
            sp.dma_start(xres, a["x"].rearrange("(t p) d -> p t d", p=P)).then_inc(xres_in, 16)
            for i in range(2):
                sp.wait_ge(scattered[i], 16 * SCATTERS // 2)
            sp.dma_start(nadj, adjd.rearrange("(t p j) b -> p t (j b)", p=P, t=T)).then_inc(adj_in, 16)

            def load_expert(e):
                if e >= WRING:
                    finished(sp, "eY", e - WRING)
                sp.dma_start(ering[:, e % WRING], a["ewT"][e].rearrange("(c p) f -> p c f", p=P)).then_inc(ew_in[e % WRING], 16)

            def load_rows(e):
                if e >= 2:
                    finished(sp, "eT", e - 2)
                sp.dma_start(xb[e % 2], xbuf[e * CAP:(e + 1) * CAP]).then_inc(xb_in[e % 2], 16)
                if e >= 2:
                    emptied(sp, "eY", e - 2)
                sp.dma_start(eb[e % 2], a["L0_ffn_expert_b"][e:e + 1].to_broadcast([CAP, D])).then_inc(eb_in[e % 2], 16)

            sp.wait_ge(p_ready, T)
            for t in range(T):
                finished(sp, "PT", t, 1)
            for e in range(WRING):
                load_expert(e)
            sp.wait_ge(rows_sent, 16 * T)
            for e in range(EXPERTS):
                load_rows(e)
                if e + WRING - 1 < EXPERTS and e >= 1:
                    load_expert(e + WRING - 1)
            for e in (EXPERTS - 2, EXPERTS - 1):
                finished(sp, "eY", e)
                emptied(sp, "eY", e)
            sp.wait_ge(y_out[0], 16 * EXPERTS // 2)
            sp.wait_ge(y_out[1], 16 * EXPERTS // 2)
            load_weight("W1a")
            load_weight("W2a")
            sp.dma_start(par[:, 0:2, :], a["splat_par"]).then_inc(par_in, 16)
            sp.dma_start(ctr[:, 0:2, :, :], a["splat_ctr"]).then_inc(par_in, 16)
            sp.dma_start(par[:, 8, 0:1], a["L1_mix_movement_scale_param"].rearrange("(a b) -> a b", a=1).to_broadcast([P, 1])).then_inc(par_in, 16)
            sp.dma_start(par[:, 8, 1:2], a["L1_mix_temperature"].rearrange("(a b) -> a b", a=1).to_broadcast([P, 1])).then_inc(par_in, 16)
            sp.wait_ge(bias_added, 1)
            sp.dma_start(rowa[:, :], a["L1_gnn_b2"].rearrange("(a d) -> a d", a=1).to_broadcast([P, D])).then_inc(rowa_in, 16)
            sp.dma_start(rowb[:, :], a["L1_ffn_b2"].rearrange("(a d) -> a d", a=1).to_broadcast([P, D])).then_inc(rowb_in, 16)
            sp.wait_ge(res_ready, 2 * T)
            sp.dma_start(w1e[0:EA], a["L1_gnn_W1"][D:D + EA]).then_inc(w1e_in, 16)
            sp.dma_start(w1e[EA:EA + 1], a["L1_gnn_b1"].rearrange("(a n) -> a n", a=1)).then_inc(w1e_in, 16)
            for name in ("W1b", "W2b", "Lq", "Lk", "Lv", "Lo"):
                load_weight(name)
            for c in range(PAIRS):
                emptied(sp, "mT", c)
                if c:
                    sp.wait_ge(m_in, 64 * c)
                for v in range(2):
                    sp.dma_start(mdram[c, v].rearrange("b (t i) -> (b t) i", t=T), f32(mneg[v])).then_inc(m_stored, 16)
                sp.wait_ge(m_stored, 32 * (c + 1))
                for b in range(2):
                    for v in range(2):
                        row = 64 * b + KROWS + v
                        sp.dma_start(f32(slot[2][row:row + 1, c // 2, 2 * (c % 2):2 * (c % 2) + 2, :]),
                                     mdram[c, v, b:b + 1].rearrange("b (a i) -> b a i", a=2)).then_inc(m_in, 16)
                if c == 0:
                    load_weight("F")
            sp.wait_ge(w_split, len(WEIGHTS))
            sp.dma_start(rwT, a["rwT"].rearrange("(c p) e -> p c e", p=P)).then_inc(rw_in, 16)
            ov = a["out"].rearrange("(t p) d -> t p d", p=P)
            for t in range(T):
                sp.wait_ge(y_ready, t + 1)
                sp.dma_start(ov[t], xres[:, t, :]).then_inc(out_sent, 16)
            sp.wait_ge(out_sent, 16 * T)

        @blk.gpsimd
        def _(pool):
            pool.memset(zero16[:, :], 0).then_inc(fills, 1)
            pool.wait_ge(fills, 3)
            pool.wait_ge(adj_cleared, 16)
            pool.wait_ge(keys_ready, 1)
            def scatter_half(i, h):
                pool.tensor_copy(keyring[:, h, :], key[:, bass.ds(i * (2 * BATCH) + h * BATCH, BATCH)]).then_inc(key_copied, 1)
                pool.wait_ge(key_copied, i * 2 + (h + 1))
                pool.sem_inc(batch_ready, 1)
                for b in range(BATCH):
                    pool.indirect_dma_start(adjd, bass.IndirectOffsetOnAxis(ap=keyring[:, h, b:b + 1], axis=0),
                                            zero16[:, :], None).then_inc(scattered[h], 16)

            for h in range(2):
                scatter_half(0, h)
            with pool.Fori(1, SCATTERS // (2 * BATCH)) as i:
                for h in range(2):
                    pool.wait_ge(scattered[h], i * (16 * BATCH))
                    scatter_half(i, h)
            pool.wait_ge(buf_cleared, 16)
            pool.wait_ge(route_ready, 1)
            for t in range(T):
                pool.wait_ge(xn_ready, T + t + 1)
                pool.indirect_dma_start(xbuf, bass.IndirectOffsetOnAxis(ap=idx[:, 0, t:t + 1], axis=0),
                                        xn[:, t, :], None).then_inc(rows_sent, 16)
            pool.wait_ge(route_ready, 2)
            pool.wait_ge(y_out[0], 16 * EXPERTS // 2)
            pool.wait_ge(y_out[1], 16 * EXPERTS // 2)
            finished(pool, "eY", EXPERTS - 1)
            for t in range(T):
                pool.indirect_dma_start(gath[:, t, :], None, ybuf,
                                        bass.IndirectOffsetOnAxis(ap=idx[:, 1, t:t + 1], axis=0)).then_inc(gathered[t], 16)

            pool.wait_ge(rowa_in, 16)
            for t in range(T):
                pool.wait_ge(xn_ready, 2 * T + t + 1)
                pool.tensor_tensor(xres[:, t, :], xres[:, t, :], xn[:, t, :], ALU.add).then_inc(rows_added, 1)
            for t in range(T):
                pool.wait_ge(rows_added, t + 1)
                pool.tensor_tensor(xres[:, t, :], xres[:, t, :], rowa[:, :], ALU.add).then_inc(rows_added, 1)

        @blk.tensor
        def _(pe):
            def open_bank(*name):
                if turn_of[name]:
                    pe.wait_ge(evicted[bank_of[name]], turn_of[name])
                return at(*name)

            def close(ins):
                ins.then_inc(mm_done, 1)

            def mm3(out, L, R, start, stop, **kw):
                pe.matmul(out, L[1], R[0], start=start, stop=False, **kw)
                pe.matmul(out, L[0], R[0], start=False, stop=False, **kw)
                return pe.matmul(out, L[0], R[1], start=False, stop=stop, **kw)

            def turn_rows(layer, t):
                pe.wait_ge(xn_ready, layer * T + t + 1)
                o = open_bank("xT", layer, t)
                for c in range(C):
                    ins = pe.transpose(o[:, c * P:(c + 1) * P], xn[:, t, c * P:(c + 1) * P], ident)
                close(ins)

            def xt(t, c):
                return hl(xT[t // TH], c, slice(t % TH * P, t % TH * P + P))

            def sl(s, c, lo=0, hi=D):
                return hl(slot[s], c, slice(lo, hi))

            def product(name, L, R, ks=C, waits=None):
                o = open_bank(*name)
                for k in range(ks):
                    if waits:
                        waits(k)
                    ins = mm3(o, L(k), R(k), k == 0, k == ks - 1)
                close(ins)

            def chunk(c):
                return slice(c * P, (c + 1) * P)

            pe.wait_ge(const_in, 16)
            pe.wait_ge(span_done, 1)
            o = open_bank("span")
            close(pe.transpose(o[0:2 * NCH, 0:P], spans[:, :, :].rearrange("p a c -> p (a c)"), ident))
            emptied(pe, "span")
            o = open_bank("spanT")
            close(pe.transpose(o[0:1, 0:2 * NCH], cols[0:2 * NCH, 172:173], ident[0:2 * NCH, 0:2 * NCH]))

            for t in range(T):
                turn_rows(0, t)
                for m in range(C):
                    if t == 0:
                        open_bank("G", m)
                    ins = pe.matmul(at("G", m), xn[:, t, chunk(m)], xn[:, t, :], start=t == 0, stop=t == T - 1)
                    if t == T - 1:
                        close(ins)
            for m in range(C):
                if m == 0:
                    pe.wait_ge(w_split, windex["mWk"] + 1)
                    for k in range(C):
                        emptied(pe, "G", k)
                product(("GK", m), lambda k: sl(0, k, m * P, m * P + P), lambda k: sl(1, k))
            pe.wait_ge(w_split, windex["mWv"] + 1)
            o = open_bank("VK")
            for p in range(C):
                for k in range(C):
                    if p == 0:
                        emptied(pe, "GK", k)
                    ins = mm3(o[:, chunk(p)], sl(3, k, p * P, p * P + P), sl(2, k, p * P, p * P + P), k == 0, k == C - 1)
            close(ins)
            pe.wait_ge(w_split, windex["mWo"] + 1)
            emptied(pe, "VK")
            for p in range(C):
                product(("M", p), lambda k: sl(0, 0, p * P, p * P + P), lambda k: sl(1, p), ks=1)
            pe.wait_ge(w_split, windex["mWqT"] + 1)
            for p in range(C):
                emptied(pe, "M", p)
            for m in range(C):
                product(("B", m), lambda k: sl(3, k, m * P, m * P + P), lambda k: sl(2, k))
            pe.wait_ge(w_split, windex["WkT"] + 1)
            pe.wait_ge(small_in, 80)
            o = open_bank("U")
            for m in range(C):
                for k in range(C):
                    for v in range(2):
                        pe.matmul(o[:, m:m + 1], f32(slot[2][:, v, k, chunk(m)]), bqc[:, k:k + 1],
                                  start=k == 0 and v == 0, stop=k == C - 1 and v == 1)
            for k in range(C):
                ins = pe.matmul(o[:, C:C + 1], bkc[:, k:k + 1].to_broadcast([P, P]), bqc[:, k:k + 1],
                                start=k == 0, stop=k == C - 1)
            close(ins)
            o = open_bank("R")
            for k in range(C):
                for v in range(2):
                    ins = pe.matmul(o, bkc[:, k:k + 1].to_broadcast([P, P]), f32(slot[0][:, v, k, :]),
                                    start=k == 0 and v == 0, stop=k == C - 1 and v == 1)
            close(ins)
            for m in range(C):
                product(("A", m), lambda k: sl(0, k, m * P, m * P + P), lambda k: sl(2, k))
            for m in range(C):
                emptied(pe, "A", m)
            for t in range(T):
                emptied(pe, "xT", 0, t)
            for th in range(2):
                for c in range(C):
                    product(("Q", c, th), lambda k: sl(3, k, c * P, c * P + P), lambda k: hl(xT[th], k))

            for i in range(3):
                pe.wait_ge(edges_in[i], 16 * (NCH // 3))
            pe.wait_ge(plan_ready, 1)
            for k in range(2):
                pe.nop().then_inc(halves, 1)
            count = pe.alloc_register("pe_half_chunks")
            pe.reg_mov(count, 0)
            for n in range(T + 1):
                if n < T:
                    o = open_bank("seg", n)[0:EA + 1, 0:P]
                    pe.matmul(o, zero_row[:, 0:EA + 1], one_row[:, 0:P], start=True, stop=False)
                    first = pe.value_load(plan[0:1, 0, n:n + 1], min_val=0, max_val=NCH - 1)
                    end = pe.value_load(plan[0:1, 1, n:n + 1], min_val=1, max_val=NCH)
                    with pe.Fori(first, end) as c:
                        done = pe.snap(count, min_val=0, max_val=2 * T * NCH)
                        for k in range(2):
                            pe.wait_ge(onehots, done + (k + 1))
                            pe.wait_ge(edges_copied, done + (k + 1))
                            for j in range(4):
                                ins = pe.matmul(o, ecopy[:, k, j, :], onehot[:, k, j, :], start=False, stop=False)
                            ins.then_inc(halves, 1)
                        pe.reg_add(count, count, 2)
                    close(pe.matmul(o, zero_row[:, 0:EA + 1], one_row[:, 0:P], start=False, stop=True))
                if n > 0:
                    emptied(pe, "seg", n - 1)
                    o = open_bank("segT", n - 1)
                    close(pe.transpose(o[:, 0:EA + 1], seg[:, (n - 1) % 2, :], ident[0:EA + 1, 0:EA + 1]))

            for th in range(2):
                for c in range(C):
                    emptied(pe, "Q", c, th)
            for it in range(T):
                for jh in range(2):
                    product(("S", it, jh), lambda k: hl(slot[2 * (it // TH)], k, slice(it % TH * P, it % TH * P + P)),
                            lambda k: hl(xT[jh], k))
            pe.wait_ge(w_split, windex["Wv"] + 1)
            for t in range(T):
                product(("V", t), lambda k: xt(t, k), lambda k: sl(3, k))
            for t in range(T):
                emptied(pe, "V", t)
            for m in range(C):
                emptied(pe, "B", m)
            for t in range(T + 1):
                if t < T:
                    pe.wait_ge(p_ready, t + 1)
                    for g in range(2):
                        o = open_bank("PT", t, g)
                        for j in range(4):
                            jt = 4 * g + j
                            ins = pe.transpose(o[:, chunk(j)], scores[:, t, jt * P:(jt + 1) * P], ident)
                        close(ins)
                if t > 0:
                    s = t - 1
                    o = open_bank("AV", s)
                    for k in range(C):
                        mm3(o, xt(s, k), sl(1, k), k == 0, False)
                    for g in range(2):
                        emptied(pe, "PT", s, g)
                        for j in range(4):
                            jt = 4 * g + j
                            ins = mm3(o, hl(slot[3], 2 * (s % 2) + g, chunk(j)), sl(2 * (jt // TH), jt % TH),
                                      False, jt == T - 1)
                    close(ins)

            for t in range(T):
                turn_rows(1, t)
            o = open_bank("rt0")
            for t in range(T):
                emptied(pe, "xT", 1, t)
                for k in range(C):
                    for v in range(2):
                        ins = pe.matmul(o[:, t * EXPERTS:(t + 1) * EXPERTS], f32(xt(t, k)[v]), swT[:, k, :],
                                        start=k == 0 and v == 0, stop=k == C - 1 and v == 1)
            close(ins)
            pe.wait_ge(onehot_ready, 1)
            oh0 = tail[:, 2, :, :].rearrange("p t e -> p (t e)")
            o = open_bank("cum0")
            close(pe.matmul(o[:, 0:P], tri, oh0, start=True, stop=True))
            o = open_bank("tot0")
            close(pe.matmul(o[:, 0:P], ones, oh0, start=True, stop=True))
            for e in range(EXPERTS):
                pe.wait_ge(xb_in[e % 2], 16 * (e // 2 + 1))
                o = open_bank("eT", e)
                for k in range(C):
                    ins = pe.transpose(o[:, k * CAP:(k + 1) * CAP], xb[e % 2][:, chunk(k)], ident[0:CAP, 0:CAP])
                close(ins)
                pe.wait_ge(ew_in[e % WRING], 16 * (e // WRING + 1))
                emptied(pe, "eT", e)
                o = open_bank("eY", e)
                for k in range(C):
                    ins = pe.matmul(o[0:CAP, :], xbT[e % 2][:, k, :], ering[:, e % WRING, k, :], start=k == 0, stop=k == C - 1)
                close(ins)

            for t in range(T):
                turn_rows(2, t)
            for g in range(2):
                o = open_bank("aggT", g)
                for j in range(4):
                    ins = pe.transpose(o[0:EA, chunk(j)], agg[:, 4 * g + j, :], ident)
                close(ins)
            pe.wait_ge(w1e_in, 32)
            for t in range(T):
                emptied(pe, "xT", 2, t)
            pe.wait_ge(blk_ready, 1)
            for g in range(2):
                emptied(pe, "aggT", g)
            for hh in range(2):
                for th in range(2):
                    pe.wait_ge(w_split, windex[("W1a", "W1b")[hh]] + 1)
                    for m in range(C):
                        o = open_bank("H", hh, th, m)
                        for k in range(C):
                            mm3(o, sl(0, k, m * P, m * P + P), hl(xT[th], k), k == 0, False)
                        ch = hh * C + m
                        close(pe.matmul(o, w1e[:, ch * P:(ch + 1) * P], aggT[:, th * HALF:(th + 1) * HALF], start=False, stop=True))
                    pe.wait_ge(w_split, windex[("W2a", "W2b")[hh]] + 1)
                    for t in range(TH):
                        product(("HW", hh, th, t), lambda k: hl(slot[2 + th], k, chunk(t)), lambda k: sl(1, k),
                                waits=lambda k: t == 0 and emptied(pe, "H", hh, th, k))

            pe.wait_ge(blk_ready, 2)
            o = open_bank("csq")
            for c in range(PAIRS):
                ins = pe.matmul(o[:, c:c + 1], qsq[:, 0, 0, chunk(c)], ones[:, 0:1], start=True, stop=True)
            close(ins)
            for n, side in enumerate("qk"):
                pe.wait_ge(w_split, windex[("Lq", "Lk")[n]] + 1)
                for c in range(PAIRS + 1):
                    if c < PAIRS:
                        for th in range(2):
                            product(("p", side, c, th), lambda k: sl(n, k, c * P, c * P + P), lambda k: hl(xT[th], k))
                    if c > 0:
                        g = n * PAIRS + c - 1
                        for th in range(2):
                            emptied(pe, "p", side, c - 1, th)
                        for th in range(2):
                            o = open_bank("d2", side, c - 1, th)
                            w = slice(th * HALF, (th + 1) * HALF)
                            pe.matmul(o, onesblk, qsq[:, g % 2, 1, w], start=True, stop=False)
                            close(pe.matmul(o, cblk[:, c - 1, :], qsq[:, g % 2, 0, w], start=False, stop=True))
            def stack(s, c, rows, lo, hi):
                v = slot[s][:, :, :, :].rearrange("p a (b x) d -> p (a b) (x d)", x=2)
                return v[rows, c, lo:hi]

            def krows(h, n):
                return slice(64 * (h % 2), 64 * (h % 2) + n)

            def two(o, lhsT, s, c, rows):
                for jh in range(2):
                    ins = pe.matmul(bank[:, o + jh, :], lhsT, stack(s, c, rows, jh * HALF, (jh + 1) * HALF), start=True, stop=True)
                return ins

            pe.wait_ge(st_ready, 4 * PAIRS)
            pe.wait_ge(w_split, windex["Lv"] + 1)
            for side in "qk":
                for c in range(PAIRS):
                    for th in range(2):
                        emptied(pe, "d2", side, c, th)
            for step in attention_steps():
                if step[0] in ("L", "E", "oU", "oT") or (step[0] == "O" and step[2] == 0):
                    name = step if step[0] != "O" else ("O", step[1])
                    open_bank(*name)
                if step == ("E", 0, 0):
                    for t in range(T):
                        emptied(pe, "V1", t)
                    emptied(pe, "L", 1, T - 1)
                if step[0] == "L":
                    _, h, it = step
                    r = krows(h, KROWS)
                    close(two(bank_of[step], stack(2, h // 2, r, it * P, (it + 1) * P), 3, h // 2, r))
                elif step[0] == "V1":
                    product(step, lambda k: xt(step[1], k), lambda k: sl(0, k))
                elif step[0] == "mT":
                    c = step[1]
                    emptied(pe, "L", 2 * c + 1, T - 1)
                    o = open_bank(*step)
                    close(pe.transpose(o[0:2 * T, 0:P], mx[:, c % 2].rearrange("p b t -> p (b t)"), ident))
                elif step[0] == "oU":
                    h = step[1]
                    emptied(pe, "O", h)
                    for it in range(T):
                        w = slice(it % TH * (HD + 1), (it % TH + 1) * (HD + 1))
                        ins = pe.transpose(bank[:, it // TH, w], otmp[:, h % 2, chunk(it)], ident[0:HD + 1, 0:HD + 1])
                    close(ins)
                elif step[0] == "oT":
                    c = step[1]
                    pe.wait_ge(o_ready, 2 * (c + 1))
                    for it in range(T):
                        ins = pe.transpose(bank[:, it // TH, chunk(it % TH)], xn[:, it, chunk(c)], ident)
                    close(ins)
                elif step[0] == "E":
                    _, h, jt = step
                    pe.wait_ge(m_in, 64 * (h // 2 + 1))
                    r = krows(h, MROWS)
                    close(two(bank_of[step], stack(3, h // 2, r, jt * P, (jt + 1) * P), 2, h // 2, r))
                else:
                    _, h, jt = step
                    n = h * T + jt
                    emptied(pe, "E", h, jt)
                    for ih in range(2):
                        ins = pe.matmul(bank[0:HD + 1, 6 + ih, :], vone[:, jt, h, :], pring[:, n % 4, ih * HALF:(ih + 1) * HALF],
                                        start=jt == 0, stop=jt == T - 1)
                    if jt == T - 1:
                        close(ins)
                    else:
                        ins.then_inc(p_used, 1)
            for step in (("E", HEADS - 1, T - 2), ("E", HEADS - 1, T - 1), ("oT", PAIRS - 1)):
                emptied(pe, *step)
            pe.wait_ge(w_split, windex["Lo"] + 1)
            for t in range(T):
                product(("X3", t), lambda k: xt(t, k), lambda k: sl(1, k))

            for t in range(T):
                turn_rows(3, t)
            pe.wait_ge(rw_in, 16)
            o = open_bank("rt1")
            for t in range(T):
                emptied(pe, "xT", 3, t)
                for k in range(C):
                    for v in range(2):
                        ins = pe.matmul(o[:, t * E2:(t + 1) * E2], f32(xt(t, k)[v]), rwT[:, k, :],
                                        start=k == 0 and v == 0, stop=k == C - 1 and v == 1)
            close(ins)
            ohs = big6[:, 4].rearrange("p t e -> p (t e)")
            pe.wait_ge(onehot_ready, 2)
            close(pe.matmul(open_bank("cum1"), tri, ohs, start=True, stop=True))
            close(pe.matmul(open_bank("tot1"), ones, ohs, start=True, stop=True))
            fw = slot[0][:, :, :, :].rearrange("p v c d -> p v (c d)")
            for f in range(2):
                for th in range(2):
                    product(("F1", f, th), lambda k: hl(fw, slice(k * FFN + f * P, k * FFN + f * P + P)), lambda k: hl(xT[th], k))
            for t in range(T):
                product(("F2", t), lambda k: hl(slot[2], 2 * k + t // TH, chunk(t % TH)),
                        lambda k: hl(fw, slice(C * FFN + k * D, C * FFN + (k + 1) * D)), ks=2,
                        waits=lambda k: t % TH == 0 and pe.wait_ge(f_ready, 2 * k + t // TH + 1))

        def send_y(act, e):
            emptied(act, "eY", e)
            act.dma_start(ybuf[e * CAP:(e + 1) * CAP], ey[e % 2]).then_inc(y_out[e % 2], 16)

        def vk_at(s, v, rows, cs):
            return s[rows, v, 0, :].rearrange("p (c e) -> p c e", c=C)[:, :, cs]

        @blk.scalar
        def _(act):
            steps = [0]

            def link(ins):
                steps[0] += 1
                ins.then_inc(achain, 1)
                act.wait_ge(achain, steps[0])

            def split_weight(name):
                i = windex[name]
                _, s, after = WEIGHTS[i]
                act.wait_ge(w_in[i % 2], 16 * (i // 2 + 1) + (16 if name == "F" else 0))
                if after:
                    finished(act, *after)
                act.activation(slot[s][:, 0, :, :].rearrange("p c d -> p (c d)"), wraw[:, i % 2, :], ACT.Copy).then_inc(w_hi, 1)

            def hi(name, **kw):
                (h, _), src = target(name)
                finished(act, *name)
                act.activation(h, src, kw.pop("func", ACT.Copy), **kw).then_inc(hi_done, 1)

            def deviation(layer):
                act.wait_ge(var_ready, layer + 1)
                act.activation(rstd, rstd, ACT.Sqrt).then_inc(std_ready, 1)

            deviation(0)
            for t in range(T):
                hi(("xT", 0, t))
            split_weight("mWk")
            split_weight("mWv")
            for m in range(C):
                hi(("G", m))
            for m in range(C):
                hi(("GK", m))
            split_weight("mWo")
            finished(act, "VK")
            vkb = bankcols(("VK",))
            for b in range(2):
                r = slice(64 * b, 64 * b + 64)
                ins = act.activation(vk_at(slot[0], 0, r, r), vkb[r, :, r], ACT.Copy, scale=MIX_SCALE)
            ins.then_inc(hi_done, 1)
            split_weight("mWqT")
            for m in range(C):
                hi(("M", m))
            split_weight("WqT")
            for m in range(C):
                hi(("B", m))
            split_weight("WkT")
            for m in range(C):
                hi(("A", m))
            emptied(act, "U")
            for th in range(2):
                for c in range(C):
                    hi(("Q", c, th), func=ACT.Identity, bias=ucol[:, c:c + 1])
            split_weight("Wv")
            emptied(act, "R")
            for i in range(3):
                act.wait_ge(edges_in[i], 16 * (NCH // 3))
            act.wait_ge(plan_ready, 1)
            count = act.alloc_register("act_half_chunks")
            act.reg_mov(count, 0)
            for n in range(T):
                first = act.value_load(plan[0:1, 0, n:n + 1], min_val=0, max_val=NCH - 1)
                end = act.value_load(plan[0:1, 1, n:n + 1], min_val=1, max_val=NCH)
                with act.Fori(first, end) as c:
                    done = act.snap(count, min_val=0, max_val=2 * T * NCH)
                    for k in range(2):
                        act.wait_ge(halves, done + (k + 1))
                        part = edges[:, bass.ds(c, 1), 4 * k:4 * k + 4, :].rearrange("p c k d -> p (c k) d")
                        act.activation(ecopy[:, k, :, :], part, ACT.Copy).then_inc(edges_copied, 1)
                    act.reg_add(count, count, 2)
            for n in range(T):
                emptied(act, "seg", n)
            for it in range(T):
                for jh in range(2):
                    finished(act, "S", it, jh)
                    act.activation(scores[:, it, jh * HALF:(jh + 1) * HALF], at("S", it, jh), ACT.Identity,
                                   bias=rcol[:, it:it + 1], scale=ATT_SCALE).then_inc(evicted[bank_of[("S", it, jh)]], 1)
            for t in range(T):
                hi(("V", t))
            for t in range(T + 1):
                if t < T:
                    act.wait_ge(masked, t + 1)
                    act.activation(scores[:, t, :], scores[:, t, :], ACT.Exp, bias=c_a[:, t:t + 1],
                                   accum_out=c_b[:, t:t + 1]).then_inc(exp_done, 1)
                if t > 0:
                    for g in range(2):
                        name = ("PT", t - 1, g)
                        if t - 1 >= 2:
                            finished(act, "AV", t - 3)
                        hi(name)
            deviation(1)
            for t in range(T):
                hi(("xT", 1, t))
            act.wait_ge(logit_ready, 1)
            act.activation(tail[:, 1], tail[:, 1], ACT.Exp).then_inc(lexp_done, 1)
            for e in range(EXPERTS):
                finished(act, "eT", e)
                if e >= 2:
                    finished(act, "eY", e - 2)
                act.activation(xbT[e % 2], at("eT", e)[:, 0:C * CAP].rearrange("p (c s) -> p c s", c=C), ACT.Copy).then_inc(evicted[bank_of[("eT", e)]], 1)
                if e >= 1:
                    send_y(act, e - 1)
            send_y(act, EXPERTS - 1)
            split_weight("W1a")
            split_weight("W2a")
            deviation(2)
            for t in range(T):
                hi(("xT", 2, t))
            act.wait_ge(par_in, 64)
            act.activation(par[:, 2:4, :], par[:, 0:2, :], ACT.Exp).then_inc(par_exp, 1)
            act.activation(par[:, 9, 0:1], par[:, 8, 0:1], ACT.Exp, scale=-1.0).then_inc(par_exp, 1)
            for hh in range(2):
                for th in range(2):
                    for m in range(C):
                        name = ("H", hh, th, m)
                        if hh:
                            finished(act, "HW", 0, th, TH - 1)
                        hi(name, func=ACT.Relu)
                if hh == 0:
                    split_weight("W1b")
                    split_weight("W2b")
            split_weight("Lq")
            split_weight("Lk")
            for n, side in enumerate("qk"):
                for c in range(PAIRS + 1):
                    if c < PAIRS:
                        g = n * PAIRS + c
                        for th in range(2):
                            name = ("p", side, c, th)
                            finished(act, *name)
                            if g >= 2:
                                finished(act, "d2", "qk"[(g - 2) // PAIRS], (g - 2) % PAIRS, th)
                            if g == 0:
                                finished(act, "csq")
                                act.wait_ge(xn_ready, 3 * T)
                            w = slice(th * HALF, (th + 1) * HALF)
                            act.activation(qsq[:, g % 2, 0, w], at(*name), ACT.Copy)
                            act.activation(qsq[:, g % 2, 1, w], at(*name), ACT.Square).then_inc(evicted[bank_of[name]], 1)
                    if c > 0:
                        g = n * PAIRS + c - 1
                        emptied(act, "csq")
                        for th in range(2):
                            name = ("d2", side, c - 1, th)
                            finished(act, *name)
                            if 2 * g + th >= 4:
                                act.wait_ge(st_ready, 2 * g + th - 3)
                            act.activation(pring[:, (2 * g + th) % 4, 0:HALF], at(*name), ACT.Exp,
                                           bias=par[:, 5, c - 1:c], scale=par[:, 4, c - 1:c]).then_inc(evicted[bank_of[name]], 1)
                if side == "q":
                    split_weight("Lv")
            split_weight("Lo")
            act.wait_ge(st_ready, 4 * PAIRS)
            for step in attention_steps():
                if step[0] == "E":
                    _, h, jt = step
                    n = h * T + jt
                    finished(act, *step)
                    if n >= 4:
                        if (n - 4) % T == T - 1:
                            finished(act, "O", (n - 4) // T)
                        else:
                            act.wait_ge(p_used, (n - 4) // T * (T - 1) + (n - 4) % T + 1)
                    b = bank_of[step]
                    act.activation(pring[:, n % 4, :], bank[:, b:b + 2, :].rearrange("p a i -> p (a i)"),
                                   ACT.Exp).then_inc(evicted[b], 1)
                if step[0] == "O" and step[2] == T - 1:
                    h = step[1]
                    finished(act, "O", h)
                    if h >= 2:
                        finished(act, "oU", h - 2)
                    act.activation(otmp[:, h % 2, :], bank[0:HD + 1, 6:8, :].rearrange("p a i -> p (a i)"), ACT.Copy).then_inc(evicted[6], 1)
                if step[0] == "oT":
                    finished(act, *step)
                    for g in range(2):
                        ins = act.activation(xT[g][:, 0, step[1], :], bank[:, g, :], ACT.Copy)
                    ins.then_inc(hi_done, 1)
                if step == ("E", 6, 1):
                    split_weight("F")
            deviation(3)
            for t in range(T):
                hi(("xT", 3, t))
            act.wait_ge(logit_ready, 2)
            act.activation(big6[:, 1], big6[:, 1], ACT.Exp).then_inc(lexp_done, 1)
            for f in range(2):
                for th in range(2):
                    name = ("F1", f, th)
                    finished(act, *name)
                    act.activation(xn[:, 2 * f + th, :], at(*name), ACT.Gelu, bias=f1c[:, f:f + 1]).then_inc(evicted[bank_of[name]], 1)

        @blk.vector
        def _(dve):
            steps = [0]

            def link(ins):
                steps[0] += 1
                ins.then_inc(chain, 1)
                dve.wait_ge(chain, steps[0])

            def split_weight(name):
                i = windex[name]
                s = WEIGHTS[i][1]
                dve.wait_ge(w_hi, i + 1)
                flat = slot[s][:, :, :, :].rearrange("p v c d -> p v (c d)")
                dve.tensor_tensor(flat[:, 1], wraw[:, i % 2, :], f32(flat[:, 0]), ALU.subtract).then_inc(w_split, 1)

            def lo(name, bias=None, op=ALU.add):
                (h, l), src = target(name)
                dve.wait_ge(hi_done, hi_number(name) + 1)
                if bias is None:
                    ins = dve.tensor_tensor(l, src, f32(h), ALU.subtract)
                else:
                    ins = dve.scalar_tensor_tensor(l, src, bias, f32(h), op, ALU.subtract)
                ins.then_inc(evicted[bank_of[name]], 1)

            def moments(t, src):
                link(dve.bn_stats(stat[:, t, :], src))
                return dve.bn_aggr(mv[:, t, :], stat[:, t, :])

            def normalise(layer, src):
                dve.tensor_scalar(rstd, mv[:, :, 1], EPS, None, ALU.add).then_inc(var_ready, 1)
                dve.wait_ge(std_ready, layer + 1)
                link(dve.reciprocal(rstd, rstd))
                for t in range(T):
                    dve.tensor_scalar(xn[:, t, :], src(t), mv[:, t, 0:1], rstd[:, t:t + 1], ALU.subtract, ALU.mult).then_inc(xn_ready, 1)

            dve.memset(agg[:, :, :].rearrange("p t e -> p (t e)").bitcast(U16), 1).then_inc(fills, 1)
            dve.memset(rowb[:, :], 0.0).then_inc(fills, 1)
            link(dve.memset(edges[:, :, :, EA:EA + 1], 1.0))
            dve.wait_ge(ids_in, 48)
            dve.scalar_tensor_tensor(key[:, :], srci, float(N), dsti, ALU.mult, ALU.add).then_inc(keys_ready, 1)
            dve.tensor_copy(dstf[:, :, :].rearrange("p c k -> p (c k)"), dstc).then_inc(dst_ready, 1)
            dve.wait_ge(dst_ready, 1)
            link(dve.tensor_reduce(spans[:, 0, :], dstf[:, :, :], AX, ALU.min))
            link(dve.tensor_reduce(spans[:, 1, :], dstf[:, :, :], AX, ALU.max))
            dve.tensor_scalar(spans[:, 0, :], spans[:, 0, :], -1.0, None, ALU.mult).then_inc(span_done, 1)
            for t in range(T):
                dve.wait_ge(x_in[t // 2], 16)
                link(moments(t, xn[:, t, :]))
            normalise(0, lambda t: xn[:, t, :])
            finished(dve, "span")
            dve.tensor_reduce(cols[0:2 * NCH, 172:173], at("span")[0:2 * NCH, 0:P], AX, ALU.max).then_inc(evicted[bank_of[("span",)]], 1)
            finished(dve, "spanT")
            scratch = slot[2][0:1, :, :, :].rearrange("p v c d -> p (v c d)")
            span = scratch[:, 0:2 * NCH]
            dve.tensor_copy(span, at("spanT")[0:1, 0:2 * NCH]).then_inc(evicted[bank_of[("spanT",)]], 1)
            for t in range(T):
                lo(("xT", 0, t))
            emptied(dve, "spanT")
            near = [scratch[:, 128 + 512 * i:128 + 512 * i + T * NCH].rearrange("p (n c) -> p n c", c=NCH) for i in range(3)]
            got = [scratch[:, 2048 + 32 * i:2048 + 32 * i + T] for i in range(4)]

            def over_n(ap):
                return ap.unsqueeze(1).to_broadcast([1, T, NCH])

            def over_c(col):
                return kst[0:1, col:col + T].unsqueeze(2).to_broadcast([1, T, NCH])

            link(dve.tensor_tensor(near[0], over_n(f32(span[:, NCH:2 * NCH])), over_c(K_LO8), ALU.is_ge))
            link(dve.tensor_tensor(near[1], over_n(f32(span[:, 0:NCH])), over_c(K_NHI), ALU.is_ge))
            link(dve.tensor_tensor(near[2], f32(near[0]), f32(near[1]), ALU.mult))
            link(dve.tensor_tensor(near[0], f32(near[2]), over_n(kst[0:1, K_CUP:K_CUP + NCH]), ALU.mult))
            link(dve.tensor_tensor(near[1], f32(near[2]), over_n(kst[0:1, K_CDN:K_CDN + NCH]), ALU.mult))
            link(dve.tensor_reduce(got[0], f32(near[0]), AX, ALU.max))
            link(dve.tensor_reduce(got[1], f32(near[1]), AX, ALU.max))
            link(dve.tensor_scalar(got[2], f32(got[1]), -1.0, float(NCH), ALU.mult, ALU.add))
            link(dve.tensor_scalar(got[2], f32(got[2]), float(NCH - 1), None, ALU.min))
            link(dve.tensor_scalar(got[3], f32(got[2]), 1.0, None, ALU.add))
            link(dve.tensor_tensor(got[3], f32(got[3]), f32(got[0]), ALU.max))
            dve.tensor_copy(plan[:, 0, :], f32(got[2]))
            dve.tensor_copy(plan[:, 1, :], f32(got[3])).then_inc(plan_ready, 1)
            split_weight("mWk")
            split_weight("mWv")
            for m in range(C):
                lo(("G", m))
            for m in range(C):
                lo(("GK", m))
            split_weight("mWo")
            finished(dve, "VK")
            link(dve.memset(f32(slot[0][0:64, :, 0, :].rearrange("p v (c e) -> p v c e", c=C)[:, :, :, 64:128]), 0.0))
            link(dve.memset(f32(slot[0][64:128, :, 0, :].rearrange("p v (c e) -> p v c e", c=C)[:, :, :, 0:64]), 0.0))
            dve.wait_ge(hi_done, hi_number(("VK",)) + 1)
            for b in range(2):
                r = slice(64 * b, 64 * b + 64)
                ins = dve.scalar_tensor_tensor(vk_at(slot[0], 1, r, r), bankcols(("VK",))[r, :, r], MIX_SCALE,
                                               f32(vk_at(slot[0], 0, r, r)), ALU.mult, ALU.subtract)
            ins.then_inc(evicted[bank_of[("VK",)]], 1)
            split_weight("mWqT")
            for m in range(C):
                lo(("M", m))
            split_weight("WqT")
            for m in range(C):
                lo(("B", m))
            split_weight("WkT")
            finished(dve, "U")
            dve.tensor_copy(cols[:, 136:141], at("U")[:, 0:C + 1]).then_inc(evicted[bank_of[("U",)]], 1)
            emptied(dve, "U")
            finished(dve, "R")
            dve.wait_ge(adj_cleared, 16)
            for t in range(T):
                ins = dve.tensor_tensor_reduce(wdump, xn[:, t, :], at("R"), 1.0, 0.0, ALU.mult, ALU.add, rcol[:, t:t + 1])
                link(ins)
            dve.tensor_scalar(rcol, rcol, bbcol, ATT_SCALE, ALU.add, ALU.mult).then_inc(evicted[bank_of[("R",)]], 1)
            for m in range(C):
                lo(("A", m))
            for th in range(2):
                for c in range(C):
                    lo(("Q", c, th), bias=ucol[:, c:c + 1])

            split_weight("Wv")

            def mean_features(n):
                finished(dve, "segT", n)
                o, c = at("segT", n), tmpc[:, n % 2:n % 2 + 1]
                link(dve.tensor_scalar(c, o[:, EA:EA + 1], 1.0, None, ALU.max))
                link(dve.reciprocal(c, c))
                dve.tensor_scalar(agg[:, n, :], o[:, 0:EA], c, None, ALU.mult).then_inc(evicted[bank_of[("segT", n)]], 1)

            count = dve.alloc_register("dve_half_chunks")
            dve.reg_mov(count, 0)
            dve.wait_ge(plan_ready, 1)
            for n in range(T):
                if n:
                    link(dve.tensor_scalar(dstf[:, :, :], dstf[:, :, :], float(-P), None, ALU.add))
                first = dve.value_load(plan[0:1, 0, n:n + 1], min_val=0, max_val=NCH - 1)
                end = dve.value_load(plan[0:1, 1, n:n + 1], min_val=1, max_val=NCH)
                with dve.Fori(first, end) as c:
                    done = dve.snap(count, min_val=0, max_val=2 * T * NCH)
                    for k in range(2):
                        dve.wait_ge(halves, done + (k + 1))
                        ids = dstf[:, bass.ds(c, 1), 4 * k:4 * k + 4].rearrange("p c k -> p (c k)")
                        dve.tensor_tensor(onehot[:, k, :, :], ids.unsqueeze(2).to_broadcast([P, 4, P]),
                                          iota.unsqueeze(1).to_broadcast([P, 4, P]), ALU.is_equal).then_inc(onehots, 1)
                    dve.reg_add(count, count, 2)
                finished(dve, "seg", n)
                if n >= 2:
                    finished(dve, "segT", n - 2)
                dve.tensor_copy(seg[:, n % 2, :], at("seg", n)[0:EA + 1, 0:P]).then_inc(evicted[bank_of[("seg", n)]], 1)
                if n > 0:
                    mean_features(n - 1)
            mean_features(T - 1)

            for t in range(T):
                lo(("V", t))
            dve.wait_ge(rows_in, 32)
            link(dve.tensor_tensor(rowa[:, :], rowa[:, :], rowb[:, :], ALU.add))
            dve.wait_ge(xres_in, 16)
            for t in range(T):
                ins = dve.tensor_tensor(xres[:, t, :], xres[:, t, :], rowa[:, :], ALU.add)
            ins.then_inc(bias_added, 1)
            dve.wait_ge(bias_added, 1)
            dve.wait_ge(adj_in, 16)
            link(dve.memset(tmpc[:, 0:1], NEG))

            def mask(t):
                for jh in range(2):
                    emptied(dve, "S", t, jh)
                link(dve.copy_predicated(scores[:, t, :], nadj[:, t, :], tmpc[:, 0:1].to_broadcast([P, N])))
                link(dve.tensor_reduce(c_c[:, t:t + 1], scores[:, t, :], AX, ALU.max))
                dve.tensor_scalar(c_a[:, t:t + 1], c_c[:, t:t + 1], -1.0, None, ALU.mult).then_inc(masked, 1)

            mask(0)
            for t in range(T + 2):
                if t + 1 < T:
                    mask(t + 1)
                if t < T:
                    dve.wait_ge(exp_done, t + 1)
                    link(dve.reciprocal(c_d[:, t:t + 1], c_b[:, t:t + 1]))
                    dve.tensor_scalar(scores[:, t, :], scores[:, t, :], c_d[:, t:t + 1], None, ALU.mult).then_inc(p_ready, 1)
                if 0 < t <= T:
                    for g in range(2):
                        lo(("PT", t - 1, g))
                if t > 1:
                    s = t - 2
                    finished(dve, "AV", s)
                    dve.tensor_tensor(xres[:, s, :], at("AV", s), xres[:, s, :], ALU.add).then_inc(evicted[bank_of[("AV", s)]], 1)
                    emptied(dve, "AV", s)
                    link(moments(s, xres[:, s, :]))
            normalise(1, lambda t: xres[:, t, :])
            for t in range(T):
                lo(("xT", 1, t))

            finished(dve, "rt0")

            def before(Z, tot, cum, n):
                for t in range(1, T):
                    ins = dve.tensor_tensor(Z[:, t, :], tot[:, t - 1, :], Z[:, t - 1, :], ALU.add)
                    if t < T - 1:
                        link(ins)
                ins.then_inc(evicted[bank_of[("tot" + n,)]], 1)
                emptied(dve, "tot" + n)
                dve.tensor_tensor(Z, cum, Z, ALU.add).then_inc(evicted[bank_of[("cum" + n,)]], 1)
                emptied(dve, "cum" + n)

            L, X, OH, Y = tail[:, 0], tail[:, 1], tail[:, 2], tail[:, 3]

            def over_e(ap, e):
                return ap.unsqueeze(2).to_broadcast([P, T, e])

            def over_t(lo_, e):
                return kst[:, lo_:lo_ + e].unsqueeze(1).to_broadcast([P, T, e])

            dve.tensor_tensor(L, at("rt0")[:, 0:P].rearrange("p (t e) -> p t e", t=T),
                              sbrow[:, :].unsqueeze(1).to_broadcast([P, T, EXPERTS]), ALU.add).then_inc(evicted[bank_of[("rt0",)]], 1)
            emptied(dve, "rt0")
            link(dve.tensor_reduce(c_a, L, AX, ALU.max))
            dve.tensor_tensor(X, L, over_e(c_a, EXPERTS), ALU.subtract).then_inc(logit_ready, 1)
            link(dve.tensor_tensor(OH, L, over_e(c_a, EXPERTS), ALU.is_equal))
            link(dve.tensor_tensor(Y, OH, over_t(K_REV16, EXPERTS), ALU.mult))
            link(dve.tensor_reduce(c_b, Y, AX, ALU.max))
            dve.tensor_tensor(OH, Y, over_e(c_b, EXPERTS), ALU.is_equal).then_inc(onehot_ready, 1)
            dve.wait_ge(lexp_done, 1)
            link(dve.tensor_reduce(c_c, X, AX, ALU.add))
            link(dve.reciprocal(c_c, c_c))
            finished(dve, "cum0")
            finished(dve, "tot0")
            tot = at("tot0")[:, 0:P].rearrange("p (t e) -> p t e", t=T)
            cum = at("cum0")[:, 0:P].rearrange("p (t e) -> p t e", t=T)
            Z = tail[:, 4]
            dve.wait_ge(onehot_ready, 1)
            link(dve.memset(Z[:, 0, :], 0.0))
            before(Z, tot, cum, "0")
            link(dve.tensor_tensor(Z, Z, OH, ALU.mult))
            link(dve.tensor_reduce(c_d, Z, AX, ALU.add))
            link(dve.tensor_scalar(c_e, c_b, -float(CAP), float(SLOTS), ALU.mult, ALU.add))
            link(dve.tensor_scalar(c_f, c_d, float(CAP), None, ALU.is_lt))
            link(dve.tensor_scalar(c_g, c_d, float(CAP - 1), None, ALU.min))
            link(dve.tensor_tensor(c_g, c_g, c_e, ALU.add))
            link(dve.tensor_scalar(c_h, c_f, -1.0, 1.0, ALU.mult, ALU.add))
            link(dve.tensor_tensor(c_d, c_g, c_f, ALU.mult))
            link(dve.tensor_tensor(c_e, kst[:, K_TOK:K_TOK + T], c_h, ALU.mult))
            dve.tensor_tensor(idx[:, 0, :], c_d, c_e, ALU.add).then_inc(route_ready, 1)
            dve.tensor_copy(idx[:, 1, :], c_g).then_inc(route_ready, 1)
            dve.wait_ge(route_ready, 2)
            link(dve.tensor_tensor(c_d, c_f, c_c, ALU.mult))
            link(dve.tensor_tensor(c_e, c_h, c_c, ALU.mult))
            for t in range(T):
                dve.scalar_tensor_tensor(xres[:, t, :], xn[:, t, :], c_e[:, t:t + 1], xres[:, t, :], ALU.mult, ALU.add).then_inc(res_ready, 1)
            for e in range(EXPERTS):
                finished(dve, "eY", e)
                dve.wait_ge(eb_in[e % 2], 16 * (e // 2 + 1))
                if e >= 2:
                    dve.wait_ge(y_out[e % 2], 16 * (e // 2))
                dve.tensor_tensor(ey[e % 2], at("eY", e)[0:CAP, :], eb[e % 2], ALU.add).then_inc(evicted[bank_of[("eY", e)]], 1)
            dve.wait_ge(res_ready, T)
            dve.wait_ge(rows_sent, 16 * T)
            for t in range(T):
                dve.wait_ge(gathered[t], 16)
                dve.scalar_tensor_tensor(xres[:, t, :], gath[:, t, :], c_d[:, t:t + 1], xres[:, t, :], ALU.mult, ALU.add).then_inc(res_ready, 1)
                dve.wait_ge(res_ready, T + t + 1)
                link(moments(t, xres[:, t, :]))
            normalise(2, lambda t: xres[:, t, :])
            split_weight("W1a")
            split_weight("W2a")
            for t in range(T):
                lo(("xT", 2, t))
            for g in range(2):
                finished(dve, "aggT", g)
                dve.tensor_copy(aggT[0:EA, g * HALF:(g + 1) * HALF], at("aggT", g)[0:EA, :]).then_inc(evicted[bank_of[("aggT", g)]], 1)
            dve.memset(aggT[EA:EA + 1, :], 1.0).then_inc(blk_ready, 1)
            dve.wait_ge(par_exp, 2)
            link(dve.tensor_scalar(par[:, 2, :], par[:, 2, :], 1e-4, 2.0, ALU.max, ALU.min))
            link(dve.tensor_tensor(par[:, 4, :], par[:, 2, :], par[:, 2, :], ALU.mult))
            link(dve.tensor_scalar(par[:, 4, :], par[:, 4, :], 1e-8, None, ALU.add))
            link(dve.reciprocal(par[:, 4, :], par[:, 4, :]))
            link(dve.tensor_scalar(par[:, 4, :], par[:, 4, :], -0.5, None, ALU.mult))
            link(dve.tensor_scalar(par[:, 6, :], par[:, 3, :], 0.02, None, ALU.is_gt))
            link(dve.tensor_tensor(par[:, 7, :], par[:, 6, :], par[:, 3, :], ALU.mult))
            link(dve.tensor_scalar(par[:, 8, 1:2], par[:, 8, 1:2], 0.1, None, ALU.max))
            link(dve.reciprocal(par[:, 8, 1:2], par[:, 8, 1:2]))
            link(dve.tensor_scalar(par[:, 6, :], par[:, 7, :], par[:, 8, 1:2], None, ALU.mult))
            link(dve.tensor_scalar(par[:, 9, 0:1], par[:, 9, 0:1], 1.0, None, ALU.add))
            link(dve.reciprocal(par[:, 9, 0:1], par[:, 9, 0:1]))
            link(dve.tensor_scalar(par[:, 9, 0:1], par[:, 9, 0:1], 0.1, None, ALU.mult))
            link(dve.scalar_tensor_tensor(ctr[:, 2], ctr[:, 1], par[:, 9, 0:1], ctr[:, 0], ALU.mult, ALU.add))
            link(dve.memset(cblk, 0.0))
            link(dve.memset(onesblk, 0.0))
            for b in range(2):
                r = slice(64 * b, 64 * b + 64)
                for j in range(3):
                    w = slice(64 * b + SPLATS * j, 64 * b + SPLATS * (j + 1))
                    dve.tensor_scalar(cblk[r, :, w], ctr[r, 2], -2.0, None, ALU.mult)
                link(dve.memset(onesblk[r, 64 * b:64 * b + KROWS], 1.0))
            flat = cblk.rearrange("p c r -> p (c r)")
            dve.wait_ge(rows_added, 2 * T)
            dve.wait_ge(xn_ready, 3 * T)
            dve.tensor_tensor(xn[:, 0, :], flat, flat, ALU.mult).then_inc(blk_ready, 1)
            for hh in range(2):
                for th in range(2):
                    for m in range(C):
                        lo(("H", hh, th, m), bias=0.0, op=ALU.max)
                    if hh == 0 and th == 1:
                        split_weight("W1b")
                    if hh == 1 and th == 1:
                        split_weight("Lq")
                    for t in range(TH):
                        s = th * TH + t
                        name = ("HW", hh, th, t)
                        finished(dve, *name)
                        if hh:
                            emptied(dve, "HW", 0, th, t)
                        else:
                            dve.wait_ge(rows_added, T + s + 1)
                        dve.tensor_tensor(xres[:, s, :], at(*name), xres[:, s, :], ALU.add).then_inc(evicted[bank_of[name]], 1)
                if hh == 0:
                    split_weight("W2b")
            split_weight("Lk")
            finished(dve, "csq")
            dve.scalar_tensor_tensor(par[:, 5, :], at("csq")[:, 0:PAIRS], 0.25, par[:, 4, :], ALU.mult, ALU.mult).then_inc(evicted[bank_of[("csq",)]], 1)
            for n, side in enumerate("qk"):
                for c in range(PAIRS):
                    for th in range(2):
                        i = 2 * (n * PAIRS + c) + th
                        emptied(dve, "d2", side, c, th)
                        w = pring[:, i % 4, 0:HALF]
                        wh = pring[:, i % 4, HALF:2 * HALF].bitcast(F32R)
                        link(dve.tensor_scalar(w, w, par[:, 6 + n, c:c + 1], None, ALU.mult))
                        link(dve.tensor_copy(wh, w))
                        dst = slot[2 + n][:, c // 2, 2 * (c % 2) + th, :]
                        col = (K_LOQ, K_LOK)[n]
                        dve.scalar_tensor_tensor(dst, f32(wh), kst[:, col:col + 1], w, ALU.mult, ALU.add).then_inc(st_ready, 1)
                if side == "q":
                    split_weight("Lv")
            split_weight("Lo")
            dve.memset(vone[:, :, :, HD:HD + 1], 1.0)

            def normalise_head(h):
                finished(dve, "oU", h)
                for g in range(2):
                    o = bank[:, g, 0:TH * (HD + 1)].rearrange("p (t m) -> p t m", t=TH)
                    r = c_a[:, g * TH:(g + 1) * TH]
                    link(dve.reciprocal(r.unsqueeze(2), o[:, :, HD:HD + 1]))
                    ins = dve.tensor_tensor(xn[:, g * TH:(g + 1) * TH, h * HD:(h + 1) * HD], o[:, :, 0:HD],
                                            r.unsqueeze(2).to_broadcast([P, TH, HD]), ALU.mult)
                    if g == 0:
                        link(ins)
                ins.then_inc(evicted[0], 1)
                emptied(dve, "oU", h)
                dve.sem_inc(o_ready, 1)

            for step in attention_steps():
                if step[0] == "L":
                    _, h, it = step
                    finished(dve, *step)
                    if h // 2 >= 2:
                        finished(dve, "mT", h // 2 - 2)
                    b = bank_of[step]
                    dve.tensor_reduce(mx[:, h // 2 % 2, h % 2, it:it + 1], bank[:, b:b + 2, :].rearrange("p a i -> p (a i)"),
                                      AX, ALU.max).then_inc(evicted[b], 1)
                elif step[0] == "V1":
                    t = step[1]
                    finished(dve, *step)
                    dve.tensor_copy(vone[:, t, :, 0:HD], at(*step).rearrange("p (h e) -> p h e", e=HD)).then_inc(evicted[bank_of[step]], 1)
                elif step[0] == "mT":
                    c = step[1]
                    finished(dve, *step)
                    if c:
                        dve.wait_ge(m_stored, 32 * c)
                    o = at(*step)[0:2 * T, 0:P]
                    link(dve.tensor_scalar(mneg[0], o, -1.0, None, ALU.mult))
                    dve.scalar_tensor_tensor(mneg[1], o, -1.0, f32(mneg[0]), ALU.mult, ALU.subtract).then_inc(evicted[0], 1)
                elif step[0] == "oU":
                    normalise_head(step[1])
                elif step[0] == "oT":
                    dve.wait_ge(hi_done, hi_number(step) + 1)
                    for g in range(2):
                        ins = dve.tensor_tensor(xT[g][:, 1, step[1], :], bank[:, g, :], f32(xT[g][:, 0, step[1], :]), ALU.subtract)
                    ins.then_inc(evicted[0], 1)
                if step == ("E", 6, 1):
                    split_weight("F")
            for t in range(T):
                finished(dve, "X3", t)
                dve.tensor_tensor(xres[:, t, :], at("X3", t), xres[:, t, :], ALU.add).then_inc(evicted[bank_of[("X3", t)]], 1)
                emptied(dve, "X3", t)
                link(moments(t, xres[:, t, :]))
            normalise(3, lambda t: xres[:, t, :])
            for t in range(T):
                lo(("xT", 3, t))

            L, X, O1, O2, OS, Y, Z, W = (big6[:, i] for i in range(8))
            finished(dve, "rt1")
            dve.tensor_copy(L, at("rt1").rearrange("p (t e) -> p t e", t=T)).then_inc(evicted[bank_of[("rt1",)]], 1)
            emptied(dve, "rt1")
            link(dve.tensor_reduce(c_a, L, AX, ALU.max))
            dve.tensor_tensor(X, L, over_e(c_a, E2), ALU.subtract).then_inc(logit_ready, 1)

            def first_of(oh, logits, greatest):
                link(dve.tensor_tensor(oh, logits, over_e(greatest, E2), ALU.is_equal))
                link(dve.tensor_tensor(Y, oh, over_t(K_REV64, E2), ALU.mult))
                link(dve.tensor_reduce(c_b, Y, AX, ALU.max))
                link(dve.tensor_tensor(oh, Y, over_e(c_b, E2), ALU.is_equal))

            first_of(O1, L, c_a)
            link(dve.scalar_tensor_tensor(W.rearrange("p t e -> p (t e)"), O1.rearrange("p t e -> p (t e)"), -BIG,
                                          L.rearrange("p t e -> p (t e)"), ALU.mult, ALU.add))
            link(dve.tensor_reduce(c_c, W, AX, ALU.max))
            first_of(O2, W, c_c)
            dve.tensor_tensor(OS, O1, O2, ALU.add).then_inc(onehot_ready, 1)
            dve.wait_ge(lexp_done, 2)
            link(dve.tensor_reduce(c_d, X, AX, ALU.add))
            link(dve.reciprocal(c_d, c_d))
            link(dve.tensor_tensor(Y, X, O2, ALU.mult))
            link(dve.tensor_reduce(c_e, Y, AX, ALU.add))
            link(dve.tensor_tensor(c_e, c_e, c_d, ALU.mult))
            finished(dve, "cum1")
            finished(dve, "tot1")
            link(dve.memset(Z[:, 0, :], 0.0))
            before(Z, at("tot1").rearrange("p (t e) -> p t e", t=T), at("cum1").rearrange("p (t e) -> p t e", t=T), "1")
            for oh, prob in ((O1, c_d), (O2, c_e)):
                link(dve.tensor_tensor(Y, Z, oh, ALU.mult))
                link(dve.tensor_reduce(c_f, Y, AX, ALU.add))
                link(dve.tensor_scalar(c_f, c_f, float(CAP2), None, ALU.is_lt))
                link(dve.tensor_tensor(prob, prob, c_f, ALU.mult))
            link(dve.tensor_tensor(c_d, c_d, c_e, ALU.add))
            for f in range(2):
                for th in range(2):
                    emptied(dve, "F1", f, th)
                    g = xn[:, 2 * f + th, :]
                    link(dve.tensor_copy(slot[2][:, 0, 2 * f + th, :], g))
                    dve.tensor_tensor(slot[2][:, 1, 2 * f + th, :], g, f32(slot[2][:, 0, 2 * f + th, :]), ALU.subtract).then_inc(f_ready, 1)
            dve.wait_ge(rowb_in, 16)
            for t in range(T):
                link(dve.scalar_tensor_tensor(xres[:, t, :], rowb[:, :], c_d[:, t:t + 1], xres[:, t, :], ALU.mult, ALU.add))
            for t in range(T):
                finished(dve, "F2", t)
                dve.scalar_tensor_tensor(xres[:, t, :], at("F2", t), c_d[:, t:t + 1], xres[:, t, :], ALU.mult, ALU.add).then_inc(y_ready, 1)


SHAPES = [("x", (N, D), F32), ("src_scatter", (P, SCATTERS), I32), ("dst_scatter", (P, SCATTERS), I32),
          ("dst_chunks", (P, SCATTERS), I32), ("edge_attr_64", (EDGES, EA), F32),
          ("L0_gnn_Wv", (D, D), F32), ("bq_col", (P, C), F32), ("bk_col", (P, C), F32), ("L0_gnn_bv", (D,), F32),
          ("L0_mix_w_qkv", (D, 3 * D), F32), ("L0_mix_w_out", (D, D), F32), ("L0_mix_b_out", (D,), F32),
          ("L0_ffn_switch_b", (EXPERTS,), F32), ("L0_ffn_expert_b", (EXPERTS, D), F32),
          ("L1_gnn_W1", (D + EA, HID), F32), ("L1_gnn_b1", (HID,), F32), ("L1_gnn_W2", (HID, D), F32),
          ("L1_gnn_b2", (D,), F32), ("L1_mix_movement_scale_param", (1,), F32), ("L1_mix_temperature", (1,), F32),
          ("ffn_b1_col", (P, FFN // P), F32), ("L1_ffn_b2", (D,), F32),
          ("consts", (P, K_COLS), F32), ("WqT", (D, D), F32), ("WkT", (D, D), F32), ("mWqT", (D, D), F32),
          ("swT", (D, EXPERTS), F32), ("ewT", (EXPERTS, D, D), F32), ("qkvT", (D, 3 * D), F32), ("outT", (D, D), F32),
          ("rwT", (D, E2), F32), ("w1T", (D, FFN), F32), ("w2T", (FFN, D), F32),
          ("splat_par", (P, 2, PAIRS), F32), ("splat_ctr", (P, 2, PAIRS, SPLATS), F32)]


def kernel(**inputs):
    import concourse.bacc as bacc
    from concourse.bass_utils import run_bass_kernel_spmd

    given = {k: np.asarray(v) for k, v in inputs.items()}

    def turn(name):
        return np.swapaxes(given[name], -1, -2)

    laid = dict(given)
    laid["consts"] = const_table()
    laid["WqT"] = turn("L0_gnn_Wq")
    laid["WkT"] = turn("L0_gnn_Wk")
    laid["mWqT"] = given["L0_mix_w_qkv"][:, 0:D].T
    for name, col in (("L0_gnn_bq", "bq_col"), ("L0_gnn_bk", "bk_col"), ("L1_ffn_b1", "ffn_b1_col")):
        laid[col] = given[name].reshape(-1, P).T
    laid["swT"] = turn("L0_ffn_switch_w")
    laid["ewT"] = turn("L0_ffn_expert_w")
    laid["qkvT"] = turn("L1_mix_qkv_w")
    laid["outT"] = turn("L1_mix_out_w")
    laid["rwT"] = turn("L1_ffn_router_w")
    laid["w1T"] = turn("L1_ffn_w1")
    laid["w2T"] = turn("L1_ffn_w2")
    batches = SCATTERS // BATCH
    order = [9 * q % batches + batches * b for q in range(batches) for b in range(BATCH)]
    for name in ("src", "dst"):
        laid[name + "_scatter"] = given[name].reshape(SCATTERS, P)[order].T
    laid["dst_chunks"] = given["dst"].reshape(NCH, P, EK).transpose(1, 0, 2).reshape(P, SCATTERS)
    par = np.zeros((2, 64, 2, PAIRS), np.float32)
    for v, name in enumerate(("L1_mix_log_scales", "L1_mix_log_amps")):
        by_pair = given[name].reshape(PAIRS, 2, SPLATS)
        for j in range(3):
            par[:, SPLATS * j:SPLATS * (j + 1), v, :] = by_pair.transpose(1, 2, 0)
    laid["splat_par"] = par.reshape(P, 2, PAIRS)
    laid["splat_ctr"] = np.stack([given[name].reshape(PAIRS, 2, SPLATS, HD).transpose(1, 3, 0, 2).reshape(P, PAIRS, SPLATS)
                                  for name in ("L1_mix_base_centers", "L1_mix_center_deltas")], axis=1)

    nc = bacc.Bacc("TRN2", target_bir_lowering=False, num_devices=1)
    arrays, aps = {}, {}
    for name, shape, dt in SHAPES:
        arrays["in_" + name] = np.ascontiguousarray(laid[name])
        aps[name] = nc.dram_tensor("in_" + name, shape, dt, kind="ExternalInput").ap()
    aps["out"] = nc.dram_tensor("out_x", (N, D), F32, kind="ExternalOutput").ap()
    build(nc, aps)
    result = run_bass_kernel_spmd(nc, [arrays], core_ids=[0])
    return result.results[0]["out_x"]
```

```python
from contextlib import ExitStack

import numpy as np

import concourse.bass as bass
from concourse import mybir

F32 = mybir.dt.float32
F32R = mybir.dt.float32r
I32 = mybir.dt.int32
BF16 = mybir.dt.bfloat16
U32 = mybir.dt.uint32
U16 = mybir.dt.uint16
ALU = mybir.AluOpType
ACT = mybir.ActivationFunctionType
AX = mybir.AxisListType.X

P = 128
N = 1024
D = 512
T = N // P
C = D // P
HALF = N // 2
TH = T // 2
EDGES = 33792
EK = 8
CHUNK = P * EK
NCH = EDGES // CHUNK
EA = 64
SCATTERS = EDGES // P
BATCH = 12
EXPERTS = 16
CAP = int(1.2 * N / EXPERTS)
SLOTS = EXPERTS * CAP
WRING = 6
E2 = 64
CAP2 = 512
HID = 1024
FFN = 256
HEADS = 8
PAIRS = HEADS // 2
HD = D // HEADS
SPLATS = 16
KROWS = 3 * SPLATS
MROWS = KROWS + 2
EPS = 1e-5
NEG = -1000000.0
BIG = 3.0e38
ATT_SCALE = float(1.0 / np.sqrt(np.float32(D)))
MIX_SCALE = 1.0 / float(np.sqrt(HD)) / N

K_ID, K_TRI, K_IOTA, K_ONE = 0, 128, 256, 384
K_TOK, K_REV16, K_REV64, K_LOQ, K_LOK, K_LO8, K_CUP, K_CDN, K_NHI = 512, 520, 536, 600, 601, 602, 610, 643, 676
K_COLS = 684


def const_table():
    t = np.zeros((P, K_COLS), np.float32)
    r = np.arange(P)
    t[:, K_ID:K_ID + P] = np.eye(P)
    t[:, K_TRI:K_TRI + P] = r[:, None] < r[None, :]
    t[:, K_IOTA:K_IOTA + P] = r[None, :]
    t[:, K_ONE:K_ONE + P] = 1.0
    t[:, K_TOK:K_TOK + T] = SLOTS + r[:, None] + P * np.arange(T)[None, :]
    t[:, K_REV16:K_REV16 + EXPERTS] = EXPERTS - np.arange(EXPERTS)[None, :]
    t[:, K_REV64:K_REV64 + E2] = E2 - np.arange(E2)[None, :]
    t[:, K_LOQ] = -((r % 64 // SPLATS) == 2).astype(np.float32)
    t[:, K_LOK] = -((r % 64 // SPLATS) == 1).astype(np.float32)
    t[:, K_LO8:K_LO8 + T] = P * np.arange(T)[None, :]
    t[:, K_NHI:K_NHI + T] = -(P * np.arange(T)[None, :] + P - 1)
    t[:, K_CUP:K_CUP + NCH] = 1 + np.arange(NCH)[None, :]
    t[:, K_CDN:K_CDN + NCH] = NCH - np.arange(NCH)[None, :]
    return t


def plan_jobs():
    jobs = []
    turn = [0]

    def add(*name, bank=None):
        if bank is None:
            bank = turn[0] % 8
            turn[0] += 1
        jobs.append((name, bank))

    for t in range(T):
        add("xT", 0, t, bank=t % 4)
    for m in range(C):
        add("G", m, bank=4 + m)
    add("span", bank=0)
    add("spanT", bank=1)
    for m in range(C):
        add("GK", m)
    add("VK")
    for m in range(C):
        add("M", m)
    for m in range(C):
        add("B", m)
    add("U")
    add("R")
    for m in range(C):
        add("A", m)
    for th in range(2):
        for c in range(C):
            add("Q", c, th)
    for n in range(T + 2):
        if n < T:
            add("seg", n)
        if n > 1:
            add("segT", n - 2)
    for it in range(T):
        for jh in range(2):
            add("S", it, jh)
    for t in range(T):
        add("V", t)
    for t in range(T):
        add("PT", t, 0, bank=2 * (t % 2))
        add("PT", t, 1, bank=2 * (t % 2) + 1)
        add("AV", t, bank=4 + t % 2)
    turn[0] = 0
    for th in range(2):
        for t in range(th * TH, (th + 1) * TH):
            add("xT", 1, t)
        add("lT", 0, th)
    add("rt0")
    add("cum0")
    add("tot0")
    for e in range(EXPERTS + 1):
        if e < EXPERTS:
            add("eT", e, bank=4 + e % 2)
        if e > 0:
            add("eY", e - 1, bank=6 + (e - 1) % 2)
    turn[0] = 0
    add("aggT", 0)
    add("aggT", 1)
    for t in range(TH):
        add("xT", 2, t)
    for hh in range(2):
        for th in range(2):
            for m in range(C):
                add("H", hh, th, m)
            if hh == 0 and th == 0:
                for t in range(TH, T):
                    add("xT", 2, t)
            for t in range(TH):
                add("HW", hh, th, t)
    add("csq")
    for side in "qk":
        for c in range(PAIRS):
            for th in range(2):
                add("p", side, c, th)
            for th in range(2):
                add("d2", side, c, th)
    for step in attention_steps():
        if step[0] in ("L", "mT", "oU", "oT"):
            add(*step, bank=6 if step[:2] == ("L", 1) else 0)
        elif step[0] == "V1":
            add(*step, bank=2 + step[1] % 4)
        elif step[0] == "E":
            add(*step, bank=2 + 2 * (step[2] % 2))
        elif step[0] == "O" and step[2] == T - 1:
            add("O", step[1], bank=6)
    turn[0] = 0
    for t in range(T):
        add("X3", t)
    for th in range(2):
        for t in range(th * TH, (th + 1) * TH):
            add("xT", 3, t)
        add("lT", 1, th)
    add("rt1")
    for f in range(2):
        for th in range(2):
            add("F1", f, th)
    add("cum1")
    add("tot1")
    for t in range(T):
        add("F2", t)
    return jobs


def attention_steps():
    steps = []
    for t in range(T):
        steps += [("L", 0, t), ("L", 1, t), ("V1", t)]
    steps.append(("mT", 0))
    ahead = 5
    steps += [("L", 2, i) for i in range(ahead)]
    later = [("L", h, it) for h in range(2, HEADS) for it in range(T)][ahead:]
    flat = [(h, jt) for h in range(HEADS) for jt in range(T)]
    for n, (h, jt) in enumerate(flat):
        steps.append(("E", h, jt))
        last = None
        if later and not (h >= 2 and n % (2 * T) == 6):
            last = later.pop(0)
            steps.append(last)
        if n > 0:
            steps.append(("O", *flat[n - 1]))
        if last and last[1] % 2 and last[2] == T - 1:
            steps.append(("mT", last[1] // 2))
        if h and jt == 2:
            steps.append(("oU", h - 1))
        if h >= 2 and n % (2 * T) == 5:
            steps.append(("oT", h // 2 - 1))
    steps += [("O", *flat[-1]), ("oU", HEADS - 1), ("oT", PAIRS - 1)]
    return steps


WEIGHTS = [("mWk", 1, None), ("mWv", 3, None), ("mWo", 1, ("GK", 3)), ("mWqT", 3, ("VK",)),
           ("WqT", 0, ("M", 3)), ("WkT", 2, ("B", 3)), ("Wv", 3, ("Q", 3, 1)),
           ("W1a", 0, ("AV", 7)), ("W2a", 1, ("AV", 7)), ("W1b", 0, ("H", 0, 1, 3)),
           ("W2b", 1, ("HW", 0, 1, 3)), ("Lq", 0, ("H", 1, 1, 3)), ("Lk", 1, ("HW", 1, 1, 3)),
           ("Lv", 0, ("p", "q", 3, 1)), ("Lo", 1, ("p", "k", 3, 1)), ("F", 0, ("V1", 7))]


ROW_LOADS = [(0, 2), (2, 8), (8, 16)]

GROUPS = [((0, 2), (2, 4), (4, 6), (6, 8)), ((0, 4), (4, 7), (7, 8)), ((0, 4), (4, 8)), ((0, 4), (4, 7), (7, 8))]


def build(nc, a):
    jobs = plan_jobs()
    index = {name: i for i, (name, _) in enumerate(jobs)}
    assert len(index) == len(jobs)
    bank_of = dict(jobs)
    turn_of, seen = {}, [0] * 8
    for name, b in jobs:
        turn_of[name] = seen[b]
        seen[b] += 1
    windex = {name: i for i, (name, _, _) in enumerate(WEIGHTS)}
    stage_of, place_of, loads = {}, {}, [0] * 4
    for name, _, _ in WEIGHTS:
        stage_of[name] = {"W1a": 2, "W2a": 3}.get(name, (loads[0] + loads[1]) % 2)
        place_of[name] = loads[stage_of[name]]
        loads[stage_of[name]] += 1
    last_staged = {name: max([i for i, (o, _, _) in enumerate(WEIGHTS[:windex[name]]) if stage_of[o] == stage_of[name]],
                             default=None) for name in windex}

    with ExitStack() as ctx:
        def sb(name, shape, dt=F32):
            return ctx.enter_context(nc.sbuf_tensor(name, shape, dt))

        def f32(ap):
            return ap[:].bitcast(F32)

        def sem(name):
            return ctx.enter_context(nc.semaphore(name))

        xn = sb("xn", [P, T, D])
        arena = sb("arena", [P, max(NCH * EK * EA, 4 * T * D + 6 * P)])
        wraw = sb("wraw", [P, 2, C * D])
        slot = [sb(f"slot{i}", [P, 2, C, D], F32R) for i in range(4)]
        xT = [sb(f"xT{i}", [P, 2, C, HALF], F32R) for i in range(2)]
        kst = sb("kst", [P, K_COLS])
        dstf = sb("dstf", [P, NCH, EK])
        key = sb("key", [P, SCATTERS], U32)
        rowa = sb("rowa", [P, D])
        rowb = sb("rowb", [P, D])
        agg = sb("agg", [P, T, EA])
        cols = sb("cols", [P, 176])
        keyring = sb("keyring", [P, 2, BATCH], U32)
        zero16 = sb("zero16", [P, 1], U16)
        spans = sb("spans", [P, 2, NCH])
        plan = sb("plan", [1, 2, T], I32)
        idx = sb("idx", [P, 2, T], U32)
        bank = ctx.enter_context(nc.psum_tensor("bank", [P, 8, 512], F32))

        iota = kst[:, K_IOTA:K_IOTA + P]
        ident = kst[:, K_ID:K_ID + P]
        tri = kst[:, K_TRI:K_TRI + P]
        ones = kst[:, K_ONE:K_ONE + P]
        zero_row = kst[0:1, K_TRI:K_TRI + 1].bitcast(BF16)[:, 0:1].to_broadcast([1, P])
        one_row = kst[0:1, K_ONE:K_ONE + 2 * P].bitcast(BF16)

        edges = arena[:, 0:NCH * EK * EA].rearrange("p (c k d) -> p c k d", k=EK, d=EA)
        AW = T * D
        xres = arena[:, 0:AW].rearrange("p (t d) -> p t d", t=T)
        scores = arena[:, AW:3 * AW].rearrange("p (t j) -> p t j", t=T)
        nadj = arena[:, 3 * AW:4 * AW].bitcast(U16).rearrange("p (t j) -> p t j", t=T)
        ering = arena[:, AW:AW + WRING * C * D].rearrange("p (w c d) -> p w c d", w=WRING, c=C)
        gath = arena[:, AW:2 * AW].rearrange("p (t d) -> p t d", t=T)
        aggT = arena[0:EA + 1, 2 * AW:2 * AW + N]
        w1e = arena[0:EA + 1, 2 * AW + N:2 * AW + 2 * N]
        vone = arena[:, AW:AW + T * HEADS * (HD + 1)].rearrange("p (t h m) -> p t h m", t=T, h=HEADS)
        otmp = arena[0:HD + 1, 3 * AW - 2 * N:3 * AW].rearrange("p (r i) -> p r i", r=2)
        pring = arena[:, 3 * AW:4 * AW].rearrange("p (r i) -> p r i", r=4)
        tail = arena[:, 4 * AW:4 * AW + 6 * P].rearrange("p (r t e) -> p r t e", r=6, t=T)
        big6 = arena[:, AW:AW + 8 * D].rearrange("p (r t e) -> p r t e", r=8, t=T)
        csquare = gath[:, 0, :]
        onehot = xn[:, 0:2, :].rearrange("p k (t n) -> p k t n", n=P)
        ecopy = xn[:, 2:4, :][:, :, 0:4 * (EA + 1)].rearrange("p k (t d) -> p k t d", t=4)
        seg = xn[0:EA + 1, 4, 0:3 * P].rearrange("p (r n) -> p r n", r=3)
        qsq = xn[:, :, :].rearrange("p (r v a) d -> p r v (a d)", r=2, v=2)
        staging = [wraw[:, 0, :], wraw[:, 1, :]] + [xn[:, TH * i:TH * (i + 1), :].rearrange("p t d -> p (t d)") for i in range(2)]
        xb = [f32(slot[2 + e // 8])[0:CAP, e % 8 // C, e % C, :] for e in range(EXPERTS)]
        eb = [wraw[0:CAP, r % 2, r // 2 * D:(r // 2 + 1) * D] for r in range(4)]
        ey = [wraw[0:CAP, r, 2 * D:3 * D] for r in range(2)]
        xbT = [wraw[:, r, 3 * D:3 * D + C * CAP].rearrange("p (c s) -> p c s", c=C) for r in range(2)]
        srci = wraw[:, 1, 0:SCATTERS].bitcast(I32)
        dsti = wraw[:, 1, SCATTERS:2 * SCATTERS].bitcast(I32)
        dstc = wraw[:, 1, 2 * SCATTERS:3 * SCATTERS].bitcast(I32)
        cblk = agg[:, :, :].rearrange("p (c a) e -> p c (a e)", c=PAIRS)
        onesblk = kst[:, K_IOTA:K_IOTA + P]
        mneg = [agg[0:2 * T, 2 * v:2 * v + 2, :].rearrange("p a e -> p (a e)").bitcast(F32R) for v in range(2)]
        wdump = agg[:, :, :].rearrange("p t e -> p (t e)")
        ctr = dstf[:, :, :].rearrange("p c k -> p (c k)")[:, 0:3 * PAIRS * SPLATS].rearrange(
            "p (v c s) -> p v c s", v=3, c=PAIRS)

        stat = cols[:, 0:48].rearrange("p (t s) -> p t s", t=T)
        mv = cols[:, 48:64].rearrange("p (t s) -> p t s", t=T)
        rstd = cols[:, 64:72]
        c_a, c_b, c_c, c_d, c_e, c_f, c_g, c_h = (cols[:, 72 + 8 * i:80 + 8 * i] for i in range(8))
        ucol = cols[:, 136:140]
        bbcol = cols[:, 140:141]
        bqc, bkc = cols[:, 144:148], cols[:, 148:152]
        rcol = cols[:, 152:160]
        f1c = cols[:, 168:170]
        tmpc = cols[:, 170:172]
        negc = cols[:, 173:174]
        sbrow = sb("sbrow", [P, EXPERTS])
        swT = sb("swT", [P, C, EXPERTS])
        swP = sb("swP", [P, 2, C, EXPERTS], F32R)
        b2_fr = [slot[1][0:1, v, 0, :] for v in range(2)]
        one_fr = slot[1][0:1, 0, 1, 0:P]
        rwP = slot[3][:, :, :, 0:E2]
        lT = [wraw[0:(EXPERTS, E2)[n], 1, 0:N] for n in range(2)]
        rwT = wraw[:, 0, 0:C * E2].rearrange("p (c e) -> p c e", c=C)
        par = dstf[:, :, :].rearrange("p c k -> p (c k)")[:, 192:192 + 10 * PAIRS].rearrange("p (r c) -> p r c", c=PAIRS)
        mx = key[:, 0:4 * T].bitcast(F32).rearrange("p (c b t) -> p c b t", c=2, b=2)

        def dram(name, shape, dt=F32):
            return nc.dram_tensor(name, shape, dt, kind="Internal").ap()

        adjd = dram("not_adjacent", (N * N, 1), U16)
        xbuf = dram("expert_rows", (SLOTS + N, D))
        ybuf = dram("expert_results", (SLOTS, D))
        mdram = dram("row_maxima", (PAIRS, 2, 2, N))

        mm_done = sem("mm_done")
        evicted = [sem(f"evicted{b}") for b in range(8)]
        hi_done = sem("hi_done")
        w_in = [sem(f"w_in{i}") for i in range(4)]
        w_hi = sem("w_hi")
        w_split = sem("w_split")
        x_in = [sem(f"x_in{i}") for i in range(4)]
        const_in = sem("const_in")
        ids_in = sem("ids_in")
        rows_in = sem("rows_in")
        small_in = sem("small_in")
        edges_in = [sem(f"edges_in{i}") for i in range(3)]
        fill_ready = sem("fill_ready")
        zero_ready = sem("zero_ready")
        ones_ready = sem("ones_ready")
        adj_cleared = sem("adj_cleared")
        buf_cleared = sem("buf_cleared")
        keys_ready = sem("keys_ready")
        dst_ready = sem("dst_ready")
        key_copied = sem("key_copied")
        batch_ready = sem("batch_ready")
        scattered = [sem(f"scattered{i}") for i in range(2)]
        adj_in = [sem(f"adj_in{t}") for t in range(T)]
        xres_in = sem("xres_in")
        span_done = sem("span_done")
        plan_ready = sem("plan_ready")
        onehots = sem("onehots")
        edges_copied = sem("edges_copied")
        halves = sem("half_chunks_summed")
        var_ready = sem("var_ready")
        std_ready = sem("std_ready")
        xn_ready = sem("xn_ready")
        masked = sem("masked")
        exp_done = sem("exp_done")
        p_ready = sem("p_ready")
        chain = sem("vector_chain")
        achain = sem("scalar_chain")
        logit_ready = sem("logit_ready")
        router_hi = sem("router_hi")
        router_split = sem("router_split")
        lexp_done = sem("lexp_done")
        onehot_ready = sem("onehot_ready")
        route_ready = sem("route_ready")
        rows_sent = sem("rows_sent")
        xb_in = [sem(f"xb_in{i}") for i in range(len(ROW_LOADS))]
        eb_in = [sem(f"eb_in{i}") for i in range(4)]
        ew_in = [sem(f"ew_in{i}") for i in range(WRING)]
        y_out = [sem(f"y_out{i}") for i in range(2)]
        gathered = [sem(f"gathered{i}") for i in range(T)]
        res_ready = sem("res_ready")
        w1e_in = sem("w1e_in")
        l1_in = sem("l1_in")
        rowa_in = sem("rowa_in")
        rowb_in = sem("rowb_in")
        bias_added = sem("bias_added")
        rows_added = sem("rows_added")
        par_exp = sem("par_exp")
        par_in = sem("par_in")
        blk_ready = sem("blk_ready")
        st_ready = sem("st_ready")
        p_used = sem("p_used")
        m_stored = sem("m_stored")
        m_in = sem("m_in")
        o_ready = sem("o_ready")
        f_hi = sem("f_hi")
        f_ready = sem("f_ready")
        b2_split = sem("b2_split")
        rw_in = sem("rw_in")
        y_ready = sem("y_ready")
        out_sent = sem("out_sent")

        def finished(eng, *name):
            eng.wait_ge(mm_done, index[name] + 1)

        def emptied(eng, *name):
            eng.wait_ge(evicted[bank_of[name]], turn_of[name] + 1)

        def group_number(layer, g):
            return sum(len(x) for x in GROUPS[:layer]) + g

        def at(*name):
            return bank[:, bank_of[name], :]

        def hl(buf, *where):
            return (buf[(slice(None), 0, *where)], buf[(slice(None), 1, *where)])


        hi_order = {}
        def hi_number(name):
            return hi_order[name]

        split_jobs = ([("xT", 0, t) for t in range(T)] + [("G", m) for m in range(C)] + [("GK", m) for m in range(C)]
                      + [("VK",)] + [("M", m) for m in range(C)] + [("B", m) for m in range(C)]
                      + [("A", m) for m in range(C)] + [("Q", c, th) for th in range(2) for c in range(C)]
                      + [("V", t) for t in range(T)]
                      + [("PT", t, g) for t in range(T) for g in range(2)]
                      + [("xT", 1, t) for t in range(T)] + [("xT", 2, t) for t in range(TH)]
                      + [("H", 0, 0, m) for m in range(C)] + [("xT", 2, t) for t in range(TH, T)]
                      + [("H", hh, th, m) for hh in range(2) for th in range(2) for m in range(C) if hh or th]
                      + [("oT", c) for c in range(PAIRS)] + [("xT", 3, t) for t in range(T)])
        for i, name in enumerate(split_jobs):
            hi_order[name] = i

        def turned(t):
            return hl(xT[t // TH], slice(None), slice(t % TH * P, t % TH * P + P))

        def bankcols(name, t=None):
            return at(*name).rearrange("p (c s) -> p c s", c=C)

        def target(name):
            k = name[0]
            if k == "xT":
                return turned(name[2]), bankcols(name)
            if k == "G":
                return hl(slot[0], name[1]), at(*name)
            if k == "GK":
                return hl(slot[2], name[1]), at(*name)
            if k == "M":
                return hl(slot[2], name[1]), at(*name)
            if k == "B":
                return hl(slot[1], name[1]), at(*name)
            if k == "A":
                return hl(slot[3], name[1]), at(*name)
            if k == "Q":
                return hl(slot[2 * name[2]], name[1]), at(*name)
            if k == "V":
                return hl(slot[2 * (name[1] // TH)], name[1] % TH), at(*name)
            if k == "PT":
                ring = 2 * (name[1] % 2) + name[2]
                return hl(slot[3], ring), at(*name)
            if k == "H":
                return hl(slot[2 + name[2]], name[3]), at(*name)
            raise KeyError(name)

        def chunk_bounds(eng, n):
            eng.wait_ge(plan_ready, 1)
            return (eng.value_load(plan[0:1, 0, n:n + 1], min_val=0, max_val=NCH - 1),
                    eng.value_load(plan[0:1, 1, n:n + 1], min_val=1, max_val=NCH))

        blk = ctx.enter_context(nc.Block())

        @blk.sync
        def _(sp):
            for ap, name in ((srci, "src_scatter"), (dsti, "dst_scatter"), (dstc, "dst_chunks")):
                sp.dma_start(ap, a[name]).then_inc(ids_in, 16)
            sp.wait_ge(fill_ready, 2)
            sp.dma_start(adjd.rearrange("(p a j) b -> p a (j b)", p=P, a=T),
                         agg[:, :, :].rearrange("p t e -> p (t e)").bitcast(U16).unsqueeze(1)
                         .to_broadcast([P, T, N])).then_inc(adj_cleared, 16)
            sp.dma_start(kst[:, :], a["consts"]).then_inc(const_in, 16)
            xv = a["x"].rearrange("(t p) d -> p t d", p=P)
            for i in range(4):
                sp.dma_start(xn[:, 2 * i:2 * i + 2, :], xv[:, 2 * i:2 * i + 2, :]).then_inc(x_in[i], 16)

            wsrc = {
                "mWk": a["L0_mix_w_qkv"].rearrange("(c p) n -> p c n", p=P)[:, :, D:2 * D],
                "mWv": a["L0_mix_w_qkv"].rearrange("(c p) n -> p c n", p=P)[:, :, 2 * D:3 * D],
                "mWo": a["L0_mix_w_out"].rearrange("(c p) n -> p c n", p=P),
                "mWqT": a["mWqT"].rearrange("(c p) n -> p c n", p=P),
                "WqT": a["WqT"].rearrange("(c p) n -> p c n", p=P),
                "WkT": a["WkT"].rearrange("(c p) n -> p c n", p=P),
                "Wv": a["L0_gnn_Wv"].rearrange("(c p) n -> p c n", p=P),
                "W1a": a["L1_gnn_W1"][0:D].rearrange("(c p) n -> p c n", p=P)[:, :, 0:D],
                "W1b": a["L1_gnn_W1"][0:D].rearrange("(c p) n -> p c n", p=P)[:, :, D:2 * D],
                "W2a": a["L1_gnn_W2"][0:D].rearrange("(c p) n -> p c n", p=P),
                "W2b": a["L1_gnn_W2"][D:2 * D].rearrange("(c p) n -> p c n", p=P),
                "Lq": a["qkvT"].rearrange("(c p) n -> p c n", p=P)[:, :, 0:D],
                "Lk": a["qkvT"].rearrange("(c p) n -> p c n", p=P)[:, :, D:2 * D],
                "Lv": a["qkvT"].rearrange("(c p) n -> p c n", p=P)[:, :, 2 * D:3 * D],
                "Lo": a["outT"].rearrange("(c p) n -> p c n", p=P),
            }

            def load_weight(name):
                raw, arrived = staging[stage_of[name]], w_in[stage_of[name]]
                dst = raw.rearrange("p (c n) -> p c n", c=C)
                if last_staged[name] is not None:
                    sp.wait_ge(w_split, last_staged[name] + 1)
                if name == "F":
                    sp.dma_start(raw[:, 0:C * FFN].rearrange("p (c n) -> p c n", c=C),
                                 a["w1T"].rearrange("(c p) n -> p c n", p=P)).then_inc(arrived, 16)
                    sp.dma_start(raw[:, C * FFN:2 * C * FFN].rearrange("p (c n) -> p c n", c=2),
                                 a["w2T"].rearrange("(c p) n -> p c n", p=P)).then_inc(arrived, 16)
                else:
                    sp.dma_start(dst, wsrc[name]).then_inc(arrived, 16)

            load_weight("mWk")
            sp.wait_ge(dst_ready, 1)
            sp.wait_ge(keys_ready, 1)
            load_weight("mWv")
            ev = a["edge_attr_64"].rearrange("(c p k) d -> p c (k d)", p=P, k=EK)
            third = NCH // 3

            def load_edges(i):
                w = slice(i * third, (i + 1) * third)
                sp.dma_start(edges[:, w].rearrange("p c k d -> p c (k d)"), ev[:, w]).then_inc(edges_in[i], 16)

            load_edges(0)
            load_edges(1)
            load_weight("mWo")
            for name, dst in (("bq_col", bqc), ("bk_col", bkc)):
                sp.dma_start(dst, a[name]).then_inc(small_in, 16)
            sp.dma_start(swT[:, :, :], a["swT"].rearrange("(c p) e -> p c e", p=P)).then_inc(small_in, 16)
            sp.dma_start(sbrow[:, :], a["L0_ffn_switch_b"].rearrange("(a e) -> a e", a=1)
                         .to_broadcast([P, EXPERTS])).then_inc(small_in, 16)
            sp.dma_start(f1c, a["ffn_b1_col"]).then_inc(small_in, 16)
            load_weight("mWqT")
            load_edges(2)
            load_weight("WqT")
            load_weight("WkT")
            sp.dma_start(rowa[:, :], a["L0_gnn_bv"].rearrange("(a d) -> a d", a=1).to_broadcast([P, D])).then_inc(rows_in, 16)
            sp.dma_start(xbuf[0:SLOTS].rearrange("(p e) d -> p e d", p=CAP),
                         rowb[0:CAP, :].unsqueeze(1).to_broadcast([CAP, EXPERTS, D])).then_inc(buf_cleared, 16)
            sp.wait_ge(buf_cleared, 16)
            sp.dma_start(rowb[:, :], a["L0_mix_b_out"].rearrange("(a d) -> a d", a=1).to_broadcast([P, D])).then_inc(rows_in, 16)
            load_weight("Wv")
            for n in range(T):
                emptied(sp, "seg", n)
            sp.dma_start(xres, a["x"].rearrange("(t p) d -> p t d", p=P)).then_inc(xres_in, 16)
            for i in range(2):
                sp.wait_ge(scattered[i], 16 * SCATTERS // 2)
            for t in range(T):
                sp.dma_start(nadj[:, t, :], adjd.rearrange("(t p j) b -> p t (j b)", p=P, t=T)[:, t, :]).then_inc(adj_in[t], 16)

            def load_expert(e):
                if e >= WRING:
                    finished(sp, "eY", e - WRING)
                sp.dma_start(ering[:, e % WRING], a["ewT"][e].rearrange("(c p) f -> p c f", p=P)).then_inc(ew_in[e % WRING], 16)

            def load_rows(group):
                lo, hi = ROW_LOADS[group]
                rows = f32(slot[2 + lo // 8])[0:CAP, :, :, :].rearrange("p v c d -> p (v c) d")[:, lo % 8:lo % 8 + hi - lo, :]
                sp.dma_start(rows, xbuf[lo * CAP:hi * CAP].rearrange("(e p) d -> p e d", p=CAP)).then_inc(xb_in[group], 16)

            def load_bias(e):
                if e >= 4:
                    emptied(sp, "eY", e - 4)
                sp.dma_start(eb[e % 4], a["L0_ffn_expert_b"][e:e + 1].to_broadcast([CAP, D])).then_inc(eb_in[e % 4], 16)

            sp.wait_ge(p_ready, T)
            for t in range(T):
                finished(sp, "PT", t, 1)
            for e in range(WRING):
                load_expert(e)
            sp.wait_ge(rows_sent, 16 * T)
            for group in range(len(ROW_LOADS)):
                load_rows(group)
                if group == 0:
                    for e in range(4):
                        load_bias(e)
            sp.wait_ge(res_ready, T)
            load_weight("W1a")
            load_weight("W2a")
            for e in range(WRING, EXPERTS):
                load_expert(e)
                load_bias(e - 2)
            for e in (EXPERTS - 2, EXPERTS - 1):
                load_bias(e)
            for e in (EXPERTS - 2, EXPERTS - 1):
                finished(sp, "eY", e)
                emptied(sp, "eY", e)
            sp.wait_ge(y_out[0], 16 * EXPERTS // 2)
            sp.wait_ge(y_out[1], 16 * EXPERTS // 2)
            sp.dma_start(par[:, 0:2, :], a["splat_par"]).then_inc(par_in, 16)
            sp.dma_start(ctr[:, 0:2, :, :], a["splat_ctr"]).then_inc(par_in, 16)
            sp.dma_start(par[:, 8, 0:1], a["L1_mix_movement_scale_param"].rearrange("(a b) -> a b", a=1).to_broadcast([P, 1])).then_inc(par_in, 16)
            sp.dma_start(par[:, 8, 1:2], a["L1_mix_temperature"].rearrange("(a b) -> a b", a=1).to_broadcast([P, 1])).then_inc(par_in, 16)
            sp.wait_ge(bias_added, 1)
            sp.dma_start(rowa[:, :], a["L1_gnn_b2"].rearrange("(a d) -> a d", a=1).to_broadcast([P, D])).then_inc(rowa_in, 16)
            sp.dma_start(rowb[:, :], a["L1_ffn_b2"].rearrange("(a d) -> a d", a=1).to_broadcast([P, D])).then_inc(rowb_in, 16)
            sp.dma_start(w1e[0:EA], a["L1_gnn_W1"][D:D + EA]).then_inc(w1e_in, 16)
            sp.dma_start(w1e[EA:EA + 1], a["L1_gnn_b1"].rearrange("(a n) -> a n", a=1)).then_inc(w1e_in, 16)
            sp.wait_ge(res_ready, 2 * T)
            for name in ("W1b", "W2b", "Lq", "Lk", "Lv", "Lo"):
                load_weight(name)
            for c in range(PAIRS):
                emptied(sp, "mT", c)
                if c:
                    sp.wait_ge(m_in, 64 * c)
                for v in range(2):
                    sp.dma_start(mdram[c, v].rearrange("b (t i) -> (b t) i", t=T), f32(mneg[v])).then_inc(m_stored, 16)
                sp.wait_ge(m_stored, 32 * (c + 1))
                for b in range(2):
                    for v in range(2):
                        row = 64 * b + KROWS + v
                        sp.dma_start(f32(slot[2][row:row + 1, c // 2, 2 * (c % 2):2 * (c % 2) + 2, :]),
                                     mdram[c, v, b:b + 1].rearrange("b (a i) -> b a i", a=2)).then_inc(m_in, 16)
                if c == 0:
                    load_weight("F")
            sp.wait_ge(w_split, len(WEIGHTS))
            sp.dma_start(rwT, a["rwT"].rearrange("(c p) e -> p c e", p=P)).then_inc(rw_in, 16)
            ov = a["out"].rearrange("(t p) d -> t p d", p=P)
            for t in range(T):
                sp.wait_ge(y_ready, t + 1)
                sp.dma_start(ov[t], xres[:, t, :]).then_inc(out_sent, 16)
            sp.wait_ge(out_sent, 16 * T)

        @blk.gpsimd
        def _(pool):
            pool.memset(zero16[:, :], 0).then_inc(zero_ready, 1)
            pool.wait_ge(zero_ready, 1)
            pool.wait_ge(adj_cleared, 16)
            pool.wait_ge(keys_ready, 1)
            def scatter_half(i, h):
                pool.tensor_copy(keyring[:, h, :], key[:, bass.ds(i * (2 * BATCH) + h * BATCH, BATCH)]).then_inc(key_copied, 1)
                pool.wait_ge(key_copied, i * 2 + (h + 1))
                pool.sem_inc(batch_ready, 1)
                for b in range(BATCH):
                    pool.indirect_dma_start(adjd, bass.IndirectOffsetOnAxis(ap=keyring[:, h, b:b + 1], axis=0),
                                            zero16[:, :], None).then_inc(scattered[h], 16)

            for h in range(2):
                scatter_half(0, h)
            with pool.Fori(1, SCATTERS // (2 * BATCH)) as i:
                for h in range(2):
                    pool.wait_ge(scattered[h], i * (16 * BATCH))
                    scatter_half(i, h)
            pool.wait_ge(buf_cleared, 16)
            pool.wait_ge(route_ready, 1)
            for t in range(T):
                pool.wait_ge(xn_ready, T + t + 1)
                pool.indirect_dma_start(xbuf, bass.IndirectOffsetOnAxis(ap=idx[:, 0, t:t + 1], axis=0),
                                        xn[:, t, :], None).then_inc(rows_sent, 16)
            pool.wait_ge(route_ready, 2)
            pool.wait_ge(y_out[0], 16 * EXPERTS // 2)
            pool.wait_ge(y_out[1], 16 * EXPERTS // 2)
            finished(pool, "eY", EXPERTS - 1)
            for t in range(T):
                pool.indirect_dma_start(gath[:, t, :], None, ybuf,
                                        bass.IndirectOffsetOnAxis(ap=idx[:, 1, t:t + 1], axis=0)).then_inc(gathered[t], 16)

            pool.wait_ge(rowa_in, 16)
            for t in range(T):
                pool.wait_ge(xn_ready, 2 * T + t + 1)
                pool.tensor_tensor(xres[:, t, :], xres[:, t, :], xn[:, t, :], ALU.add).then_inc(rows_added, 1)
            for t in range(T):
                pool.wait_ge(rows_added, t + 1)
                pool.tensor_tensor(xres[:, t, :], xres[:, t, :], rowa[:, :], ALU.add).then_inc(rows_added, 1)
            for i in range(4):
                pool.wait_ge(f_hi, i + 1)
                pool.tensor_tensor(slot[2][:, 1, i, :], xn[:, i, :], f32(slot[2][:, 0, i, :]), ALU.subtract).then_inc(f_ready, 1)

        @blk.tensor
        def _(pe):
            def open_bank(*name):
                if turn_of[name]:
                    pe.wait_ge(evicted[bank_of[name]], turn_of[name])
                return at(*name)

            def close(ins):
                ins.then_inc(mm_done, 1)

            def mm3(out, L, R, start, stop, **kw):
                pe.matmul(out, L[1], R[0], start=start, stop=False, **kw)
                pe.matmul(out, L[0], R[0], start=False, stop=False, **kw)
                return pe.matmul(out, L[0], R[1], start=False, stop=stop, **kw)

            def turn_rows(layer, t):
                pe.wait_ge(xn_ready, layer * T + t + 1)
                o = open_bank("xT", layer, t)
                for c in range(C):
                    ins = pe.transpose(o[:, c * P:(c + 1) * P], xn[:, t, c * P:(c + 1) * P], ident)
                close(ins)

            def xt(t, c):
                return hl(xT[t // TH], c, slice(t % TH * P, t % TH * P + P))

            def sl(s, c, lo=0, hi=D):
                return hl(slot[s], c, slice(lo, hi))

            def product(name, L, R, ks=C, waits=None):
                o = open_bank(*name)
                for k in range(ks):
                    if waits:
                        waits(k)
                    ins = mm3(o, L(k), R(k), k == 0, k == ks - 1)
                close(ins)

            def chunk(c):
                return slice(c * P, (c + 1) * P)

            def router_logits(n, w):
                e = (EXPERTS, E2)[n]
                for th in range(2):
                    for t in range(th * TH, (th + 1) * TH):
                        turn_rows(2 * n + 1, t)
                    pe.wait_ge(router_split, n + 1)
                    for t in range(th * TH, (th + 1) * TH):
                        emptied(pe, "xT", 2 * n + 1, t)
                    o = open_bank("lT", n, th)
                    for k in range(C):
                        ins = mm3(o[0:e, :], hl(w, k), hl(xT[th], k), k == 0, k == C - 1)
                    close(ins)
                name = "rt%d" % n
                o = open_bank(name)
                for t in range(T):
                    if t % TH == 0:
                        emptied(pe, "lT", n, t // TH)
                    ins = pe.transpose(o[:, t * e:(t + 1) * e], lT[n][:, chunk(t)], ident[0:e, 0:e])
                close(ins)

            pe.wait_ge(const_in, 16)
            for t in range(T):
                turn_rows(0, t)
                for m in range(C):
                    if t == 0:
                        open_bank("G", m)
                    ins = pe.matmul(at("G", m), xn[:, t, chunk(m)], xn[:, t, :], start=t == 0, stop=t == T - 1)
                    if t == T - 1:
                        close(ins)
            pe.wait_ge(span_done, 1)
            o = open_bank("span")
            close(pe.transpose(o[0:2 * NCH, 0:P], spans[:, :, :].rearrange("p a c -> p (a c)"), ident))
            emptied(pe, "span")
            o = open_bank("spanT")
            close(pe.transpose(o[0:1, 0:2 * NCH], cols[0:2 * NCH, 172:173], ident[0:2 * NCH, 0:2 * NCH]))

            for m in range(C):
                if m == 0:
                    pe.wait_ge(w_split, windex["mWk"] + 1)
                    for k in range(C):
                        emptied(pe, "G", k)
                product(("GK", m), lambda k: sl(0, k, m * P, m * P + P), lambda k: sl(1, k))
            bounds = [chunk_bounds(pe, 0)]
            pe.wait_ge(w_split, windex["mWv"] + 1)
            o = open_bank("VK")
            for p in range(C):
                for k in range(C):
                    if p == 0:
                        emptied(pe, "GK", k)
                    ins = mm3(o[:, chunk(p)], sl(3, k, p * P, p * P + P), sl(2, k, p * P, p * P + P), k == 0, k == C - 1)
            close(ins)
            bounds.append(chunk_bounds(pe, 1))
            pe.wait_ge(w_split, windex["mWo"] + 1)
            emptied(pe, "VK")
            for p in range(C):
                product(("M", p), lambda k: sl(0, 0, p * P, p * P + P), lambda k: sl(1, p), ks=1)
            bounds.append(chunk_bounds(pe, 2))
            pe.wait_ge(w_split, windex["mWqT"] + 1)
            for p in range(C):
                emptied(pe, "M", p)
            for m in range(C):
                product(("B", m), lambda k: sl(3, k, m * P, m * P + P), lambda k: sl(2, k))
            bounds += [chunk_bounds(pe, n) for n in (3, 4, 5)]
            pe.wait_ge(w_split, windex["WkT"] + 1)
            pe.wait_ge(small_in, 80)
            o = open_bank("U")
            for m in range(C):
                for k in range(C):
                    for v in range(2):
                        pe.matmul(o[:, m:m + 1], f32(slot[2][:, v, k, chunk(m)]), bqc[:, k:k + 1],
                                  start=k == 0 and v == 0, stop=k == C - 1 and v == 1)
            for k in range(C):
                ins = pe.matmul(o[:, C:C + 1], bkc[:, k:k + 1].to_broadcast([P, P]), bqc[:, k:k + 1],
                                start=k == 0, stop=k == C - 1)
            close(ins)
            o = open_bank("R")
            for k in range(C):
                for v in range(2):
                    ins = pe.matmul(o, bkc[:, k:k + 1].to_broadcast([P, P]), f32(slot[0][:, v, k, :]),
                                    start=k == 0 and v == 0, stop=k == C - 1 and v == 1)
            close(ins)
            for m in range(C):
                product(("A", m), lambda k: sl(0, k, m * P, m * P + P), lambda k: sl(2, k))
            bounds.append(chunk_bounds(pe, 6))
            for m in range(C):
                emptied(pe, "A", m)
            for t in range(T):
                emptied(pe, "xT", 0, t)
            for th in range(2):
                for c in range(C):
                    product(("Q", c, th), lambda k: sl(3, k, c * P, c * P + P), lambda k: hl(xT[th], k))

            bounds.append(chunk_bounds(pe, 7))
            for i in range(3):
                pe.wait_ge(edges_in[i], 16)
            pe.wait_ge(plan_ready, 1)
            pe.wait_ge(ones_ready, 1)
            for k in range(2):
                pe.nop().then_inc(halves, 1)
            count = pe.alloc_register("pe_half_chunks")
            pe.reg_mov(count, 0)
            for n in range(T + 2):
                if n < T:
                    o = open_bank("seg", n)[0:EA + 1, 0:P]
                    pe.matmul(o, zero_row[:, 0:EA + 1], one_row[:, 0:P], start=True, stop=False)
                    with pe.Fori(*bounds[n]) as c:
                        done = pe.snap(count, min_val=0, max_val=2 * T * NCH)
                        for k in range(2):
                            pe.wait_ge(onehots, done + (k + 1))
                            pe.wait_ge(edges_copied, done + (k + 1))
                            for j in range(4):
                                ins = pe.matmul(o, ecopy[:, k, j, :], onehot[:, k, j, :], start=False, stop=False)
                            ins.then_inc(halves, 1)
                        pe.reg_add(count, count, 2)
                    close(pe.matmul(o, zero_row[:, 0:EA + 1], one_row[:, 0:P], start=False, stop=True))
                if n > 1:
                    emptied(pe, "seg", n - 2)
                    o = open_bank("segT", n - 2)
                    close(pe.transpose(o[:, 0:EA + 1], seg[:, (n - 2) % 3, :], ident[0:EA + 1, 0:EA + 1]))

            for th in range(2):
                for c in range(C):
                    emptied(pe, "Q", c, th)
            for it in range(T):
                for jh in range(2):
                    product(("S", it, jh), lambda k: hl(slot[2 * (it // TH)], k, slice(it % TH * P, it % TH * P + P)),
                            lambda k: hl(xT[jh], k))
            pe.wait_ge(w_split, windex["Wv"] + 1)
            for t in range(T):
                product(("V", t), lambda k: xt(t, k), lambda k: sl(3, k))
            for t in range(T):
                emptied(pe, "V", t)
            for m in range(C):
                emptied(pe, "B", m)
            for t in range(T):
                pe.wait_ge(p_ready, t + 1)
                for g in range(2):
                    o = open_bank("PT", t, g)
                    for j in range(4):
                        jt = 4 * g + j
                        ins = pe.transpose(o[:, chunk(j)], scores[:, t, jt * P:(jt + 1) * P], ident)
                    close(ins)
                o = open_bank("AV", t)
                for k in range(C):
                    mm3(o, xt(t, k), sl(1, k), k == 0, False)
                for g in range(2):
                    emptied(pe, "PT", t, g)
                    for j in range(4):
                        jt = 4 * g + j
                        ins = mm3(o, hl(slot[3], 2 * (t % 2) + g, chunk(j)), sl(2 * (jt // TH), jt % TH),
                                  False, jt == T - 1)
                close(ins)

            router_logits(0, swP)
            pe.wait_ge(onehot_ready, 1)
            oh0 = tail[:, 2, :, :].rearrange("p t e -> p (t e)")
            o = open_bank("cum0")
            close(pe.matmul(o[:, 0:P], tri, oh0, start=True, stop=True))
            o = open_bank("tot0")
            close(pe.matmul(o[:, 0:P], ones, oh0, start=True, stop=True))
            for e in range(EXPERTS + 1):
                if e < EXPERTS:
                    for group, (lo, _) in enumerate(ROW_LOADS):
                        if e == lo:
                            pe.wait_ge(xb_in[group], 16)
                    o = open_bank("eT", e)
                    for k in range(C):
                        ins = pe.transpose(o[:, k * CAP:(k + 1) * CAP], xb[e][:, chunk(k)], ident[0:CAP, 0:CAP])
                    close(ins)
                if e > 0:
                    m = e - 1
                    pe.wait_ge(ew_in[m % WRING], 16 * (m // WRING + 1))
                    emptied(pe, "eT", m)
                    o = open_bank("eY", m)
                    for k in range(C):
                        ins = pe.matmul(o[0:CAP, :], xbT[m % 2][:, k, :], ering[:, m % WRING, k, :], start=k == 0, stop=k == C - 1)
                    close(ins)

            for g in range(2):
                o = open_bank("aggT", g)
                for j in range(4):
                    ins = pe.transpose(o[0:EA, chunk(j)], agg[:, 4 * g + j, :], ident)
                close(ins)
            for t in range(TH):
                turn_rows(2, t)
            pe.wait_ge(w1e_in, 32)
            pe.wait_ge(blk_ready, 1)
            for g in range(2):
                emptied(pe, "aggT", g)
            for hh in range(2):
                for th in range(2):
                    pe.wait_ge(w_split, windex[("W1a", "W1b")[hh]] + 1)
                    for t in range(th * TH, (th + 1) * TH):
                        emptied(pe, "xT", 2, t)
                    for m in range(C):
                        o = open_bank("H", hh, th, m)
                        for k in range(C):
                            mm3(o, sl(0, k, m * P, m * P + P), hl(xT[th], k), k == 0, False)
                        ch = hh * C + m
                        close(pe.matmul(o, w1e[:, ch * P:(ch + 1) * P], aggT[:, th * HALF:(th + 1) * HALF], start=False, stop=True))
                    if hh == 0 and th == 0:
                        for t in range(TH, T):
                            turn_rows(2, t)
                    pe.wait_ge(w_split, windex[("W2a", "W2b")[hh]] + 1)
                    for t in range(TH):
                        product(("HW", hh, th, t), lambda k: hl(slot[2 + th], k, chunk(t)), lambda k: sl(1, k),
                                waits=lambda k: t == 0 and emptied(pe, "H", hh, th, k))

            pe.wait_ge(blk_ready, 2)
            o = open_bank("csq")
            for c in range(PAIRS):
                ins = pe.matmul(o[:, c:c + 1], csquare[:, chunk(c)], ones[:, 0:1], start=True, stop=True)
            close(ins)
            for n, side in enumerate("qk"):
                pe.wait_ge(w_split, windex[("Lq", "Lk")[n]] + 1)
                for c in range(PAIRS + 1):
                    if c < PAIRS:
                        for th in range(2):
                            product(("p", side, c, th), lambda k: sl(n, k, c * P, c * P + P), lambda k: hl(xT[th], k))
                    if c > 0:
                        g = n * PAIRS + c - 1
                        for th in range(2):
                            emptied(pe, "p", side, c - 1, th)
                        for th in range(2):
                            o = open_bank("d2", side, c - 1, th)
                            w = slice(th * HALF, (th + 1) * HALF)
                            pe.matmul(o, onesblk, qsq[:, g % 2, 1, w], start=True, stop=False)
                            close(pe.matmul(o, cblk[:, c - 1, :], qsq[:, g % 2, 0, w], start=False, stop=True))
            def stack(s, c, rows, lo, hi):
                v = slot[s][:, :, :, :].rearrange("p a (b x) d -> p (a b) (x d)", x=2)
                return v[rows, c, lo:hi]

            def krows(h, n):
                return slice(64 * (h % 2), 64 * (h % 2) + n)

            def two(o, lhsT, s, c, rows):
                for jh in range(2):
                    ins = pe.matmul(bank[:, o + jh, :], lhsT, stack(s, c, rows, jh * HALF, (jh + 1) * HALF), start=True, stop=True)
                return ins

            pe.wait_ge(st_ready, 4 * PAIRS)
            pe.wait_ge(w_split, windex["Lv"] + 1)
            for side in "qk":
                for c in range(PAIRS):
                    for th in range(2):
                        emptied(pe, "d2", side, c, th)
            for step in attention_steps():
                if step[0] in ("L", "E", "oU", "oT") or (step[0] == "O" and step[2] == 0):
                    name = step if step[0] != "O" else ("O", step[1])
                    open_bank(*name)
                if step == ("E", 0, 0):
                    for t in range(T):
                        emptied(pe, "V1", t)
                    emptied(pe, "L", 1, T - 1)
                if step[0] == "L":
                    _, h, it = step
                    r = krows(h, KROWS)
                    close(two(bank_of[step], stack(2, h // 2, r, it * P, (it + 1) * P), 3, h // 2, r))
                elif step[0] == "V1":
                    product(step, lambda k: xt(step[1], k), lambda k: sl(0, k))
                elif step[0] == "mT":
                    c = step[1]
                    emptied(pe, "L", 2 * c + 1, T - 1)
                    o = open_bank(*step)
                    close(pe.transpose(o[0:2 * T, 0:P], mx[:, c % 2].rearrange("p b t -> p (b t)"), ident))
                elif step[0] == "oU":
                    h = step[1]
                    emptied(pe, "O", h)
                    for it in range(T):
                        w = slice(it % TH * (HD + 1), (it % TH + 1) * (HD + 1))
                        ins = pe.transpose(bank[:, it // TH, w], otmp[:, h % 2, chunk(it)], ident[0:HD + 1, 0:HD + 1])
                    close(ins)
                elif step[0] == "oT":
                    c = step[1]
                    pe.wait_ge(o_ready, 2 * (c + 1))
                    for it in range(T):
                        ins = pe.transpose(bank[:, it // TH, chunk(it % TH)], xn[:, it, chunk(c)], ident)
                    close(ins)
                elif step[0] == "E":
                    _, h, jt = step
                    pe.wait_ge(m_in, 64 * (h // 2 + 1))
                    r = krows(h, MROWS)
                    close(two(bank_of[step], stack(3, h // 2, r, jt * P, (jt + 1) * P), 2, h // 2, r))
                else:
                    _, h, jt = step
                    n = h * T + jt
                    emptied(pe, "E", h, jt)
                    for ih in range(2):
                        ins = pe.matmul(bank[0:HD + 1, 6 + ih, :], vone[:, jt, h, :], pring[:, n % 4, ih * HALF:(ih + 1) * HALF],
                                        start=jt == 0, stop=jt == T - 1)
                    if jt == T - 1:
                        close(ins)
                    else:
                        ins.then_inc(p_used, 1)
            for step in (("E", HEADS - 1, T - 2), ("E", HEADS - 1, T - 1), ("oT", PAIRS - 1)):
                emptied(pe, *step)
            pe.wait_ge(w_split, windex["Lo"] + 1)
            for t in range(T):
                product(("X3", t), lambda k: xt(t, k), lambda k: sl(1, k))

            router_logits(1, rwP)
            fw = slot[0][:, :, :, :].rearrange("p v c d -> p v (c d)")
            for f in range(2):
                for th in range(2):
                    product(("F1", f, th), lambda k: hl(fw, slice(k * FFN + f * P, k * FFN + f * P + P)), lambda k: hl(xT[th], k))
            ohs = big6[:, 4].rearrange("p t e -> p (t e)")
            pe.wait_ge(onehot_ready, 2)
            close(pe.matmul(open_bank("cum1"), tri, ohs, start=True, stop=True))
            close(pe.matmul(open_bank("tot1"), ones, ohs, start=True, stop=True))
            pe.wait_ge(b2_split, 1)
            for t in range(T):
                o = open_bank("F2", t)
                for v in range(2):
                    pe.matmul(o, one_fr, b2_fr[v], start=v == 0, stop=False)
                for k in range(2):
                    if t % TH == 0:
                        pe.wait_ge(f_ready, 2 * k + t // TH + 1)
                    ins = mm3(o, hl(slot[2], 2 * k + t // TH, chunk(t % TH)), hl(fw, slice(C * FFN + k * D, C * FFN + (k + 1) * D)),
                              False, k == 1)
                close(ins)

        def send_y(act, e):
            emptied(act, "eY", e)
            act.dma_start(ybuf[e * CAP:(e + 1) * CAP], ey[e % 2]).then_inc(y_out[e % 2], 16)

        def vk_at(s, v, rows, cs):
            return s[rows, v, 0, :].rearrange("p (c e) -> p c e", c=C)[:, :, cs]

        @blk.scalar
        def _(act):
            steps = [0]

            def link(ins):
                steps[0] += 1
                ins.then_inc(achain, 1)
                act.wait_ge(achain, steps[0])

            def split_weight(name):
                i = windex[name]
                _, s, after = WEIGHTS[i]
                act.wait_ge(w_in[stage_of[name]], 16 * (place_of[name] + (2 if name == "F" else 1)))
                if after:
                    finished(act, *after)
                act.activation(slot[s][:, 0, :, :].rearrange("p c d -> p (c d)"), staging[stage_of[name]], ACT.Copy).then_inc(w_hi, 1)

            def hi(name, **kw):
                (h, _), src = target(name)
                finished(act, *name)
                act.activation(h, src, kw.pop("func", ACT.Copy), **kw).then_inc(hi_done, 1)

            def deviation(layer, g):
                w = slice(*GROUPS[layer][g])
                act.wait_ge(var_ready, group_number(layer, g) + 1)
                act.activation(rstd[:, w], rstd[:, w], ACT.Sqrt).then_inc(std_ready, 1)

            for g in range(len(GROUPS[0])):
                deviation(0, g)
            for t in range(T):
                hi(("xT", 0, t))
                if t in (1, 3):
                    split_weight(("mWk", "mWv")[t // 2])
            for m in range(C):
                hi(("G", m))
            act.wait_ge(plan_ready, 1)
            for m in range(C):
                hi(("GK", m))
            split_weight("mWo")
            finished(act, "VK")
            vkb = bankcols(("VK",))
            for b in range(2):
                r = slice(64 * b, 64 * b + 64)
                ins = act.activation(vk_at(slot[0], 0, r, r), vkb[r, :, r], ACT.Copy, scale=MIX_SCALE)
            ins.then_inc(hi_done, 1)
            split_weight("mWqT")
            for m in range(C):
                hi(("M", m))
            split_weight("WqT")
            for m in range(C):
                hi(("B", m))
            split_weight("WkT")
            for m in range(C):
                hi(("A", m))
            emptied(act, "U")
            bounds = []
            for th in range(2):
                for c in range(C):
                    hi(("Q", c, th), func=ACT.Identity, bias=ucol[:, c:c + 1])
                    bounds.append(chunk_bounds(act, th * C + c))
            split_weight("Wv")
            act.wait_ge(small_in, 80)
            act.activation(swP[:, 0], swT[:, :, :], ACT.Copy).then_inc(router_hi, 1)
            emptied(act, "R")
            for i in range(3):
                act.wait_ge(edges_in[i], 16)
            act.wait_ge(plan_ready, 1)
            count = act.alloc_register("act_half_chunks")
            act.reg_mov(count, 0)
            for n in range(T):
                with act.Fori(*bounds[n]) as c:
                    done = act.snap(count, min_val=0, max_val=2 * T * NCH)
                    for k in range(2):
                        act.wait_ge(halves, done + (k + 1))
                        part = edges[:, bass.ds(c, 1), 4 * k:4 * k + 4, :].rearrange("p c k d -> p (c k) d")
                        act.activation(ecopy[:, k, :, 0:EA], part, ACT.Copy).then_inc(edges_copied, 1)
                    act.reg_add(count, count, 2)
            for n in range(T):
                emptied(act, "seg", n)
            for it in range(T):
                for jh in range(2):
                    finished(act, "S", it, jh)
                    act.activation(scores[:, it, jh * HALF:(jh + 1) * HALF], at("S", it, jh), ACT.Identity,
                                   bias=rcol[:, it:it + 1], scale=ATT_SCALE).then_inc(evicted[bank_of[("S", it, jh)]], 1)
            def exponentials(t):
                act.wait_ge(masked, t + 1)
                act.activation(scores[:, t, :], scores[:, t, :], ACT.Exp, bias=c_a[:, t:t + 1],
                               accum_out=c_b[:, t:t + 1]).then_inc(exp_done, 1)

            for t in range(T):
                hi(("V", t))
                if t == 5:
                    exponentials(0)
            for t in range(T):
                for g in range(2):
                    if t >= 2:
                        finished(act, "AV", t - 2)
                    hi(("PT", t, g))
                if t + 1 < T:
                    exponentials(t + 1)
                if t == T - 2:
                    deviation(1, 0)
            deviation(1, 1)
            for th in range(2):
                for t in range(th * TH, (th + 1) * TH):
                    hi(("xT", 1, t))
                if th == 0:
                    deviation(1, 2)
                finished(act, "lT", 0, th)
                act.activation(lT[0][:, th * HALF:(th + 1) * HALF], at("lT", 0, th)[0:EXPERTS, :], ACT.Copy).then_inc(evicted[bank_of[("lT", 0, th)]], 1)
            act.wait_ge(logit_ready, 1)
            act.activation(tail[:, 1], tail[:, 1], ACT.Exp).then_inc(lexp_done, 1)
            for e in range(EXPERTS):
                finished(act, "eT", e)
                if e >= 2:
                    finished(act, "eY", e - 2)
                act.activation(xbT[e % 2], at("eT", e)[:, 0:C * CAP].rearrange("p (c s) -> p c s", c=C), ACT.Copy).then_inc(evicted[bank_of[("eT", e)]], 1)
                if e >= 1:
                    send_y(act, e - 1)
                if e in (6, 8):
                    split_weight("W1a" if e == 6 else "W2a")
            send_y(act, EXPERTS - 1)
            deviation(2, 0)
            for t in range(TH):
                hi(("xT", 2, t))
            deviation(2, 1)
            act.wait_ge(par_in, 64)
            act.activation(par[:, 2:4, :], par[:, 0:2, :], ACT.Exp).then_inc(par_exp, 1)
            act.activation(par[:, 9, 0:1], par[:, 8, 0:1], ACT.Exp, scale=-1.0).then_inc(par_exp, 1)
            for hh in range(2):
                for th in range(2):
                    for m in range(C):
                        name = ("H", hh, th, m)
                        if hh:
                            finished(act, "HW", 0, th, TH - 1)
                        hi(name, func=ACT.Relu)
                    if hh == 0 and th == 0:
                        for t in range(TH, T):
                            hi(("xT", 2, t))
                if hh == 0:
                    split_weight("W1b")
                    split_weight("W2b")
            split_weight("Lq")
            split_weight("Lk")
            for n, side in enumerate("qk"):
                for c in range(PAIRS + 1):
                    if c < PAIRS:
                        g = n * PAIRS + c
                        for th in range(2):
                            name = ("p", side, c, th)
                            finished(act, *name)
                            if g >= 2:
                                finished(act, "d2", "qk"[(g - 2) // PAIRS], (g - 2) % PAIRS, th)
                            if g == 0:
                                act.wait_ge(rows_added, 2 * T)
                            w = slice(th * HALF, (th + 1) * HALF)
                            act.activation(qsq[:, g % 2, 0, w], at(*name), ACT.Copy)
                            act.activation(qsq[:, g % 2, 1, w], at(*name), ACT.Square).then_inc(evicted[bank_of[name]], 1)
                    if c > 0:
                        g = n * PAIRS + c - 1
                        emptied(act, "csq")
                        for th in range(2):
                            name = ("d2", side, c - 1, th)
                            finished(act, *name)
                            if 2 * g + th >= 4:
                                act.wait_ge(st_ready, 2 * g + th - 3)
                            act.activation(pring[:, (2 * g + th) % 4, 0:HALF], at(*name), ACT.Exp,
                                           bias=par[:, 5, c - 1:c], scale=par[:, 4, c - 1:c]).then_inc(evicted[bank_of[name]], 1)
                if side == "q":
                    split_weight("Lv")
            act.wait_ge(st_ready, 4 * PAIRS)
            for step in attention_steps():
                if step[0] == "V1":
                    finished(act, *step)
                    act.activation(vone[:, step[1], :, 0:HD], at(*step).rearrange("p (h e) -> p h e", e=HD),
                                   ACT.Copy).then_inc(evicted[bank_of[step]], 1)
                if step[0] == "E":
                    _, h, jt = step
                    n = h * T + jt
                    finished(act, *step)
                    if n >= 4:
                        if (n - 4) % T == T - 1:
                            finished(act, "O", (n - 4) // T)
                        else:
                            act.wait_ge(p_used, (n - 4) // T * (T - 1) + (n - 4) % T + 1)
                    b = bank_of[step]
                    act.activation(pring[:, n % 4, :], bank[:, b:b + 2, :].rearrange("p a i -> p (a i)"),
                                   ACT.Exp).then_inc(evicted[b], 1)
                if step[0] == "O" and step[2] == T - 1:
                    h = step[1]
                    finished(act, "O", h)
                    if h >= 2:
                        finished(act, "oU", h - 2)
                    act.activation(otmp[:, h % 2, :], bank[0:HD + 1, 6:8, :].rearrange("p a i -> p (a i)"), ACT.Copy).then_inc(evicted[6], 1)
                if step[0] == "oT":
                    finished(act, *step)
                    for g in range(2):
                        ins = act.activation(xT[g][:, 0, step[1], :], bank[:, g, :], ACT.Copy)
                    ins.then_inc(hi_done, 1)
                if step in (("E", 6, 1), ("E", 6, 5)):
                    split_weight("Lo" if step[2] == 1 else "F")
            act.wait_ge(rw_in, 16)
            act.activation(rwP[:, 0], rwT, ACT.Copy).then_inc(router_hi, 1)
            for g in range(2):
                deviation(3, g)
            for th in range(2):
                for t in range(th * TH, (th + 1) * TH):
                    hi(("xT", 3, t))
                if th == 0:
                    deviation(3, 2)
                finished(act, "lT", 1, th)
                act.activation(lT[1][:, th * HALF:(th + 1) * HALF], at("lT", 1, th)[0:E2, :], ACT.Copy).then_inc(evicted[bank_of[("lT", 1, th)]], 1)
            act.wait_ge(logit_ready, 2)
            act.activation(big6[:, 1], big6[:, 1], ACT.Exp).then_inc(lexp_done, 1)
            for f in range(2):
                for th in range(2):
                    name = ("F1", f, th)
                    finished(act, *name)
                    act.activation(xn[:, 2 * f + th, :], at(*name), ACT.Gelu, bias=f1c[:, f:f + 1]).then_inc(evicted[bank_of[name]], 1)
                    emptied(act, *name)
                    act.activation(slot[2][:, 0, 2 * f + th, :], xn[:, 2 * f + th, :], ACT.Copy).then_inc(f_hi, 1)

        @blk.vector
        def _(dve):
            steps = [0]

            def link(ins):
                steps[0] += 1
                ins.then_inc(chain, 1)
                dve.wait_ge(chain, steps[0])

            def split_weight(name):
                i = windex[name]
                s = WEIGHTS[i][1]
                dve.wait_ge(w_hi, i + 1)
                flat = slot[s][:, :, :, :].rearrange("p v c d -> p v (c d)")
                dve.tensor_tensor(flat[:, 1], staging[stage_of[name]], f32(flat[:, 0]), ALU.subtract).then_inc(w_split, 1)

            def lo(name, bias=None, op=ALU.add):
                (h, l), src = target(name)
                dve.wait_ge(hi_done, hi_number(name) + 1)
                if bias is None:
                    ins = dve.tensor_tensor(l, src, f32(h), ALU.subtract)
                else:
                    ins = dve.scalar_tensor_tensor(l, src, bias, f32(h), op, ALU.subtract)
                ins.then_inc(evicted[bank_of[name]], 1)

            def moments(t, src):
                link(dve.bn_stats(stat[:, t, :], src))
                return dve.bn_aggr(mv[:, t, :], stat[:, t, :])

            def variance(layer, g):
                w = slice(*GROUPS[layer][g])
                dve.tensor_scalar(rstd[:, w], mv[:, w, 1], EPS, None, ALU.add).then_inc(var_ready, 1)

            def normalise(layer, g, src):
                w = slice(*GROUPS[layer][g])
                dve.wait_ge(std_ready, group_number(layer, g) + 1)
                link(dve.reciprocal(rstd[:, w], rstd[:, w]))
                for t in range(*GROUPS[layer][g]):
                    dve.tensor_scalar(xn[:, t, :], src(t), mv[:, t, 0:1], rstd[:, t:t + 1], ALU.subtract, ALU.mult).then_inc(xn_ready, 1)

            dve.memset(agg[:, :, :].rearrange("p t e -> p (t e)").bitcast(U16), 1).then_inc(fill_ready, 1)
            dve.memset(rowb[:, :], 0.0).then_inc(fill_ready, 1)
            dve.wait_ge(ids_in, 48)
            dve.scalar_tensor_tensor(key[:, :], srci, float(N), dsti, ALU.mult, ALU.add).then_inc(keys_ready, 1)
            dve.tensor_copy(dstf[:, :, :].rearrange("p c k -> p (c k)"), dstc).then_inc(dst_ready, 1)
            dve.wait_ge(dst_ready, 1)
            link(dve.tensor_reduce(spans[:, 0, :], dstf[:, :, :], AX, ALU.min))
            link(dve.tensor_reduce(spans[:, 1, :], dstf[:, :, :], AX, ALU.max))
            dve.tensor_scalar(spans[:, 0, :], spans[:, 0, :], -1.0, None, ALU.mult).then_inc(span_done, 1)
            for t in range(T):
                dve.wait_ge(x_in[t // 2], 16)
                link(moments(t, xn[:, t, :]))
                if t % 2:
                    variance(0, t // 2)
                    if t > 2:
                        normalise(0, t // 2 - 1, lambda t: xn[:, t, :])
            normalise(0, 3, lambda t: xn[:, t, :])
            for t in range(T):
                lo(("xT", 0, t))
                if t in (1, 3):
                    split_weight(("mWk", "mWv")[t // 2])
            finished(dve, "span")
            dve.tensor_reduce(cols[0:2 * NCH, 172:173], at("span")[0:2 * NCH, 0:P], AX, ALU.max).then_inc(evicted[bank_of[("span",)]], 1)
            finished(dve, "spanT")
            scratch = slot[2][0:1, :, :, :].rearrange("p v c d -> p (v c d)")
            span = scratch[:, 0:2 * NCH]
            dve.tensor_copy(span, at("spanT")[0:1, 0:2 * NCH]).then_inc(evicted[bank_of[("spanT",)]], 1)
            for m in range(C):
                lo(("G", m))
            emptied(dve, "spanT")
            near = [scratch[:, 128 + 512 * i:128 + 512 * i + T * NCH].rearrange("p (n c) -> p n c", c=NCH) for i in range(3)]
            got = [scratch[:, 2048 + 32 * i:2048 + 32 * i + T] for i in range(4)]

            def over_n(ap):
                return ap.unsqueeze(1).to_broadcast([1, T, NCH])

            def over_c(col):
                return kst[0:1, col:col + T].unsqueeze(2).to_broadcast([1, T, NCH])

            link(dve.tensor_tensor(near[0], over_n(f32(span[:, NCH:2 * NCH])), over_c(K_LO8), ALU.is_ge))
            link(dve.tensor_tensor(near[1], over_n(f32(span[:, 0:NCH])), over_c(K_NHI), ALU.is_ge))
            link(dve.tensor_tensor(near[2], f32(near[0]), f32(near[1]), ALU.mult))
            link(dve.tensor_tensor(near[0], f32(near[2]), over_n(kst[0:1, K_CUP:K_CUP + NCH]), ALU.mult))
            link(dve.tensor_tensor(near[1], f32(near[2]), over_n(kst[0:1, K_CDN:K_CDN + NCH]), ALU.mult))
            link(dve.tensor_reduce(got[0], f32(near[0]), AX, ALU.max))
            link(dve.tensor_reduce(got[1], f32(near[1]), AX, ALU.max))
            link(dve.tensor_scalar(got[2], f32(got[1]), -1.0, float(NCH), ALU.mult, ALU.add))
            link(dve.tensor_scalar(got[2], f32(got[2]), float(NCH - 1), None, ALU.min))
            link(dve.tensor_scalar(got[3], f32(got[2]), 1.0, None, ALU.add))
            link(dve.tensor_tensor(got[3], f32(got[3]), f32(got[0]), ALU.max))
            dve.tensor_copy(plan[:, 0, :], f32(got[2]))
            dve.tensor_copy(plan[:, 1, :], f32(got[3])).then_inc(plan_ready, 1)
            for m in range(C):
                lo(("GK", m))
            split_weight("mWo")
            finished(dve, "VK")
            link(dve.memset(f32(slot[0][0:64, :, 0, :].rearrange("p v (c e) -> p v c e", c=C)[:, :, :, 64:128]), 0.0))
            link(dve.memset(f32(slot[0][64:128, :, 0, :].rearrange("p v (c e) -> p v c e", c=C)[:, :, :, 0:64]), 0.0))
            dve.wait_ge(hi_done, hi_number(("VK",)) + 1)
            for b in range(2):
                r = slice(64 * b, 64 * b + 64)
                ins = dve.scalar_tensor_tensor(vk_at(slot[0], 1, r, r), bankcols(("VK",))[r, :, r], MIX_SCALE,
                                               f32(vk_at(slot[0], 0, r, r)), ALU.mult, ALU.subtract)
            ins.then_inc(evicted[bank_of[("VK",)]], 1)
            split_weight("mWqT")
            for m in range(C):
                lo(("M", m))
            split_weight("WqT")
            for m in range(C):
                lo(("B", m))
            split_weight("WkT")
            finished(dve, "U")
            dve.tensor_copy(cols[:, 136:141], at("U")[:, 0:C + 1]).then_inc(evicted[bank_of[("U",)]], 1)
            emptied(dve, "U")
            finished(dve, "R")
            dve.wait_ge(adj_cleared, 16)
            for t in range(T):
                ins = dve.tensor_tensor_reduce(wdump, xn[:, t, :], at("R"), 1.0, 0.0, ALU.mult, ALU.add, rcol[:, t:t + 1])
                link(ins)
            dve.tensor_scalar(rcol, rcol, bbcol, ATT_SCALE, ALU.add, ALU.mult).then_inc(evicted[bank_of[("R",)]], 1)
            for m in range(C):
                lo(("A", m))
            bounds = []
            for th in range(2):
                for c in range(C):
                    lo(("Q", c, th), bias=ucol[:, c:c + 1])
                    bounds.append(chunk_bounds(dve, th * C + c))

            split_weight("Wv")
            dve.wait_ge(router_hi, 1)
            dve.tensor_tensor(swP[:, 1], swT[:, :, :], f32(swP[:, 0]), ALU.subtract).then_inc(router_split, 1)

            def mean_features(n):
                finished(dve, "segT", n)
                o, c = at("segT", n), tmpc[:, n % 2:n % 2 + 1]
                link(dve.tensor_scalar(c, o[:, EA:EA + 1], 1.0, None, ALU.max))
                link(dve.reciprocal(c, c))
                dve.tensor_scalar(agg[:, n, :], o[:, 0:EA], c, None, ALU.mult).then_inc(evicted[bank_of[("segT", n)]], 1)

            dve.memset(ecopy[:, :, :, EA:EA + 1], 1.0).then_inc(ones_ready, 1)

            def copy_sums(n):
                finished(dve, "seg", n)
                if n >= 3:
                    finished(dve, "segT", n - 3)
                dve.tensor_copy(seg[:, n % 3, :], at("seg", n)[0:EA + 1, 0:P]).then_inc(evicted[bank_of[("seg", n)]], 1)

            count = dve.alloc_register("dve_half_chunks")
            dve.reg_mov(count, 0)
            dve.wait_ge(plan_ready, 1)
            for n in range(T):
                with dve.Fori(*bounds[n]) as c:
                    done = dve.snap(count, min_val=0, max_val=2 * T * NCH)
                    for k in range(2):
                        dve.wait_ge(halves, done + (k + 1))
                        ids = dstf[:, bass.ds(c, 1), 4 * k:4 * k + 4].rearrange("p c k -> p (c k)")
                        dve.scalar_tensor_tensor(onehot[:, k, :, :], iota.unsqueeze(1).to_broadcast([P, 4, P]), float(n * P),
                                                 ids.unsqueeze(2).to_broadcast([P, 4, P]), ALU.add, ALU.is_equal).then_inc(onehots, 1)
                    dve.reg_add(count, count, 2)
                if n >= 3:
                    mean_features(n - 3)
                if n >= 1:
                    copy_sums(n - 1)
            copy_sums(T - 1)
            for n in range(T - 3, T):
                mean_features(n)

            dve.wait_ge(rows_in, 32)
            link(dve.tensor_tensor(rowa[:, :], rowa[:, :], rowb[:, :], ALU.add))
            dve.wait_ge(xres_in, 16)
            for t in range(T):
                ins = dve.tensor_tensor(xres[:, t, :], xres[:, t, :], rowa[:, :], ALU.add)
            ins.then_inc(bias_added, 1)
            link(dve.memset(negc, NEG))

            def mask(t):
                dve.wait_ge(adj_in[t], 16)
                for jh in range(2):
                    emptied(dve, "S", t, jh)
                link(dve.copy_predicated(scores[:, t, :], nadj[:, t, :], negc.to_broadcast([P, N])))
                link(dve.tensor_reduce(c_c[:, t:t + 1], scores[:, t, :], AX, ALU.max))
                dve.tensor_scalar(c_a[:, t:t + 1], c_c[:, t:t + 1], -1.0, None, ALU.mult).then_inc(masked, 1)

            def scale(t):
                dve.wait_ge(exp_done, t + 1)
                link(dve.reciprocal(c_d[:, t:t + 1], c_b[:, t:t + 1]))
                dve.tensor_scalar(scores[:, t, :], scores[:, t, :], c_d[:, t:t + 1], None, ALU.mult).then_inc(p_ready, 1)

            for t in range(T):
                lo(("V", t))
                if t == 4:
                    mask(0)
                if t == 5:
                    mask(1)
                if t == 6:
                    scale(0)
            dve.wait_ge(bias_added, 1)
            for t in range(T + 1):
                if t < T:
                    for g in range(2):
                        lo(("PT", t, g))
                if t > 0:
                    s = t - 1
                    finished(dve, "AV", s)
                    dve.tensor_tensor(xres[:, s, :], at("AV", s), xres[:, s, :], ALU.add).then_inc(evicted[bank_of[("AV", s)]], 1)
                    emptied(dve, "AV", s)
                    link(moments(s, xres[:, s, :]))
                    if s in (3, 6, 7):
                        variance(1, (3, 6, 7).index(s))
                if t + 2 < T:
                    mask(t + 2)
                if t + 1 < T:
                    scale(t + 1)
                if t == T - 1:
                    normalise(1, 0, lambda t: xres[:, t, :])
            for t in range(TH):
                lo(("xT", 1, t))
            for g in (1, 2):
                normalise(1, g, lambda t: xres[:, t, :])
            for t in range(TH, T):
                lo(("xT", 1, t))

            finished(dve, "rt0")

            def before(Z, tot, cum, n):
                for t in range(1, T):
                    ins = dve.tensor_tensor(Z[:, t, :], tot[:, t - 1, :], Z[:, t - 1, :], ALU.add)
                    if t < T - 1:
                        link(ins)
                ins.then_inc(evicted[bank_of[("tot" + n,)]], 1)
                emptied(dve, "tot" + n)
                dve.tensor_tensor(Z, cum, Z, ALU.add).then_inc(evicted[bank_of[("cum" + n,)]], 1)
                emptied(dve, "cum" + n)

            L, X, OH, Y = tail[:, 0], tail[:, 1], tail[:, 2], tail[:, 3]

            def over_e(ap, e):
                return ap.unsqueeze(2).to_broadcast([P, T, e])

            def over_t(lo_, e):
                return kst[:, lo_:lo_ + e].unsqueeze(1).to_broadcast([P, T, e])

            dve.tensor_tensor(L, at("rt0")[:, 0:P].rearrange("p (t e) -> p t e", t=T),
                              sbrow[:, :].unsqueeze(1).to_broadcast([P, T, EXPERTS]), ALU.add).then_inc(evicted[bank_of[("rt0",)]], 1)
            emptied(dve, "rt0")
            link(dve.tensor_reduce(c_a, L, AX, ALU.max))
            dve.tensor_tensor(X, L, over_e(c_a, EXPERTS), ALU.subtract).then_inc(logit_ready, 1)
            link(dve.tensor_tensor(OH, L, over_e(c_a, EXPERTS), ALU.is_equal))
            link(dve.tensor_tensor(Y, OH, over_t(K_REV16, EXPERTS), ALU.mult))
            link(dve.tensor_reduce(c_b, Y, AX, ALU.max))
            dve.tensor_tensor(OH, Y, over_e(c_b, EXPERTS), ALU.is_equal).then_inc(onehot_ready, 1)
            dve.wait_ge(lexp_done, 1)
            link(dve.tensor_reduce(c_c, X, AX, ALU.add))
            link(dve.reciprocal(c_c, c_c))
            finished(dve, "cum0")
            finished(dve, "tot0")
            tot = at("tot0")[:, 0:P].rearrange("p (t e) -> p t e", t=T)
            cum = at("cum0")[:, 0:P].rearrange("p (t e) -> p t e", t=T)
            Z = tail[:, 4]
            dve.wait_ge(onehot_ready, 1)
            link(dve.memset(Z[:, 0, :], 0.0))
            before(Z, tot, cum, "0")
            link(dve.tensor_tensor(Z, Z, OH, ALU.mult))
            link(dve.tensor_reduce(c_d, Z, AX, ALU.add))
            link(dve.tensor_scalar(c_e, c_b, -float(CAP), float(SLOTS), ALU.mult, ALU.add))
            link(dve.tensor_scalar(c_f, c_d, float(CAP), None, ALU.is_lt))
            link(dve.tensor_scalar(c_g, c_d, float(CAP - 1), None, ALU.min))
            link(dve.tensor_tensor(c_g, c_g, c_e, ALU.add))
            link(dve.tensor_scalar(c_h, c_f, -1.0, 1.0, ALU.mult, ALU.add))
            link(dve.tensor_tensor(c_d, c_g, c_f, ALU.mult))
            link(dve.tensor_tensor(c_e, kst[:, K_TOK:K_TOK + T], c_h, ALU.mult))
            dve.tensor_tensor(idx[:, 0, :], c_d, c_e, ALU.add).then_inc(route_ready, 1)
            dve.tensor_copy(idx[:, 1, :], c_g).then_inc(route_ready, 1)
            dve.wait_ge(route_ready, 2)
            link(dve.tensor_tensor(c_d, c_f, c_c, ALU.mult))
            link(dve.tensor_tensor(c_e, c_h, c_c, ALU.mult))
            for t in range(T):
                dve.scalar_tensor_tensor(xres[:, t, :], xn[:, t, :], c_e[:, t:t + 1], xres[:, t, :], ALU.mult, ALU.add).then_inc(res_ready, 1)
            for e in range(EXPERTS):
                finished(dve, "eY", e)
                dve.wait_ge(eb_in[e % 4], 16 * (e // 4 + 1))
                if e >= 2:
                    dve.wait_ge(y_out[e % 2], 16 * (e // 2))
                dve.tensor_tensor(ey[e % 2], at("eY", e)[0:CAP, :], eb[e % 4], ALU.add).then_inc(evicted[bank_of[("eY", e)]], 1)
                if e in (6, 8):
                    split_weight("W1a" if e == 6 else "W2a")
            for g in range(2):
                finished(dve, "aggT", g)
                dve.tensor_copy(aggT[0:EA, g * HALF:(g + 1) * HALF], at("aggT", g)[0:EA, :]).then_inc(evicted[bank_of[("aggT", g)]], 1)
            dve.memset(aggT[EA:EA + 1, :], 1.0).then_inc(blk_ready, 1)
            dve.wait_ge(res_ready, T)
            dve.wait_ge(rows_sent, 16 * T)
            for n in range(T + 1):
                if n < T:
                    dve.wait_ge(gathered[n], 16)
                    dve.scalar_tensor_tensor(xres[:, n, :], gath[:, n, :], c_d[:, n:n + 1], xres[:, n, :], ALU.mult, ALU.add).then_inc(res_ready, 1)
                if n > 0:
                    t = n - 1
                    dve.wait_ge(res_ready, T + t + 1)
                    link(moments(t, xres[:, t, :]))
                    if t % TH == TH - 1:
                        variance(2, t // TH)
                    if t == TH:
                        normalise(2, 0, lambda t: xres[:, t, :])
                        for i in range(TH):
                            lo(("xT", 2, i))
            normalise(2, 1, lambda t: xres[:, t, :])
            dve.wait_ge(par_exp, 2)
            link(dve.tensor_scalar(par[:, 2, :], par[:, 2, :], 1e-4, 2.0, ALU.max, ALU.min))
            link(dve.tensor_tensor(par[:, 4, :], par[:, 2, :], par[:, 2, :], ALU.mult))
            link(dve.tensor_scalar(par[:, 4, :], par[:, 4, :], 1e-8, None, ALU.add))
            link(dve.reciprocal(par[:, 4, :], par[:, 4, :]))
            link(dve.tensor_scalar(par[:, 4, :], par[:, 4, :], -0.5, None, ALU.mult))
            link(dve.tensor_scalar(par[:, 6, :], par[:, 3, :], 0.02, None, ALU.is_gt))
            link(dve.tensor_tensor(par[:, 7, :], par[:, 6, :], par[:, 3, :], ALU.mult))
            link(dve.tensor_scalar(par[:, 8, 1:2], par[:, 8, 1:2], 0.1, None, ALU.max))
            link(dve.reciprocal(par[:, 8, 1:2], par[:, 8, 1:2]))
            link(dve.tensor_scalar(par[:, 6, :], par[:, 7, :], par[:, 8, 1:2], None, ALU.mult))
            link(dve.tensor_scalar(par[:, 9, 0:1], par[:, 9, 0:1], 1.0, None, ALU.add))
            link(dve.reciprocal(par[:, 9, 0:1], par[:, 9, 0:1]))
            link(dve.tensor_scalar(par[:, 9, 0:1], par[:, 9, 0:1], 0.1, None, ALU.mult))
            link(dve.scalar_tensor_tensor(ctr[:, 2], ctr[:, 1], par[:, 9, 0:1], ctr[:, 0], ALU.mult, ALU.add))
            link(dve.memset(cblk, 0.0))
            link(dve.memset(onesblk, 0.0))
            for b in range(2):
                r = slice(64 * b, 64 * b + 64)
                for j in range(3):
                    w = slice(64 * b + SPLATS * j, 64 * b + SPLATS * (j + 1))
                    dve.tensor_scalar(cblk[r, :, w], ctr[r, 2], -2.0, None, ALU.mult)
                link(dve.memset(onesblk[r, 64 * b:64 * b + KROWS], 1.0))
            flat = cblk.rearrange("p c r -> p (c r)")
            dve.tensor_tensor(csquare, flat, flat, ALU.mult).then_inc(blk_ready, 1)
            for hh in range(2):
                for th in range(2):
                    for m in range(C):
                        lo(("H", hh, th, m), bias=0.0, op=ALU.max)
                    if hh == 0 and th == 0:
                        for t in range(TH, T):
                            lo(("xT", 2, t))
                    if hh == 0 and th == 1:
                        split_weight("W1b")
                    if hh == 1 and th == 1:
                        split_weight("Lq")
                    for t in range(TH):
                        s = th * TH + t
                        name = ("HW", hh, th, t)
                        finished(dve, *name)
                        if hh:
                            emptied(dve, "HW", 0, th, t)
                        else:
                            dve.wait_ge(rows_added, T + s + 1)
                        dve.tensor_tensor(xres[:, s, :], at(*name), xres[:, s, :], ALU.add).then_inc(evicted[bank_of[name]], 1)
                if hh == 0:
                    split_weight("W2b")
            split_weight("Lk")
            finished(dve, "csq")
            dve.scalar_tensor_tensor(par[:, 5, :], at("csq")[:, 0:PAIRS], 0.25, par[:, 4, :], ALU.mult, ALU.mult).then_inc(evicted[bank_of[("csq",)]], 1)
            for n, side in enumerate("qk"):
                for c in range(PAIRS):
                    for th in range(2):
                        i = 2 * (n * PAIRS + c) + th
                        emptied(dve, "d2", side, c, th)
                        w = pring[:, i % 4, 0:HALF]
                        wh = pring[:, i % 4, HALF:2 * HALF].bitcast(F32R)
                        link(dve.tensor_scalar(w, w, par[:, 6 + n, c:c + 1], None, ALU.mult))
                        link(dve.tensor_copy(wh, w))
                        dst = slot[2 + n][:, c // 2, 2 * (c % 2) + th, :]
                        col = (K_LOQ, K_LOK)[n]
                        dve.scalar_tensor_tensor(dst, f32(wh), kst[:, col:col + 1], w, ALU.mult, ALU.add).then_inc(st_ready, 1)
                if side == "q":
                    split_weight("Lv")
            dve.memset(vone[:, :, :, HD:HD + 1], 1.0)

            def normalise_head(h):
                finished(dve, "oU", h)
                for g in range(2):
                    o = bank[:, g, 0:TH * (HD + 1)].rearrange("p (t m) -> p t m", t=TH)
                    r = c_a[:, g * TH:(g + 1) * TH]
                    link(dve.reciprocal(r.unsqueeze(2), o[:, :, HD:HD + 1]))
                    ins = dve.tensor_tensor(xn[:, g * TH:(g + 1) * TH, h * HD:(h + 1) * HD], o[:, :, 0:HD],
                                            r.unsqueeze(2).to_broadcast([P, TH, HD]), ALU.mult)
                    if g == 0:
                        link(ins)
                ins.then_inc(evicted[0], 1)
                emptied(dve, "oU", h)
                dve.sem_inc(o_ready, 1)

            for step in attention_steps():
                if step[0] == "L":
                    _, h, it = step
                    finished(dve, *step)
                    if h // 2 >= 2:
                        finished(dve, "mT", h // 2 - 2)
                    b = bank_of[step]
                    dve.tensor_reduce(mx[:, h // 2 % 2, h % 2, it:it + 1], bank[:, b:b + 2, :].rearrange("p a i -> p (a i)"),
                                      AX, ALU.max).then_inc(evicted[b], 1)
                elif step[0] == "mT":
                    c = step[1]
                    finished(dve, *step)
                    if c:
                        dve.wait_ge(m_stored, 32 * c)
                    o = at(*step)[0:2 * T, 0:P]
                    link(dve.tensor_scalar(mneg[0], o, -1.0, None, ALU.mult))
                    dve.scalar_tensor_tensor(mneg[1], o, -1.0, f32(mneg[0]), ALU.mult, ALU.subtract).then_inc(evicted[0], 1)
                elif step[0] == "oU":
                    normalise_head(step[1])
                elif step[0] == "oT":
                    dve.wait_ge(hi_done, hi_number(step) + 1)
                    for g in range(2):
                        ins = dve.tensor_tensor(xT[g][:, 1, step[1], :], bank[:, g, :], f32(xT[g][:, 0, step[1], :]), ALU.subtract)
                    ins.then_inc(evicted[0], 1)
                if step in (("E", 6, 1), ("E", 6, 5)):
                    split_weight("Lo" if step[2] == 1 else "F")
            for t in range(T):
                finished(dve, "X3", t)
                dve.tensor_tensor(xres[:, t, :], at("X3", t), xres[:, t, :], ALU.add).then_inc(evicted[bank_of[("X3", t)]], 1)
                emptied(dve, "X3", t)
                link(moments(t, xres[:, t, :]))
                if t in (3, 6, 7):
                    variance(3, (3, 6, 7).index(t))
                if t == 5:
                    normalise(3, 0, lambda t: xres[:, t, :])
                if t == 6:
                    dve.wait_ge(router_hi, 2)
                    dve.tensor_tensor(rwP[:, 1], rwT, f32(rwP[:, 0]), ALU.subtract).then_inc(router_split, 1)
            for t in range(TH):
                lo(("xT", 3, t))
            for g in (1, 2):
                normalise(3, g, lambda t: xres[:, t, :])
            for t in range(TH, T):
                lo(("xT", 3, t))
            dve.wait_ge(rowb_in, 16)
            link(dve.memset(f32(one_fr), 1.0))
            link(dve.tensor_copy(b2_fr[0], rowb[0:1, :]))
            dve.tensor_tensor(b2_fr[1], rowb[0:1, :], f32(b2_fr[0]), ALU.subtract).then_inc(b2_split, 1)

            L, X, O1, O2, OS, Y, Z, W = (big6[:, i] for i in range(8))
            finished(dve, "rt1")
            dve.tensor_copy(L, at("rt1").rearrange("p (t e) -> p t e", t=T)).then_inc(evicted[bank_of[("rt1",)]], 1)
            emptied(dve, "rt1")
            link(dve.tensor_reduce(c_a, L, AX, ALU.max))
            dve.tensor_tensor(X, L, over_e(c_a, E2), ALU.subtract).then_inc(logit_ready, 1)

            def first_of(oh, logits, greatest):
                link(dve.tensor_tensor(oh, logits, over_e(greatest, E2), ALU.is_equal))
                link(dve.tensor_tensor(Y, oh, over_t(K_REV64, E2), ALU.mult))
                link(dve.tensor_reduce(c_b, Y, AX, ALU.max))
                link(dve.tensor_tensor(oh, Y, over_e(c_b, E2), ALU.is_equal))

            first_of(O1, L, c_a)
            link(dve.scalar_tensor_tensor(W.rearrange("p t e -> p (t e)"), O1.rearrange("p t e -> p (t e)"), -BIG,
                                          L.rearrange("p t e -> p (t e)"), ALU.mult, ALU.add))
            link(dve.tensor_reduce(c_c, W, AX, ALU.max))
            first_of(O2, W, c_c)
            dve.tensor_tensor(OS, O1, O2, ALU.add).then_inc(onehot_ready, 1)
            dve.wait_ge(lexp_done, 2)
            link(dve.tensor_reduce(c_d, X, AX, ALU.add))
            link(dve.reciprocal(c_d, c_d))
            link(dve.tensor_tensor(Y, X, O2, ALU.mult))
            link(dve.tensor_reduce(c_e, Y, AX, ALU.add))
            link(dve.tensor_tensor(c_e, c_e, c_d, ALU.mult))
            finished(dve, "cum1")
            finished(dve, "tot1")
            link(dve.memset(Z[:, 0, :], 0.0))
            before(Z, at("tot1").rearrange("p (t e) -> p t e", t=T), at("cum1").rearrange("p (t e) -> p t e", t=T), "1")
            for oh, prob in ((O1, c_d), (O2, c_e)):
                link(dve.tensor_tensor(Y, Z, oh, ALU.mult))
                link(dve.tensor_reduce(c_f, Y, AX, ALU.add))
                link(dve.tensor_scalar(c_f, c_f, float(CAP2), None, ALU.is_lt))
                link(dve.tensor_tensor(prob, prob, c_f, ALU.mult))
            link(dve.tensor_tensor(c_d, c_d, c_e, ALU.add))
            for t in range(T):
                finished(dve, "F2", t)
                dve.scalar_tensor_tensor(xres[:, t, :], at("F2", t), c_d[:, t:t + 1], xres[:, t, :], ALU.mult, ALU.add).then_inc(y_ready, 1)


SHAPES = [("x", (N, D), F32), ("src_scatter", (P, SCATTERS), I32), ("dst_scatter", (P, SCATTERS), I32),
          ("dst_chunks", (P, SCATTERS), I32), ("edge_attr_64", (EDGES, EA), F32),
          ("L0_gnn_Wv", (D, D), F32), ("bq_col", (P, C), F32), ("bk_col", (P, C), F32), ("L0_gnn_bv", (D,), F32),
          ("L0_mix_w_qkv", (D, 3 * D), F32), ("L0_mix_w_out", (D, D), F32), ("L0_mix_b_out", (D,), F32),
          ("L0_ffn_switch_b", (EXPERTS,), F32), ("L0_ffn_expert_b", (EXPERTS, D), F32),
          ("L1_gnn_W1", (D + EA, HID), F32), ("L1_gnn_b1", (HID,), F32), ("L1_gnn_W2", (HID, D), F32),
          ("L1_gnn_b2", (D,), F32), ("L1_mix_movement_scale_param", (1,), F32), ("L1_mix_temperature", (1,), F32),
          ("ffn_b1_col", (P, FFN // P), F32), ("L1_ffn_b2", (D,), F32),
          ("consts", (P, K_COLS), F32), ("WqT", (D, D), F32), ("WkT", (D, D), F32), ("mWqT", (D, D), F32),
          ("swT", (D, EXPERTS), F32), ("ewT", (EXPERTS, D, D), F32), ("qkvT", (D, 3 * D), F32), ("outT", (D, D), F32),
          ("rwT", (D, E2), F32), ("w1T", (D, FFN), F32), ("w2T", (FFN, D), F32),
          ("splat_par", (P, 2, PAIRS), F32), ("splat_ctr", (P, 2, PAIRS, SPLATS), F32)]


def kernel(**inputs):
    import concourse.bacc as bacc
    from concourse.bass_utils import run_bass_kernel_spmd

    given = {k: np.asarray(v) for k, v in inputs.items()}

    def turn(name):
        return np.swapaxes(given[name], -1, -2)

    laid = dict(given)
    laid["consts"] = const_table()
    laid["WqT"] = turn("L0_gnn_Wq")
    laid["WkT"] = turn("L0_gnn_Wk")
    laid["mWqT"] = given["L0_mix_w_qkv"][:, 0:D].T
    for name, col in (("L0_gnn_bq", "bq_col"), ("L0_gnn_bk", "bk_col"), ("L1_ffn_b1", "ffn_b1_col")):
        laid[col] = given[name].reshape(-1, P).T
    laid["swT"] = turn("L0_ffn_switch_w")
    laid["ewT"] = turn("L0_ffn_expert_w")
    laid["qkvT"] = turn("L1_mix_qkv_w")
    laid["outT"] = turn("L1_mix_out_w")
    laid["rwT"] = turn("L1_ffn_router_w")
    laid["w1T"] = turn("L1_ffn_w1")
    laid["w2T"] = turn("L1_ffn_w2")
    batches = SCATTERS // BATCH
    order = [9 * q % batches + batches * b for q in range(batches) for b in range(BATCH)]
    for name in ("src", "dst"):
        laid[name + "_scatter"] = given[name].reshape(SCATTERS, P)[order].T
    laid["dst_chunks"] = given["dst"].reshape(NCH, P, EK).transpose(1, 0, 2).reshape(P, SCATTERS)
    par = np.zeros((2, 64, 2, PAIRS), np.float32)
    for v, name in enumerate(("L1_mix_log_scales", "L1_mix_log_amps")):
        by_pair = given[name].reshape(PAIRS, 2, SPLATS)
        for j in range(3):
            par[:, SPLATS * j:SPLATS * (j + 1), v, :] = by_pair.transpose(1, 2, 0)
    laid["splat_par"] = par.reshape(P, 2, PAIRS)
    laid["splat_ctr"] = np.stack([given[name].reshape(PAIRS, 2, SPLATS, HD).transpose(1, 3, 0, 2).reshape(P, PAIRS, SPLATS)
                                  for name in ("L1_mix_base_centers", "L1_mix_center_deltas")], axis=1)

    nc = bacc.Bacc("TRN2", target_bir_lowering=False, num_devices=1)
    arrays, aps = {}, {}
    for name, shape, dt in SHAPES:
        arrays["in_" + name] = np.ascontiguousarray(laid[name])
        aps[name] = nc.dram_tensor("in_" + name, shape, dt, kind="ExternalInput").ap()
    aps["out"] = nc.dram_tensor("out_x", (N, D), F32, kind="ExternalOutput").ap()
    build(nc, aps)
    result = run_bass_kernel_spmd(nc, [arrays], core_ids=[0])
    return result.results[0]["out_x"]
```
